# Optimizing a Trainium2 kernel written in Bass

```python
import numpy as np
import jax
import jax.numpy as jnp

def _softmax(x, axis=-1):
    return jax.nn.softmax(x, axis=axis)

def _gelu(x):
    return jax.nn.gelu(x, approximate=True)

def _silu(x):
    return jax.nn.silu(x)

def _sigmoid(x):
    return jax.nn.sigmoid(x)

def _layernorm(x, axis=-1, eps=1e-05):
    m = jnp.mean(x, axis=axis, keepdims=True)
    v = jnp.var(x, axis=axis, keepdims=True)
    return (x - m) / jnp.sqrt(v + eps)

def _scatter_add(tgt, idx, src, axis=0):
    return tgt.at[idx].add(src)

def _segment_sum(src, seg, n):
    return jax.ops.segment_sum(src, seg, n)
kernel_name = 'mk_lm_tower_d2_tok_ids256_r4_262116'

def setup_inputs(seed: int=0):
    np.random.seed(seed)
    _w = jnp.asarray

    def _rec_inputs():
        import jax
        import jax.numpy as jnp
        _rk = jax.random.key(seed)
        x = jax.random.randint(jax.random.fold_in(_rk, 1), (16, 128), 0, 64, jnp.int32)
        return x
    x = _rec_inputs()

    def _L0_tok_setup():
        import jax, jax.numpy as jnp
        import numpy as np
        D_MODEL = 128
        N_LAYERS = 4
        VOCAB = 64
        SEQ = 512
        BATCH = 8
        EPS = 1e-05

        def _ln(x, g, b):
            mu = jnp.mean(x, axis=-1, keepdims=True)
            var = jnp.mean(jnp.square(x - mu), axis=-1, keepdims=True)
            return (x - mu) * jax.lax.rsqrt(var + EPS) * g + b

        def _fast_memory(x, mask, W_upd, b_upd, W_f, b_f, decay_param):
            decay = jax.nn.sigmoid(decay_param[0])
            u = jnp.einsum('bsd,de->bse', x, W_upd) + b_upd
            u_t = jnp.swapaxes(u, 0, 1)
            m_t = jnp.swapaxes(mask, 0, 1)[..., None]

            def step(mem, inp):
                u_i, msk = inp
                new = decay * mem + u_i
                mem = msk * new + (1.0 - msk) * mem
                return (mem, mem)
            mem0 = jnp.zeros((x.shape[0], x.shape[2]), x.dtype)
            _, mems = jax.lax.scan(step, mem0, (u_t, m_t))
            mems = jnp.swapaxes(mems, 0, 1)
            return jnp.einsum('bsd,de->bse', mems, W_f) + b_f
        key = jax.random.key(seed)
        ks = jax.random.split(key, 16)
        d, dff = (D_MODEL, 4 * D_MODEL)
        s = 0.02
        inp = {'tokens': jax.random.randint(ks[0], (BATCH, SEQ), 0, VOCAB, dtype=jnp.int64), 'emb': jax.random.normal(ks[1], (VOCAB, d), jnp.float32) * s, 'W_upd': jax.random.normal(ks[2], (d, d), jnp.float32) * s, 'b_upd': jnp.zeros((d,), jnp.float32), 'W_f': jax.random.normal(ks[3], (d, d), jnp.float32) * s, 'b_f': jnp.zeros((d,), jnp.float32), 'decay_param': jnp.zeros((1,), jnp.float32), 'norm_g': jnp.ones((d,), jnp.float32), 'norm_b': jnp.zeros((d,), jnp.float32), 'cms_ln_g': jnp.ones((N_LAYERS, d), jnp.float32), 'cms_ln_b': jnp.zeros((N_LAYERS, d), jnp.float32), 'cms_W1': jax.random.normal(ks[4], (N_LAYERS, d, dff), jnp.float32) * s, 'cms_b1': jnp.zeros((N_LAYERS, dff), jnp.float32), 'cms_W2': jax.random.normal(ks[5], (N_LAYERS, dff, d), jnp.float32) * s, 'cms_b2': jnp.zeros((N_LAYERS, d), jnp.float32), 'head_W': jax.random.normal(ks[6], (d, VOCAB), jnp.float32) * s, 'head_b': jnp.zeros((VOCAB,), jnp.float32)}
        return inp
    _L0_tok_all = _L0_tok_setup()
    _L0_tok_in = {k: v for k, v in _L0_tok_all.items() if k in ('emb', 'W_upd', 'b_upd', 'W_f', 'b_f', 'decay_param', 'norm_g', 'norm_b', 'cms_ln_g', 'cms_ln_b', 'cms_W1', 'cms_b1', 'cms_W2', 'cms_b2', 'head_W', 'head_b')}
    del _L0_tok_all

    def _L0_attn_setup():
        import jax, jax.numpy as jnp
        import numpy as np
        key = jax.random.key(seed)
        inputs = jax.random.normal(key, (8, 512, 64), dtype=jnp.float32)
        return {'inputs': inputs}
    _L0_attn_all = _L0_attn_setup()
    _L0_attn_in = {k: v for k, v in _L0_attn_all.items() if k in ()}
    del _L0_attn_all

    def _L0_ffn_setup():
        import math
        import jax, jax.numpy as jnp
        import numpy as np
        CAPACITY_FACTOR = 1.25
        key = jax.random.key(seed)
        ks = jax.random.split(key, 5)
        B, L, D, F, E = (8, 2048, 64, 256, 8)
        h = jax.random.normal(ks[0], (B, L, D), dtype=jnp.float32)
        gate_w = jax.random.normal(ks[1], (D, E), dtype=jnp.float32) * 0.02
        gate_b = jnp.zeros((E,), dtype=jnp.float32)
        w1 = jax.random.normal(ks[2], (E, D, F), dtype=jnp.float32) * (1.0 / math.sqrt(D))
        b1 = jnp.zeros((E, F), dtype=jnp.float32)
        w2 = jax.random.normal(ks[3], (E, F, D), dtype=jnp.float32) * (1.0 / math.sqrt(F))
        b2 = jnp.zeros((E, D), dtype=jnp.float32)
        return {'h': h, 'gate_w': gate_w, 'gate_b': gate_b, 'w1': w1, 'b1': b1, 'w2': w2, 'b2': b2}
    _L0_ffn_all = _L0_ffn_setup()
    _L0_ffn_in = {k: v for k, v in _L0_ffn_all.items() if k in ('gate_w', 'gate_b', 'w1', 'b1', 'w2', 'b2')}
    del _L0_ffn_all

    def _L1_attn_setup():
        import jax, jax.numpy as jnp
        import numpy as np
        DIM = 64
        WS = 64
        H = 8
        HD = DIM // H
        SCALE = HD ** (-0.5)
        key = jax.random.key(seed)
        k1, k2, k3, k4 = jax.random.split(key, 4)
        B, L = (8, 4096)
        x = jax.random.normal(k1, (B, L, DIM), dtype=jnp.float32)
        w_qkv = jax.random.normal(k2, (3 * DIM, DIM), dtype=jnp.float32) * DIM ** (-0.5)
        w_proj = jax.random.normal(k3, (DIM, DIM), dtype=jnp.float32) * DIM ** (-0.5)
        b_proj = jnp.zeros((DIM,), dtype=jnp.float32)
        rel_bias = jax.random.normal(k4, (2 * WS - 1,), dtype=jnp.float32) * 0.02
        return {'x': x, 'w_qkv': w_qkv, 'w_proj': w_proj, 'b_proj': b_proj, 'rel_bias': rel_bias}
    _L1_attn_all = _L1_attn_setup()
    _L1_attn_in = {k: v for k, v in _L1_attn_all.items() if k in ('w_qkv', 'w_proj', 'b_proj', 'rel_bias')}
    del _L1_attn_all

    def _L1_ffn_setup():
        import jax, jax.numpy as jnp
        import numpy as np
        E, D, H, TOP_K = (6, 64, 64, 2)
        ROUTER_H = D // 2
        key = jax.random.key(seed)
        ks = jax.random.split(key, 12)
        s = 1.0 / np.sqrt(D)
        sh = 1.0 / np.sqrt(H)
        sr = 1.0 / np.sqrt(ROUTER_H)
        return {'features': jax.random.normal(ks[0], (8, 1024, D), dtype=jnp.float32), 'router_w1': jax.random.uniform(ks[1], (D, ROUTER_H), jnp.float32, -s, s), 'router_b1': jnp.zeros((ROUTER_H,), jnp.float32), 'router_w2': jax.random.uniform(ks[2], (ROUTER_H, E), jnp.float32, -sr, sr), 'router_b2': jnp.zeros((E,), jnp.float32), 'expert_w1': jax.random.uniform(ks[3], (E, D, H), jnp.float32, -s, s), 'expert_b1': jnp.zeros((E, H), jnp.float32), 'expert_w2': jax.random.uniform(ks[4], (E, H, H), jnp.float32, -sh, sh), 'expert_b2': jnp.zeros((E, H), jnp.float32), 'expert_w3': jax.random.uniform(ks[5], (E, H, D), jnp.float32, -sh, sh), 'expert_b3': jnp.zeros((E, D), jnp.float32)}
    _L1_ffn_all = _L1_ffn_setup()
    _L1_ffn_in = {k: v for k, v in _L1_ffn_all.items() if k in ('router_w1', 'router_b1', 'router_w2', 'router_b2', 'expert_w1', 'expert_b1', 'expert_w2', 'expert_b2', 'expert_w3', 'expert_b3')}
    del _L1_ffn_all
    return {'x': x, 'L0_tok_emb': _L0_tok_in['emb'], 'L0_tok_W_upd': _L0_tok_in['W_upd'], 'L0_tok_b_upd': _L0_tok_in['b_upd'], 'L0_tok_W_f': _L0_tok_in['W_f'], 'L0_tok_b_f': _L0_tok_in['b_f'], 'L0_tok_decay_param': _L0_tok_in['decay_param'], 'L0_tok_norm_g': _L0_tok_in['norm_g'], 'L0_tok_norm_b': _L0_tok_in['norm_b'], 'L0_tok_cms_ln_g': _L0_tok_in['cms_ln_g'], 'L0_tok_cms_ln_b': _L0_tok_in['cms_ln_b'], 'L0_tok_cms_W1': _L0_tok_in['cms_W1'], 'L0_tok_cms_b1': _L0_tok_in['cms_b1'], 'L0_tok_cms_W2': _L0_tok_in['cms_W2'], 'L0_tok_cms_b2': _L0_tok_in['cms_b2'], 'L0_tok_head_W': _L0_tok_in['head_W'], 'L0_tok_head_b': _L0_tok_in['head_b'], 'L0_ffn_gate_w': _L0_ffn_in['gate_w'], 'L0_ffn_gate_b': _L0_ffn_in['gate_b'], 'L0_ffn_w1': _L0_ffn_in['w1'], 'L0_ffn_b1': _L0_ffn_in['b1'], 'L0_ffn_w2': _L0_ffn_in['w2'], 'L0_ffn_b2': _L0_ffn_in['b2'], 'L1_attn_w_qkv': _L1_attn_in['w_qkv'], 'L1_attn_w_proj': _L1_attn_in['w_proj'], 'L1_attn_b_proj': _L1_attn_in['b_proj'], 'L1_attn_rel_bias': _L1_attn_in['rel_bias'], 'L1_ffn_router_w1': _L1_ffn_in['router_w1'], 'L1_ffn_router_b1': _L1_ffn_in['router_b1'], 'L1_ffn_router_w2': _L1_ffn_in['router_w2'], 'L1_ffn_router_b2': _L1_ffn_in['router_b2'], 'L1_ffn_expert_w1': _L1_ffn_in['expert_w1'], 'L1_ffn_expert_b1': _L1_ffn_in['expert_b1'], 'L1_ffn_expert_w2': _L1_ffn_in['expert_w2'], 'L1_ffn_expert_b2': _L1_ffn_in['expert_b2'], 'L1_ffn_expert_w3': _L1_ffn_in['expert_w3'], 'L1_ffn_expert_b3': _L1_ffn_in['expert_b3']}

def reference(x, L0_tok_emb, L0_tok_W_upd, L0_tok_b_upd, L0_tok_W_f, L0_tok_b_f, L0_tok_decay_param, L0_tok_norm_g, L0_tok_norm_b, L0_tok_cms_ln_g, L0_tok_cms_ln_b, L0_tok_cms_W1, L0_tok_cms_b1, L0_tok_cms_W2, L0_tok_cms_b2, L0_tok_head_W, L0_tok_head_b, L0_ffn_gate_w, L0_ffn_gate_b, L0_ffn_w1, L0_ffn_b1, L0_ffn_w2, L0_ffn_b2, L1_attn_w_qkv, L1_attn_w_proj, L1_attn_b_proj, L1_attn_rel_bias, L1_ffn_router_w1, L1_ffn_router_b1, L1_ffn_router_w2, L1_ffn_router_b2, L1_ffn_expert_w1, L1_ffn_expert_b1, L1_ffn_expert_w2, L1_ffn_expert_b2, L1_ffn_expert_w3, L1_ffn_expert_b3):
    import jax
    import jax.numpy as jnp

    def _L0_tok_ref(tokens, emb, W_upd, b_upd, W_f, b_f, decay_param, norm_g, norm_b, cms_ln_g, cms_ln_b, cms_W1, cms_b1, cms_W2, cms_b2, head_W, head_b):
        import jax, jax.numpy as jnp
        import numpy as np
        D_MODEL = 128
        N_LAYERS = 4
        VOCAB = 64
        SEQ = 512
        BATCH = 8
        EPS = 1e-05

        def _ln(x, g, b):
            mu = jnp.mean(x, axis=-1, keepdims=True)
            var = jnp.mean(jnp.square(x - mu), axis=-1, keepdims=True)
            return (x - mu) * jax.lax.rsqrt(var + EPS) * g + b

        def _fast_memory(x, mask, W_upd, b_upd, W_f, b_f, decay_param):
            decay = jax.nn.sigmoid(decay_param[0])
            u = jnp.einsum('bsd,de->bse', x, W_upd) + b_upd
            u_t = jnp.swapaxes(u, 0, 1)
            m_t = jnp.swapaxes(mask, 0, 1)[..., None]

            def step(mem, inp):
                u_i, msk = inp
                new = decay * mem + u_i
                mem = msk * new + (1.0 - msk) * mem
                return (mem, mem)
            mem0 = jnp.zeros((x.shape[0], x.shape[2]), x.dtype)
            _, mems = jax.lax.scan(step, mem0, (u_t, m_t))
            mems = jnp.swapaxes(mems, 0, 1)
            return jnp.einsum('bsd,de->bse', mems, W_f) + b_f
        mask = (tokens != 0).astype(emb.dtype)
        x = emb[tokens]
        x = x + _fast_memory(x, mask, W_upd, b_upd, W_f, b_f, decay_param)
        x = _ln(x, norm_g, norm_b)
        for i in range(N_LAYERS):
            h = _ln(x, cms_ln_g[i], cms_ln_b[i])
            h = jax.nn.gelu(jnp.einsum('bsd,df->bsf', h, cms_W1[i]) + cms_b1[i], approximate=False)
            h = jnp.einsum('bsf,fd->bsd', h, cms_W2[i]) + cms_b2[i]
            x = x + h
        return jnp.einsum('bsd,dv->bsv', x, head_W) + head_b

    def _L0_attn_ref(inputs):
        import jax, jax.numpy as jnp
        import numpy as np
        d_k = jnp.asarray(inputs.shape[-1], dtype=inputs.dtype)
        scores = jnp.einsum('bnd,bmd->bnm', inputs, inputs) / jnp.sqrt(d_k)
        weights = jax.nn.softmax(scores, axis=-1)
        context = jnp.einsum('bnm,bmd->bnd', weights, inputs)
        return context

    def _L0_ffn_ref(h, gate_w, gate_b, w1, b1, w2, b2):
        import math
        import jax, jax.numpy as jnp
        import numpy as np
        CAPACITY_FACTOR = 1.25
        B, L, D = h.shape
        E = gate_w.shape[1]
        T = B * L
        C = max(1, math.ceil(CAPACITY_FACTOR * T / E))
        x = h.reshape(T, D)
        logits = x @ gate_w + gate_b
        probs = jax.nn.softmax(logits, axis=-1)
        idx = jnp.argmax(probs, axis=-1)
        prb = jnp.take_along_axis(probs, idx[:, None], axis=1)[:, 0]
        one_hot = jax.nn.one_hot(idx, E, dtype=jnp.float32)
        pos = (jnp.cumsum(one_hot, axis=0) * one_hot).sum(-1).astype(jnp.int32) - 1
        kept = pos < C
        pos_safe = jnp.where(kept, pos, C)
        buf = jnp.zeros((E, C, D), dtype=h.dtype).at[idx, pos_safe].set(x, mode='drop')
        hmid = jax.nn.relu(jnp.einsum('ecd,edf->ecf', buf, w1) + b1[:, None, :])
        ybuf = jnp.einsum('ecf,efd->ecd', hmid, w2) + b2[:, None, :]
        pos_g = jnp.minimum(pos, C - 1)
        y_tok = ybuf[idx, pos_g] * (prb * kept)[:, None]
        y = y_tok.reshape(B, L, D)
        y = jnp.nan_to_num(y, nan=0.0, posinf=10000.0, neginf=-10000.0)
        return y

    def _L1_attn_ref(x, w_qkv, w_proj, b_proj, rel_bias):
        import jax, jax.numpy as jnp
        import numpy as np
        DIM = 64
        WS = 64
        H = 8
        HD = DIM // H
        SCALE = HD ** (-0.5)
        B, L, C = x.shape
        pad_len = (WS - L % WS) % WS
        if pad_len > 0:
            x = jnp.pad(x, ((0, 0), (0, pad_len), (0, 0)))
        padded_L = x.shape[1]
        nw = padded_L // WS
        xw = x.reshape(B, nw, WS, C)
        qkv = jnp.einsum('bnwc,oc->bnwo', xw, w_qkv)
        qkv = qkv.reshape(B, nw, WS, 3, H, HD)
        q = jnp.transpose(qkv[..., 0, :, :], (0, 1, 3, 2, 4))
        k = jnp.transpose(qkv[..., 1, :, :], (0, 1, 3, 2, 4))
        v = jnp.transpose(qkv[..., 2, :, :], (0, 1, 3, 2, 4))
        attn = jnp.einsum('bnhqd,bnhkd->bnhqk', q, k) * SCALE
        pos = jnp.arange(WS)
        rel_idx = pos[None, :] - pos[:, None] + WS - 1
        attn = attn + rel_bias[rel_idx]
        attn = jax.nn.softmax(attn, axis=-1)
        out = jnp.einsum('bnhqk,bnhkd->bnhqd', attn, v)
        out = jnp.transpose(out, (0, 1, 3, 2, 4)).reshape(B, nw, WS, C)
        out = jnp.einsum('bnwc,oc->bnwo', out, w_proj) + b_proj
        out = out.reshape(B, padded_L, C)
        if pad_len > 0:
            out = out[:, :L, :]
        return out

    def _L1_ffn_ref(features, router_w1, router_b1, router_w2, router_b2, expert_w1, expert_b1, expert_w2, expert_b2, expert_w3, expert_b3):
        import jax, jax.numpy as jnp
        import numpy as np
        E, D, H, TOP_K = (6, 64, 64, 2)
        ROUTER_H = D // 2
        rh = jax.nn.relu(features @ router_w1 + router_b1)
        expert_logits = jax.nn.softmax(rh @ router_w2 + router_b2, axis=-1)
        top_w, top_i = jax.lax.top_k(expert_logits, TOP_K)
        routing_weights = jax.nn.softmax(top_w, axis=-1)
        h1 = jax.nn.relu(jnp.einsum('bsd,edh->bseh', features, expert_w1) + expert_b1)
        h2 = jax.nn.relu(jnp.einsum('bseh,ehf->bsef', h1, expert_w2) + expert_b2)
        expert_out = jnp.einsum('bsef,efo->bseo', h2, expert_w3) + expert_b3
        sel = jnp.take_along_axis(expert_out, top_i[:, :, :, None], axis=2)
        combined = jnp.sum(sel * routing_weights[..., None], axis=2)
        return combined
    h = _L0_tok_ref(x, L0_tok_emb, L0_tok_W_upd, L0_tok_b_upd, L0_tok_W_f, L0_tok_b_f, L0_tok_decay_param, L0_tok_norm_g, L0_tok_norm_b, L0_tok_cms_ln_g, L0_tok_cms_ln_b, L0_tok_cms_W1, L0_tok_cms_b1, L0_tok_cms_W2, L0_tok_cms_b2, L0_tok_head_W, L0_tok_head_b)
    h = h + _L0_attn_ref(_layernorm(h, axis=-1))
    h = h + _L0_ffn_ref(_layernorm(h, axis=-1), L0_ffn_gate_w, L0_ffn_gate_b, L0_ffn_w1, L0_ffn_b1, L0_ffn_w2, L0_ffn_b2)
    h = h + _L1_attn_ref(_layernorm(h, axis=-1), L1_attn_w_qkv, L1_attn_w_proj, L1_attn_b_proj, L1_attn_rel_bias)
    h = h + _L1_ffn_ref(_layernorm(h, axis=-1), L1_ffn_router_w1, L1_ffn_router_b1, L1_ffn_router_w2, L1_ffn_router_b2, L1_ffn_expert_w1, L1_ffn_expert_b1, L1_ffn_expert_w2, L1_ffn_expert_b2, L1_ffn_expert_w3, L1_ffn_expert_b3)
    return h

_drawn_inputs = setup_inputs


def setup_inputs(seed=0):
    import zlib

    import numpy as np

    out = dict(_drawn_inputs(seed))
    spreads = {'L0_tok_b_upd': (0.0, 0.1),
     'L0_tok_b_f': (0.0, 0.1),
     'L0_tok_norm_g': (1.0, 0.2),
     'L0_tok_norm_b': (0.0, 0.1),
     'L0_tok_cms_ln_g': (1.0, 0.6),
     'L0_tok_cms_ln_b': (0.0, 0.8),
     'L0_tok_cms_b1': (0.0, 0.1),
     'L0_tok_cms_b2': (0.0, 0.1),
     'L0_tok_head_b': (0.0, 0.1),
     'L0_ffn_gate_b': (0.0, 0.1),
     'L0_ffn_b1': (0.0, 2.0),
     'L0_ffn_b2': (0.0, 0.8),
     'L1_attn_b_proj': (0.0, 0.1),
     'L1_ffn_router_b1': (0.0, 2.0),
     'L1_ffn_router_b2': (0.0, 2.0),
     'L1_ffn_expert_b1': (0.0, 0.8),
     'L1_ffn_expert_b2': (0.0, 0.455),
     'L1_ffn_expert_b3': (0.0, 0.1)}
    factors = {'L0_tok_W_upd': 21.389,
     'L1_attn_rel_bias': 200.0,
     'L1_ffn_router_w2': 8.0,
     'L1_ffn_router_w1': 8.0}
    for name, (base, spread) in spreads.items():
        noise = np.random.default_rng([zlib.crc32(name.encode()), seed]).standard_normal(out[name].shape)
        drawn = base * np.exp(spread * noise) if base else spread * noise
        out[name] = jnp.asarray(drawn.astype(out[name].dtype))
    for name, factor in factors.items():
        out[name] = (out[name] * factor).astype(out[name].dtype)
    return out
```

```python
from contextlib import ExitStack

import concourse.bass as bass
from concourse import mybir

F32 = mybir.dt.float32
BF16 = mybir.dt.bfloat16
I32 = mybir.dt.int32
U32 = mybir.dt.uint32
ALU = mybir.AluOpType
ACT = mybir.ActivationFunctionType
AX = mybir.AxisListType.X

P = 128
EPS = 1e-5
FLT_MAX = 3.4028234e38
CLIP = 1e4


class Ring:

    def __init__(self, banks, filled, freed):
        self.banks, self.filled, self.freed = banks, filled, freed
        self.at, self.readers = {}, []

    def add(self, key, reader):
        self.at[key] = len(self.readers)
        self.readers.append(reader)

    def bank(self, key):
        return self.banks[self.at[key] % len(self.banks)]

    def number(self, key):
        return self.at[key] + 1

    def wait_free(self, pe, key):
        before = self.at[key] - len(self.banks)
        if before >= 0:
            reader = self.readers[before]
            pe.wait_ge(self.freed[reader], self.readers[:before + 1].count(reader))

    def wait_read(self, eng, key):
        reader = self.readers[self.at[key]]
        eng.wait_ge(self.freed[reader], self.readers[:self.at[key] + 1].count(reader))


def build(nc, a, out):
    NB, S = a["x"].shape
    V, D = a["L0_tok_emb"].shape
    L, _, FF = a["L0_tok_cms_W1"].shape
    FC = FF // P
    _, E, W = None, *a["L0_ffn_gate_w"].shape[::-1]
    EF = a["L0_ffn_w1"].shape[2]
    EC = EF // P
    T = NB * S
    NT = T // P
    GT = 4
    NG = NT // GT
    GN = GT * P
    CAP = -(-5 * T // (4 * E))
    SLOTS = E * CAP
    ST = SLOTS // P
    WS = 64
    H1 = 8
    HD = W // H1
    HP = H1 // 2
    X, RH = a["L1_ffn_router_w1"].shape[0] and a["L1_ffn_expert_w1"].shape[0], a["L1_ffn_router_w1"].shape[1]
    XP = X // 2
    assert S == P and D == P and W == 64 and SLOTS % P == 0 and V == 64 and P == 2 * WS

    NSTEP = L * NG

    xbuf = nc.dram_tensor("expert_rows", (SLOTS + T, W), F32, kind="Internal").ap()
    ybuf = nc.dram_tensor("expert_out", (SLOTS, W), F32, kind="Internal").ap()

    with ExitStack() as ctx:
        def sb(name, shape, dt=F32):
            return ctx.enter_context(nc.sbuf_tensor(name, shape, dt))

        def sem(name):
            return ctx.enter_context(nc.semaphore(name))

        ident = sb("ident", [P, P])
        tri = sb("tri", [P, P], BF16)
        ones_b = sb("ones_b", [P, P], BF16)
        iota_v = sb("iota_v", [V, 1], I32)
        iota_vf = sb("iota_vf", [V, 1])
        not_zero = sb("not_zero", [V, 1])
        rank8 = sb("rank8", [P, E])
        rank6 = sb("rank6", [P, X])
        rank_i = sb("rank_i", [P, E], I32)
        trash_i = sb("trash_i", [P, NT], I32)
        trash = sb("trash", [P, NT])
        headmask = sb("headmask", [P, H1])
        zeros = sb("zeros", [P, ST * W])
        tokens = sb("tokens", [P, T], I32)
        emb = sb("emb", [V, D])
        embf = sb("embf", [V, D])
        embT = sb("embT", [D, V])
        w_upd = sb("w_upd", [D, D])
        w_f = sb("w_f", [D, D])
        b_upd = sb("b_upd", [V, D])
        b_f = sb("b_f", [V, D])
        table0 = sb("table0", [V, D])
        table = sb("table", [V, D])
        decay_in = sb("decay_in", [P, 1])
        decay = sb("decay", [P, 4])
        norm_g = sb("norm_g", [P, D])
        norm_b = sb("norm_b", [P, D])
        NR = 2 * L + L * FC + XP + E * EC
        R_B1, R_X2, R_E1 = 2 * L, 2 * L + L * FC, 2 * L + L * FC + XP
        rows = sb("rows", [NR, P])
        cols = sb("cols", [P, NR])
        w1 = sb("w1", [D, L, FF])
        w1s = sb("w1s", [D, L, FF])
        w2 = sb("w2", [P, L, FC, D])
        b1 = sb("b1", [P, L * FC])
        b2 = sb("b2", [P, L, D])
        head_w = sb("head_w", [D, W])
        head_b = sb("head_b", [P, W])
        gate_w = sb("gate_w", [W + 1, E])
        e_w1 = sb("e_w1", [W, E, EF])
        e_w2 = sb("e_w2", [P, E, EC, W])
        e_b2 = sb("e_b2", [P, E, W])
        qkv_rows = sb("qkv_rows", [P, 2, W])
        qkv_w = sb("qkv_w", [W, 3 * W])
        proj_rows = sb("proj_rows", [W, W])
        proj_w = sb("proj_w", [W + 1, W])
        relb_up = sb("relb_up", [WS, WS])
        flip = sb("flip", [WS, 2, WS])
        relb = sb("relb", [P, WS])
        r_w1 = sb("r_w1", [W + 1, RH])
        r_w2 = sb("r_w2", [RH + 1, X])
        x_w1 = sb("x_w1", [W + 1, X * W])
        x_w2 = sb("x_w2", [P, XP, P])
        x_w3 = sb("x_w3", [P, XP, P])
        x_b3 = sb("x_b3", [X, W])

        onehot = sb("onehot", [V, T])
        scan_io = sb("scan_io", [P, 2, T])
        keep_mem = scan_io[:, 0, :]
        mems = scan_io[:, 1, :]
        ln_t = sb("ln_t", [P, GT, D])
        stream = sb("stream", [P, 2, NT, D])
        x = stream[:, 0, :, :]
        xb = stream[:, 1, :, :]
        hn = sb("hn", [P, NG, GN])
        hT = sb("hT", [P, 2, GN])
        gT = sb("gT", [P, 2, FC, GN])
        st = sb("st", [P, 2, GT, 6])
        mv = sb("mv", [P, 2, GT, 2])
        ve = sb("ve", [P, 2, GT])
        rstd = sb("rstd", [P, 2, GT])
        neg_half = sb("neg_half", [P, GT])
        h = sb("h", [P, NT, W])
        z0 = sb("z0", [P, NT, W + 1])
        z = sb("z", [P, NT, W])
        zT = sb("zT", [W + 1, 2, GN])
        ex = sb("ex", [P, 2, GN])
        rs = sb("rs", [P, 2, GT])
        gm = sb("gm", [P, NT])
        gd = sb("gd", [P, NT, E])
        gv = sb("gv", [P, NT, E])
        gbest = sb("gbest", [P, NT])
        goh = sb("goh", [P, NT, E], BF16)
        gex = sb("gex", [P, NT, E])
        gsum = sb("gsum", [P, NT])
        prob = sb("prob", [P, NT])
        pc = sb("pc", [P, NT, E])
        pos1 = sb("pos1", [P, NT])
        kept = sb("kept", [P, NT])
        base = sb("base", [P, NT])
        slot = sb("slot", [P, NT])
        slot2 = sb("slot2", [P, NT])
        cpos = sb("cpos", [P, NT])
        idx_s = sb("idx_s", [P, NT], I32)
        idx_g = sb("idx_g", [P, NT], I32)
        pk = sb("pk", [P, NT])
        xe = w1[:, :, :].rearrange("p l f -> p (l f)")[:, 0:ST * W].rearrange("p (t w) -> p t w", t=ST)
        xeT = stream[0:W, :, :, :].rearrange("p a t d -> p (a t d)")[:, 0:ST * P]
        hm = sb("hm", [P, 2, EC, CAP])
        ye = w1s[:, :, :].rearrange("p l f -> p (l f)")[:, 0:E * 3 * W].rearrange("p (e m w) -> p e m w", e=E, m=3)
        yg = sb("yg", [P, NT, W])
        yp = sb("yp", [P, GT, W])
        ya = sb("ya", [P, GT, W])
        yc = sb("yc", [P, GT, W])
        yn = sb("yn", [P, GT, W])
        yfin = sb("yfin", [P, GT, W], U32)
        km = gT[:, :, :, :].rearrange("p b t (h k) -> p b t h k", h=H1)
        qbd = sb("qbd", [P, 2, GT, P])
        VW = 2 * (HD + 1)
        vz = sb("vz", [P, 2, GT * 2, HP, VW])
        hn_flat = hn[:, :, :].rearrange("p g n -> p (g n)")
        sm = hn_flat[:, 0:2 * H1 * WS].rearrange("p (b h k) -> p b h k", b=2, h=H1)
        smx = sb("smx", [P, 2, H1])
        sd = hn_flat[:, 2 * H1 * WS:4 * H1 * WS].rearrange("p (b h k) -> p b h k", b=2, h=H1)
        pe_ = sb("pe_", [P, 2, H1 * WS])
        pT = sb("pT", [P, 2, HP, P])
        rden = sb("rden", [P, 2, H1])
        o = sb("o", [P, NT, W])
        rhT = sb("rhT", [RH + 1, 2, GN])
        tm = sb("tm", [P, GT])
        td = sb("td", [P, GT, X])
        te = sb("te", [P, GT, X])
        tsum = sb("tsum", [P, GT])
        trs = sb("trs", [P, GT])
        tp = sb("tp", [P, GT, X])
        m1 = sb("m1", [P, GT])
        m2 = sb("m2", [P, GT])
        teq = sb("teq", [P, GT, X])
        tv = sb("tv", [P, GT, X])
        tb = sb("tb", [P, GT])
        o1 = sb("o1", [P, GT, X])
        o2 = sb("o2", [P, GT, X])
        tdl = sb("tdl", [P, GT])
        tex = sb("tex", [P, GT])
        tw0 = sb("tw0", [P, GT])
        tw1 = sb("tw1", [P, GT])
        tw2 = sb("tw2", [P, GT])
        route = sb("route", [P, NT, X])
        routeT = sb("routeT", [X, 2, GN])
        h1T = scan_io[:, :, :].rearrange("p a n -> p (a n)")[:, 0:2 * XP * GN].rearrange("p (b q n) -> p b q n", b=2, q=XP)
        h2T = stream[:, :, :, :].rearrange("p a t d -> p (a t d)")[:, 0:2 * XP * GN].rearrange("p (b q n) -> p b q n", b=2, q=XP)
        res = w2[:, :, :, :].rearrange("p l c d -> p (l c d)")[:, 0:NT * W].rearrange("p (t w) -> p t w", t=NT)

        banks = [ctx.enter_context(nc.psum_tensor(f"bank{i}", [P, 512], F32)) for i in range(8)]
        wide = Ring(banks[0:4], sem("wide_filled"), {"act": sem("wide_freed_act"), "dve": sem("wide_freed_dve")})
        turn = Ring(banks[4:6], sem("turn_filled"), {"act": sem("turn_freed_act")})
        outp = Ring(banks[6:8], sem("outp_filled"), {"act": sem("outp_freed_act"), "dve": sem("outp_freed_dve")})

        turn.add("emb", "act")
        turn.add("rows", "act")
        outp.add("table", "dve")
        outp.add("b1", "dve")
        for g in range(NG + 1):
            if g < NG:
                wide.add(("u", g), "dve")
            if g >= 1:
                outp.add(("y", g - 1), "dve")
        for n in range(NSTEP + 1):
            if n < NSTEP:
                turn.add(("hT", n), "act")
                for c in range(FC):
                    wide.add(("h", n, c), "act")
            if n >= 1:
                outp.add(("o", n - 1), "dve")
        for g in range(NG):
            turn.add(("xT", g), "act")
            outp.add(("head", g), "dve")
        for s in range(NG + 1):
            if s < NG:
                turn.add(("a0", s), "act")
                wide.add(("s0", s), "act")
            if s >= 1:
                outp.add(("ctx", s - 1), "dve")
        for s in range(NG + 1):
            if s < NG:
                turn.add(("f0", s), "act")
                outp.add(("gate", s), "dve")
            if s >= 1:
                outp.add(("pos", s - 1), "dve")
        turn.add("qkv_w", "act")
        turn.add("proj_w", "act")
        outp.add("relb", "act")
        XG = ST // 4
        for k in range(XG):
            turn.add(("xe", k), "act")
        for e in range(E + 1):
            if e < E:
                wide.add(("em", e, 0), "act")
                wide.add(("em", e, 1), "dve")
            if e >= 1:
                outp.add(("ey", e - 1), "dve")
        LAG_T, LAG_A, LAG_P = 3, 4, 6
        STEPS1 = NT + LAG_P

        def qkv_group(s):
            return s // GT if s % GT == 0 and s < NT else None

        def proj_group(s):
            t = s - LAG_P + 1
            return t // GT - 1 if t > 0 and t % GT == 0 and t // GT <= NG else None

        for s in range(STEPS1):
            if (g := qkv_group(s)) is not None:
                turn.add(("a1", g), "act")
                wide.add(("k", g), "dve")
                wide.add(("q", g), "act")
                outp.add(("v", g), "act")
            if s < NT:
                wide.add(("s1", s), "dve")
            if 0 <= s - LAG_T < NT:
                turn.add(("pT", s - LAG_T), "act")
            if 0 <= s - LAG_A < NT:
                outp.add(("av", s - LAG_A), "dve")
            if (g := proj_group(s)) is not None:
                turn.add(("oT", g), "act")
                outp.add(("proj", g), "dve")
        for s in range(NG + 1):
            if s < NG:
                turn.add(("f1", s), "act")
                wide.add(("rh", s), "act")
                for q in range(XP):
                    wide.add(("h1", s, q), "act")
                outp.add(("rl", s), "dve")
                for q in range(XP):
                    wide.add(("h2", s, q), "dve")
            if s >= 1:
                turn.add(("rT", s - 1), "act")
                outp.add(("b3", s - 1), "dve")
                for j in range(GT):
                    wide.add(("eo", s - 1, j), "dve")

        LNS = []
        for g in range(NG):
            LNS += [("y", g), ("c", g)]
        for n in range(NG, NSTEP):
            LNS.append(("c", n))
        for g in range(NG):
            LNS.append(("a0", g))
        for g in range(NG):
            LNS.append(("f0", g))
        for g in range(NG):
            LNS.append(("a1", g))
        for g in range(NG):
            LNS.append(("f1", g))

        in_emb, in_tok, in_rows, in_wf, in_norm = map(sem, ["in_emb", "in_tok", "in_rows", "in_wf", "in_norm"])
        in_w1 = [sem(f"in_w1_{i}") for i in range(L)]
        in_w2 = [sem(f"in_w2_{i}") for i in range(L)]
        in_b2, in_head, in_gate, in_exp, in_att, in_x1, in_xbd = map(
            sem, ["in_b2", "in_head", "in_gate", "in_exp", "in_att", "in_x1", "in_xbd"])
        zero_rows, scattered, rows_back, ye_out, gathered, stored = map(
            sem, ["zero_rows", "scattered", "rows_back", "ye_out", "gathered", "stored"])
        pool_step, ident_ready, const_ready, zeros_ready, xb_ready, rstd_ready, sd_ready = map(
            sem, ["pool_step", "ident_ready", "const_ready", "zeros_ready", "xb_ready", "rstd_ready", "sd_ready"])
        dve_step, stats_ready, table_ready, hot_ready, mems_ready, b1_ready, w1s_ready, x_ready, hn_ready = map(
            sem, ["dve_step", "stats_ready", "table_ready", "hot_ready", "mems_ready", "b1_ready", "w1s_ready",
                  "x_ready", "hn_ready"])
        z_ready, goh_ready, gd_ready, idx_ready, em_dve, ye_ready, km_ready, smx_ready, o_ready = map(
            sem, ["z_ready", "goh_ready", "gd_ready", "idx_ready", "em_dve", "ye_ready", "km_ready", "smx_ready",
                  "o_ready"])
        td_ready, tdl_ready, route_ready, h2_ready, res_ready, embf_ready = map(
            sem, ["td_ready", "tdl_ready", "route_ready", "h2_ready", "res_ready", "embf_ready"])
        act_step, embT_ready, cols_ready, decay_exp, hT_ready, gelu_ready, zT_ready, ex_ready, gex_ready = map(
            sem, ["act_step", "embT_ready", "cols_ready", "decay_exp", "hT_ready", "gelu_ready", "zT_ready",
                  "ex_ready", "gex_ready"])
        wT_ready, xeT_ready, em_act, qv_ready, pexp_ready, pT_ready, rh_ready, h1_ready, te_ready, tex_ready, rT_ready = map(
            sem, ["wT_ready", "xeT_ready", "em_act", "qv_ready", "pexp_ready", "pT_ready", "rh_ready", "h1_ready",
                  "te_ready", "tex_ready", "rT_ready"])

        ZT = [("a0", g) for g in range(NG)] + [("f0", g) for g in range(NG)]
        for s in range(STEPS1):
            if (g := qkv_group(s)) is not None:
                ZT.append(("a1", g))
            if (g := proj_group(s)) is not None:
                ZT.append(("oT", g))
        ZT += [("f1", g) for g in range(NG)]
        ZT_LAST = {"a0": (wide, lambda g: ("s0", g)), "f0": (outp, lambda g: ("gate", g)),
                   "a1": (outp, lambda g: ("v", g)), "oT": (outp, lambda g: ("proj", g)),
                   "f1": (wide, lambda g: ("h1", g, XP - 1))}

        def bc(ap, n):
            return ap.unsqueeze(2).broadcast_to([ap.shape[0], ap.shape[1], n])

        def bm(ap, n):
            return ap.unsqueeze(1).broadcast_to([ap.shape[0], n, ap.shape[1]])

        def over_partitions(ap, n=P):
            return bass.AP(ap.tensor, ap.offset, [[0, n]] + [list(d) for d in ap.ap])

        def row(ap):
            return ap.unsqueeze(0)

        block = ctx.enter_context(nc.Block())

        @block.sync
        def _(sp):
            sp.dma_start(tokens[:, :], over_partitions(a["x"].rearrange("b s -> (b s)"))).then_inc(in_tok, 16)
            sp.dma_start(emb[:, :], a["L0_tok_emb"]).then_inc(in_emb, 16)
            sp.dma_start(w_upd[:, :], a["L0_tok_W_upd"]).then_inc(in_emb, 16)
            sp.dma_start(b_upd[:, :], over_partitions(a["L0_tok_b_upd"], V)).then_inc(in_emb, 16)
            sp.dma_start(b_f[:, :], over_partitions(a["L0_tok_b_f"], V)).then_inc(in_emb, 16)
            sp.dma_start(decay_in[:, :], over_partitions(a["L0_tok_decay_param"])).then_inc(in_emb, 16)
            sp.dma_start(w_f[:, :], a["L0_tok_W_f"]).then_inc(in_wf, 16)
            sp.dma_start(norm_g[:, :], over_partitions(a["L0_tok_norm_g"])).then_inc(in_norm, 16)
            sp.dma_start(norm_b[:, :], over_partitions(a["L0_tok_norm_b"])).then_inc(in_norm, 16)
            sp.dma_start(rows[0:L, :], a["L0_tok_cms_ln_g"]).then_inc(in_rows, 16)
            sp.dma_start(rows[L:2 * L, :], a["L0_tok_cms_ln_b"]).then_inc(in_rows, 16)
            sp.dma_start(rows[R_B1:R_X2, :], a["L0_tok_cms_b1"].rearrange("l (c p) -> (l c) p", p=P)).then_inc(in_rows, 16)
            sp.dma_start(rows[R_X2:R_E1, :], a["L1_ffn_expert_b2"].rearrange("(q i) f -> q (i f)", i=2)).then_inc(in_rows, 16)
            sp.dma_start(rows[R_E1:NR, :], a["L0_ffn_b1"].rearrange("e (c p) -> (e c) p", p=P)).then_inc(in_rows, 16)
            for i in range(L):
                sp.dma_start(w1[:, i, :], a["L0_tok_cms_W1"][i]).then_inc(in_w1[i], 16)
                sp.dma_start(w2[:, i, :, :], a["L0_tok_cms_W2"][i].rearrange("(c p) d -> p c d", p=P)).then_inc(in_w2[i], 16)
                if i == 0:
                    sp.dma_start(b2[:, :, :], over_partitions(a["L0_tok_cms_b2"])).then_inc(in_b2, 16)
            sp.dma_start(head_w[:, :], a["L0_tok_head_W"]).then_inc(in_head, 16)
            sp.dma_start(head_b[:, :], over_partitions(a["L0_tok_head_b"])).then_inc(in_head, 16)
            sp.dma_start(gate_w[0:W, :], a["L0_ffn_gate_w"]).then_inc(in_gate, 16)
            sp.dma_start(gate_w[W:W + 1, :], row(a["L0_ffn_gate_b"])).then_inc(in_gate, 16)
            sp.wait_ge(zeros_ready, 1)
            sp.dma_start(xbuf[0:SLOTS, :].rearrange("(p k) w -> p (k w)", p=P), zeros[:, :]).then_inc(zero_rows, 16)
            sp.dma_start(qkv_rows[:, 0, :], a["L1_attn_w_qkv"][0:P, :]).then_inc(in_att, 16)
            sp.dma_start(qkv_rows[0:W, 1, :], a["L1_attn_w_qkv"][P:3 * W, :]).then_inc(in_att, 16)
            sp.dma_start(proj_rows[:, :], a["L1_attn_w_proj"]).then_inc(in_att, 16)
            sp.dma_start(proj_w[W:W + 1, :], row(a["L1_attn_b_proj"])).then_inc(in_att, 16)
            rb = a["L1_attn_rel_bias"]
            sp.dma_start(relb_up[:, :], bass.AP(rb.tensor, rb.offset, [[1, WS], [1, WS]])).then_inc(in_att, 16)
            sp.dma_start(e_w1[:, :, :], a["L0_ffn_w1"].rearrange("e d f -> d e f")).then_inc(in_exp, 16)
            for e in range(E):
                sp.dma_start(e_w2[:, e, :, :], a["L0_ffn_w2"][e].rearrange("(c p) w -> p c w", p=P)).then_inc(in_exp, 16)
            sp.dma_start(e_b2[:, :, :], over_partitions(a["L0_ffn_b2"])).then_inc(in_exp, 16)
            sp.dma_start(r_w1[0:W, :], a["L1_ffn_router_w1"]).then_inc(in_x1, 16)
            sp.dma_start(r_w1[W:W + 1, :], row(a["L1_ffn_router_b1"])).then_inc(in_x1, 16)
            sp.dma_start(r_w2[0:RH, :], a["L1_ffn_router_w2"]).then_inc(in_x1, 16)
            sp.dma_start(r_w2[RH:RH + 1, :], row(a["L1_ffn_router_b2"])).then_inc(in_x1, 16)
            sp.dma_start(x_w1[0:W, :].rearrange("d (e f) -> d e f", e=X), a["L1_ffn_expert_w1"].rearrange("e d f -> d e f")).then_inc(in_x1, 16)
            sp.dma_start(x_w1[W:W + 1, :], row(a["L1_ffn_expert_b1"].rearrange("e f -> (e f)"))).then_inc(in_x1, 16)
            sp.dma_start(x_b3[:, :], a["L1_ffn_expert_b3"]).then_inc(in_x1, 16)
            sp.wait_ge(zeros_ready, 3)
            for i in range(2):
                part = slice(i * W, (i + 1) * W)
                sp.dma_start(x_w2[part, :, part], a["L1_ffn_expert_w2"].rearrange("(q i) f g -> i f q g", i=2)[i]).then_inc(in_xbd, 16)
                sp.dma_start(x_w3[part, :, part], a["L1_ffn_expert_w3"].rearrange("(q i) f g -> i f q g", i=2)[i]).then_inc(in_xbd, 16)
            sp.wait_ge(scattered, 16 * NT)
            xr = xbuf[0:SLOTS, :].rearrange("(t p) w -> p t w", p=P)
            for k in range(XG):
                sp.dma_start(xe[:, 4 * k:4 * k + 4, :], xr[:, 4 * k:4 * k + 4, :]).then_inc(rows_back, 16)
                sp.wait_ge(rows_back, 16 * (k + 1))
            for e in range(E):
                sp.wait_ge(ye_ready, e + 1)
                sp.dma_start(ybuf[e * CAP:e * CAP + 2 * P, :].rearrange("(m p) w -> p m w", p=P), ye[:, e, 0:2, :]).then_inc(ye_out, 16)
                sp.dma_start(ybuf[e * CAP + 2 * P:(e + 1) * CAP, :], ye[0:CAP - 2 * P, e, 2, :]).then_inc(ye_out, 16)
            for g in range(NG):
                sp.wait_ge(res_ready, g + 1)
                sp.dma_start(out.rearrange("b s w -> s b w")[:, g * GT:(g + 1) * GT, :], res[:, g * GT:(g + 1) * GT, :]).then_inc(stored, 16)
            sp.wait_ge(stored, 16 * NG)

        @block.gpsimd
        def _(pool):
            steps = [0]

            def link(ins):
                steps[0] += 1
                ins.then_inc(pool_step, 1)
                pool.wait_ge(pool_step, steps[0])

            link(nc.gpsimd.memset(ident[:, :], 0.0))
            nc.gpsimd.affine_select(out=ident[:, :], in_=ident[:, :], compare_op=ALU.not_equal, fill=1.0, base=0,
                                    pattern=[[-1, P]], channel_multiplier=1).then_inc(ident_ready, 1)
            pool.wait_ge(ident_ready, 1)
            nc.gpsimd.iota(iota_v[:, :], pattern=[[0, 1]], base=0, channel_multiplier=1).then_inc(const_ready, 1)
            pool.wait_ge(const_ready, 1)
            nc.gpsimd.memset(neg_half[:, :], -0.5).then_inc(const_ready, 1)
            pool.wait_ge(const_ready, 2)
            link(nc.gpsimd.memset(tri[:, :], 1.0))
            nc.gpsimd.affine_select(out=tri[:, :], in_=tri[:, :], compare_op=ALU.is_ge, fill=0.0, base=0,
                                    pattern=[[1, P]], channel_multiplier=-1).then_inc(const_ready, 1)
            pool.wait_ge(const_ready, 3)
            nc.gpsimd.memset(ones_b[:, :], 1.0).then_inc(const_ready, 1)
            pool.wait_ge(const_ready, 4)
            nc.gpsimd.iota(rank_i[:, :], pattern=[[-1, E]], base=E, channel_multiplier=0).then_inc(const_ready, 1)
            pool.wait_ge(const_ready, 5)
            nc.gpsimd.iota(trash_i[:, :], pattern=[[P, NT]], base=SLOTS, channel_multiplier=1).then_inc(const_ready, 1)
            pool.wait_ge(const_ready, 6)
            link(nc.gpsimd.memset(flip[:, :, :], 0.0))
            nc.gpsimd.affine_select(out=flip[:, :, :], in_=flip[:, :, :], compare_op=ALU.not_equal, fill=1.0, base=1 - WS,
                                    pattern=[[0, 2], [1, WS]], channel_multiplier=1).then_inc(const_ready, 1)
            pool.wait_ge(const_ready, 7)
            link(nc.gpsimd.memset(headmask[:, :], 1.0))
            for w in range(2):
                part = headmask[w * W:(w + 1) * W, :]
                link(nc.gpsimd.affine_select(out=part, in_=part, compare_op=ALU.is_ge, fill=0.0, base=0,
                                             pattern=[[-HD, H1]], channel_multiplier=1))
                last = nc.gpsimd.affine_select(out=part, in_=part, compare_op=ALU.is_ge, fill=0.0, base=HD - 1,
                                               pattern=[[HD, H1]], channel_multiplier=-1)
                if w == 0:
                    link(last)
            last.then_inc(const_ready, 1)
            pool.wait_ge(const_ready, 8)
            nc.gpsimd.memset(zeros[:, :], 0.0).then_inc(zeros_ready, 1)
            pool.wait_ge(zeros_ready, 1)
            nc.gpsimd.memset(x_w2[:, :, :], 0.0).then_inc(zeros_ready, 1)
            pool.wait_ge(zeros_ready, 2)
            nc.gpsimd.memset(x_w3[:, :, :], 0.0).then_inc(zeros_ready, 1)
            pool.wait_ge(zeros_ready, 3)

            def ln_root(k):
                pool.wait_ge(stats_ready, k + 1)
                link(nc.gpsimd.tensor_scalar_add(ve[:, k % 2, :], mv[:, k % 2, :, 1], EPS))
                nc.gpsimd.tensor_tensor(rstd[:, k % 2, :], ve[:, k % 2, :], neg_half[:, :], ALU.pow).then_inc(rstd_ready, 1)
                pool.wait_ge(rstd_ready, k + 1)

            def add_b2(n):
                i, g = n // NG, n % NG
                if n == 0:
                    pool.wait_ge(in_b2, 16)
                pool.wait_ge(x_ready, n + 1)
                t = slice(g * GT, (g + 1) * GT)
                nc.gpsimd.tensor_tensor(xb[:, t, :], x[:, t, :], bm(b2[:, i, :], GT), ALU.add).then_inc(xb_ready, 1)
                pool.wait_ge(xb_ready, n + 1)

            for k, (kind, n) in enumerate(LNS):
                if kind == "a1" and n == 0:
                    break
                ln_root(k)
                if kind == "c":
                    add_b2(n)
                if kind == "y" and n == 1:
                    link(nc.gpsimd.memset(z0[:, :, W], 1.0))
                    link(nc.gpsimd.memset(zT[W:W + 1, :, :], 1.0))
                    link(nc.gpsimd.memset(rhT[RH:RH + 1, :, :], 1.0))
                    link(nc.gpsimd.memset(qbd[:, :, :, :], 0.0))
                    link(nc.gpsimd.memset(vz[:, :, :, :, :], 0.0))
                    link(nc.gpsimd.memset(vz[0:WS, :, :, :, HD], 1.0))
                    nc.gpsimd.memset(vz[WS:P, :, :, :, VW - 1], 1.0).then_inc(zeros_ready, 1)
                    pool.wait_ge(zeros_ready, 4)
            k1 = k
            pool.wait_ge(zero_rows, 16)
            for g in range(NG):
                pool.wait_ge(idx_ready, g + 1)
                for t in range(g * GT, (g + 1) * GT):
                    nc.gpsimd.indirect_dma_start(out=xbuf[:, :], out_offset=bass.IndirectOffsetOnAxis(ap=idx_s[:, t:t + 1], axis=0),
                                                 in_=z[:, t, :], in_offset=None).then_inc(scattered, 16)
            pool.wait_ge(ye_out, 32 * E)
            for t in range(NT):
                nc.gpsimd.indirect_dma_start(out=yg[:, t, :], out_offset=None, in_=ybuf[:, :],
                                             in_offset=bass.IndirectOffsetOnAxis(ap=idx_g[:, t:t + 1], axis=0)).then_inc(gathered, 16)
            for g in range(NG):
                ln_root(k1 + g)

            def sub_max(t):
                pool.wait_ge(smx_ready, t + 1)
                if t >= 2:
                    pool.wait_ge(pexp_ready, t - 1)
                nc.gpsimd.tensor_tensor(sd[:, t % 2, :, :], sm[:, t % 2, :, :], bc(smx[:, t % 2, :], WS), ALU.subtract).then_inc(sd_ready, 1)
                pool.wait_ge(sd_ready, t + 1)

            for s in range(STEPS1):
                if s < NT:
                    sub_max(s)
                if (g := proj_group(s)) is not None:
                    ln_root(k1 + NG + g)

        @block.scalar
        def _(act):
            steps = [0]

            def link(ins):
                steps[0] += 1
                ins.then_inc(act_step, 1)
                act.wait_ge(act_step, steps[0])

            def copy(dst, src):
                return nc.scalar.activation(dst, src, ACT.Copy)

            act.wait_ge(in_emb, 80)
            nc.scalar.activation(decay[:, 0:1], decay_in[:, :], ACT.Exp, scale=-1.0).then_inc(decay_exp, 1)
            act.wait_ge(turn.filled, turn.number("emb"))
            link(copy(embT[:, :], turn.bank("emb")[:, 0:V]))
            act.sem_inc(embT_ready, 1)
            act.sem_inc(turn.freed["act"], 1)
            act.wait_ge(turn.filled, turn.number("rows"))
            link(copy(cols[:, :], turn.bank("rows")[:, 0:NR]))
            act.sem_inc(cols_ready, 1)
            act.sem_inc(turn.freed["act"], 1)

            for n in range(NSTEP):
                i = n // NG
                act.wait_ge(turn.filled, turn.number(("hT", n)))
                if n >= 2:
                    act.wait_ge(wide.filled, wide.number(("h", n - 2, FC - 1)))
                copy(hT[:, n % 2, :], turn.bank(("hT", n))[:, :]).then_inc(turn.freed["act"], 1)
                if n == 0:
                    act.wait_ge(b1_ready, 1)
                for c in range(FC):
                    act.wait_ge(wide.filled, wide.number(("h", n, c)))
                    if n >= 2 and c == 0:
                        act.wait_ge(outp.filled, outp.number(("o", n - 2)))
                    nc.scalar.activation(gT[:, n % 2, c, :], wide.bank(("h", n, c))[:, :], ACT.Gelu,
                                         bias=b1[:, i * FC + c:i * FC + c + 1]).then_inc(wide.freed["act"], 1)
            for g in range(NG):
                act.wait_ge(turn.filled, turn.number(("xT", g)))
                act.wait_ge(wide.filled, wide.number(("h", NSTEP - 1, FC - 1)))
                if g >= 2:
                    act.wait_ge(outp.filled, outp.number(("head", g - 2)))
                copy(hT[:, g % 2, :], turn.bank(("xT", g))[:, :]).then_inc(turn.freed["act"], 1)

            def zT_copy(key):
                i = ZT.index(key)
                if i == 0:
                    act.wait_ge(zeros_ready, 4)
                act.wait_ge(turn.filled, turn.number(key))
                if i >= 2:
                    kind, g = ZT[i - 2]
                    ring, job = ZT_LAST[kind]
                    act.wait_ge(ring.filled, ring.number(job(g)))
                copy(zT[0:W, i % 2, :], turn.bank(key)[0:W, :]).then_inc(turn.freed["act"], 1)

            for g in range(NG):
                zT_copy(("a0", g))
                act.wait_ge(wide.filled, wide.number(("s0", g)))
                if g >= 2:
                    act.wait_ge(outp.filled, outp.number(("ctx", g - 2)))
                nc.scalar.activation(ex[:, g % 2, :], wide.bank(("s0", g))[:, :], ACT.Exp, scale=float(W) ** -0.5).then_inc(wide.freed["act"], 1)
            for g in range(NG):
                zT_copy(("f0", g))
                act.wait_ge(gd_ready, g + 1)
                t = slice(g * GT, (g + 1) * GT)
                nc.scalar.activation(gex[:, t, :], gd[:, t, :], ACT.Exp).then_inc(gex_ready, 1)
            act.wait_ge(turn.filled, turn.number("qkv_w"))
            link(copy(qkv_w[:, :], turn.bank("qkv_w")[0:W, 0:3 * W]))
            act.sem_inc(turn.freed["act"], 1)
            act.wait_ge(turn.filled, turn.number("proj_w"))
            act.wait_ge(in_att, 80)
            link(copy(proj_w[0:W, :], turn.bank("proj_w")[0:W, 0:W]))
            act.sem_inc(turn.freed["act"], 1)
            act.wait_ge(outp.filled, outp.number("relb"))
            copy(relb[:, :], outp.bank("relb")[:, 0:WS]).then_inc(outp.freed["act"], 1)
            act.wait_ge(outp.freed["act"], 1)
            act.sem_inc(wT_ready, 1)
            for k in range(XG):
                act.wait_ge(turn.filled, turn.number(("xe", k)))
                copy(xeT[:, k * 512:(k + 1) * 512], turn.bank(("xe", k))[0:W, :]).then_inc(turn.freed["act"], 1)
            for e in range(E):
                act.wait_ge(wide.filled, wide.number(("em", e, 0)))
                if e >= 2:
                    act.wait_ge(outp.filled, outp.number(("ey", e - 2)))
                nc.scalar.activation(hm[:, e % 2, 0, :], wide.bank(("em", e, 0))[:, 0:CAP], ACT.Relu,
                                     bias=cols[:, R_E1 + e * EC:R_E1 + e * EC + 1]).then_inc(wide.freed["act"], 1)

            def qkv_copies(g):
                zT_copy(("a1", g))
                act.wait_ge(wide.filled, wide.number(("q", g)))
                if g >= 2:
                    act.wait_ge(wide.filled, wide.number(("s1", (g - 1) * GT - 1)))
                q = wide.bank(("q", g))[:, 0:GT * WS].rearrange("p (t q) -> p t q", t=GT)
                for w in range(2):
                    part = slice(w * W, (w + 1) * W)
                    last = copy(qbd[part, g % 2, :, w * WS:(w + 1) * WS], q[part])
                last.then_inc(wide.freed["act"], 1)
                act.wait_ge(outp.filled, outp.number(("v", g)))
                if g >= 2:
                    act.wait_ge(outp.filled, outp.number(("av", (g - 1) * GT - 1)))
                v = outp.bank(("v", g))[:, :].rearrange("p (t h i d) -> p t h i d", t=2 * GT, h=HP, i=2)
                for i in range(2):
                    part = slice(i * WS, (i + 1) * WS)
                    last = copy(vz[part, g % 2, :, :, i * (HD + 1):i * (HD + 1) + HD], v[part, :, :, i, :])
                last.then_inc(outp.freed["act"], 1)

            def probs(t):
                act.wait_ge(sd_ready, t + 1)
                if t >= 2:
                    act.wait_ge(turn.filled, turn.number(("pT", t - 2)))
                nc.scalar.activation(pe_[:, t % 2, :], sd[:, t % 2, :, :].rearrange("p h k -> p (h k)"), ACT.Exp).then_inc(pexp_ready, 1)

            def probs_turned(t):
                act.wait_ge(turn.filled, turn.number(("pT", t)))
                if t >= 2:
                    act.wait_ge(outp.filled, outp.number(("av", t - 2)))
                copy(pT[:, t % 2, :, :].rearrange("p h q -> p (h q)"), turn.bank(("pT", t))[:, :]).then_inc(turn.freed["act"], 1)

            for s in range(STEPS1):
                if (g := qkv_group(s)) is not None:
                    qkv_copies(g)
                if 0 <= s - 1 < NT:
                    probs(s - 1)
                if 0 <= s - LAG_T < NT:
                    probs_turned(s - LAG_T)
                if (g := proj_group(s)) is not None:
                    zT_copy(("oT", g))

            for s in range(NG + 1):
                if s < NG:
                    zT_copy(("f1", s))
                    act.wait_ge(wide.filled, wide.number(("rh", s)))
                    if s >= 2:
                        act.wait_ge(outp.filled, outp.number(("rl", s - 2)))
                    nc.scalar.activation(rhT[0:RH, s % 2, :], wide.bank(("rh", s))[0:RH, :], ACT.Relu).then_inc(wide.freed["act"], 1)
                    for q in range(XP):
                        act.wait_ge(wide.filled, wide.number(("h1", s, q)))
                        if s >= 2:
                            act.wait_ge(wide.filled, wide.number(("h2", s - 2, XP - 1)))
                        nc.scalar.activation(h1T[:, s % 2, q, :], wide.bank(("h1", s, q))[:, :], ACT.Relu).then_inc(wide.freed["act"], 1)
                    act.wait_ge(td_ready, s + 1)
                    nc.scalar.activation(te[:, :, :], td[:, :, :], ACT.Exp).then_inc(te_ready, 1)
                    act.wait_ge(tdl_ready, s + 1)
                    nc.scalar.activation(tex[:, :], tdl[:, :], ACT.Exp).then_inc(tex_ready, 1)
                if s >= 1:
                    act.wait_ge(turn.filled, turn.number(("rT", s - 1)))
                    if s >= 3:
                        act.wait_ge(outp.filled, outp.number(("b3", s - 3)))
                    copy(routeT[:, (s - 1) % 2, :], turn.bank(("rT", s - 1))[0:X, :]).then_inc(turn.freed["act"], 1)

        @block.vector
        def _(dve):
            steps = [0]
            v = nc.vector

            def link(ins):
                steps[0] += 1
                ins.then_inc(dve_step, 1)
                dve.wait_ge(dve_step, steps[0])

            def group(g):
                return slice(g * GT, (g + 1) * GT)

            def ln_stats(key, src):
                k = LNS.index(key)
                for j in range(GT):
                    last = v.bn_stats(st[:, k % 2, j, :], src(j))
                link(last)
                for j in range(GT):
                    last = v.bn_aggr(mv[:, k % 2, j, :], st[:, k % 2, j, :])
                last.then_inc(stats_ready, 1)
                dve.wait_ge(stats_ready, k + 1)

            def ln_norm(key, src, dst):
                k = LNS.index(key)
                dve.wait_ge(rstd_ready, k + 1)
                for j in range(GT):
                    last = v.tensor_scalar(dst(j), src(j), mv[:, k % 2, j, 0:1], rstd[:, k % 2, j:j + 1], ALU.subtract, ALU.mult)
                return last

            dve.wait_ge(const_ready, 8)
            link(v.tensor_copy(iota_vf[:, :], iota_v[:, :]))
            v.tensor_copy(rank8[:, :], rank_i[:, :])
            v.tensor_scalar(rank6[:, :], rank_i[:, 0:X], float(X - E), None, ALU.add)
            v.tensor_copy(trash[:, :], trash_i[:, :])
            link(v.tensor_scalar(not_zero[:, :], iota_vf[:, :], 0.0, None, ALU.not_equal))
            dve.wait_ge(in_emb, 80)
            v.tensor_tensor(embf[:, :], emb[:, :], b_f[:, :], ALU.add).then_inc(embf_ready, 1)
            dve.wait_ge(decay_exp, 1)
            link(v.tensor_scalar(decay[:, 1:2], decay[:, 0:1], 1.0, None, ALU.add))
            link(v.reciprocal(decay[:, 2:3], decay[:, 1:2]))
            link(v.tensor_scalar(decay[:, 3:4], decay[:, 2:3], -1.0, None, ALU.add))
            dve.wait_ge(in_tok, 16)
            for g in range(NG):
                c = slice(g * GN, (g + 1) * GN)
                v.tensor_scalar(onehot[:, c], tokens[0:V, c], iota_vf[:, 0:1], None, ALU.is_equal).then_inc(hot_ready, 1)
                if g == 0:
                    dve.wait_ge(outp.filled, outp.number("table"))
                    v.tensor_tensor(table0[:, :], outp.bank("table")[0:V, 0:D], b_upd[:, :], ALU.add).then_inc(outp.freed["dve"], 1)
                    dve.wait_ge(outp.freed["dve"], 1)
                    v.tensor_scalar(table[:, :], table0[:, :], not_zero[:, 0:1], None, ALU.mult).then_inc(table_ready, 1)
                link(v.tensor_scalar(keep_mem[:, c], tokens[:, c], 0.0, None, ALU.not_equal))
                link(v.tensor_scalar(keep_mem[:, c], keep_mem[:, c], decay[:, 3:4], 1.0, ALU.mult, ALU.add))
                link(v.memset(keep_mem[:, c].rearrange("p (t s) -> p t s", s=P)[:, :, 0:1], 0.0))
            dve.wait_ge(cols_ready, 1)
            dve.wait_ge(outp.filled, outp.number("b1"))
            v.tensor_tensor(b1[:, :], outp.bank("b1")[:, 0:L * FC], cols[:, R_B1:R_X2], ALU.add).then_inc(outp.freed["dve"], 1)
            dve.wait_ge(outp.freed["dve"], 2)
            dve.sem_inc(b1_ready, 1)
            for i in range(L):
                v.tensor_scalar(w1s[:, i, :], w1[:, i, :], cols[:, i:i + 1], None, ALU.mult).then_inc(w1s_ready, 1)

            dve.wait_ge(in_norm, 32)
            for s in range(NG + 1):
                if s < NG:
                    c = slice(s * GN, (s + 1) * GN)
                    dve.wait_ge(wide.filled, wide.number(("u", s)))
                    v.tensor_tensor_scan(mems[:, c], keep_mem[:, c], wide.bank(("u", s))[:, :], 0.0, ALU.mult, ALU.add).then_inc(wide.freed["dve"], 1)
                if s >= 1:
                    g = s - 1
                    dve.wait_ge(outp.filled, outp.number(("y", g)))
                    y = outp.bank(("y", g))[:, :].rearrange("p (t d) -> p t d", t=GT)
                    ln_stats(("y", g), lambda j: y[:, j, :])
                    k = LNS.index(("y", g))
                    dve.wait_ge(rstd_ready, k + 1)
                    for j in range(GT):
                        last = v.scalar_tensor_tensor(out=ln_t[:, j, :], in0=y[:, j, :], scalar=mv[:, k % 2, j, 0:1], in1=norm_g[:, :],
                                                      op0=ALU.subtract, op1=ALU.mult)
                    last.then_inc(outp.freed["dve"], 1)
                    dve.wait_ge(outp.freed["dve"], 3 + g)
                    for j in range(GT):
                        last = v.scalar_tensor_tensor(out=x[:, g * GT + j, :], in0=ln_t[:, j, :], scalar=rstd[:, k % 2, j:j + 1],
                                                      in1=norm_b[:, :], op0=ALU.mult, op1=ALU.add)
                    last.then_inc(x_ready, 1)
                    dve.wait_ge(x_ready, g + 1)
                    ln_stats(("c", g), lambda j: x[:, g * GT + j, :])
                    ln_norm(("c", g), lambda j: x[:, g * GT + j, :],
                            lambda j: hn[:, g, j * P:(j + 1) * P]).then_inc(hn_ready, 1)

            def norm_next(n):
                g = n % NG
                ln_norm(("c", n), lambda j: x[:, g * GT + j, :], lambda j: hn[:, g, j * P:(j + 1) * P]).then_inc(hn_ready, 1)

            for n in range(NSTEP):
                g = n % NG
                dve.wait_ge(outp.filled, outp.number(("o", n)))
                dve.wait_ge(xb_ready, n + 1)
                v.tensor_tensor(x[:, group(g), :], outp.bank(("o", n))[:, :].rearrange("p (t d) -> p t d", t=GT), xb[:, group(g), :],
                                ALU.add).then_inc(x_ready, 1)
                dve.wait_ge(x_ready, NG + n + 1)
                dve.sem_inc(outp.freed["dve"], 1)
                if n + NG < NSTEP:
                    ln_stats(("c", n + NG), lambda j: x[:, g * GT + j, :])
                    norm_next(n + NG)
            dve.wait_ge(in_head, 32)
            for g in range(NG):
                dve.wait_ge(outp.filled, outp.number(("head", g)))
                link(v.tensor_tensor(h[:, group(g), :], outp.bank(("head", g))[:, 0:GT * W].rearrange("p (t w) -> p t w", t=GT),
                                     bm(head_b[:, :], GT), ALU.add))
                dve.sem_inc(outp.freed["dve"], 1)
                ln_stats(("a0", g), lambda j: h[:, g * GT + j, :])
                ln_norm(("a0", g), lambda j: h[:, g * GT + j, :], lambda j: z0[:, g * GT + j, 0:W]).then_inc(z_ready, 1)
            for g in range(NG):
                dve.wait_ge(outp.filled, outp.number(("ctx", g)))
                c = outp.bank(("ctx", g))[:, 0:GT * (W + 1)].rearrange("p (t w) -> p t w", t=GT)
                link(v.reciprocal(rs[:, g % 2, :], c[:, :, W]))
                for j in range(GT):
                    last = v.scalar_tensor_tensor(out=h[:, g * GT + j, :], in0=c[:, j, 0:W], scalar=rs[:, g % 2, j:j + 1],
                                                  in1=h[:, g * GT + j, :], op0=ALU.mult, op1=ALU.add)
                link(last)
                dve.sem_inc(outp.freed["dve"], 1)
                ln_stats(("f0", g), lambda j: h[:, g * GT + j, :])
                ln_norm(("f0", g), lambda j: h[:, g * GT + j, :], lambda j: z[:, g * GT + j, :]).then_inc(z_ready, 1)

            def gate(g):
                t = group(g)
                dve.wait_ge(outp.filled, outp.number(("gate", g)))
                lg = outp.bank(("gate", g))[:, 0:GT * E].rearrange("p (t e) -> p t e", t=GT)
                link(v.tensor_reduce(gm[:, t], lg, AX, ALU.max))
                v.tensor_tensor(gd[:, t, :], lg, bc(gm[:, t], E), ALU.subtract).then_inc(gd_ready, 1)
                dve.wait_ge(gd_ready, g + 1)
                dve.sem_inc(outp.freed["dve"], 1)
                link(v.scalar_tensor_tensor(out=gv[:, t, :], in0=gd[:, t, :], scalar=0.0, in1=bm(rank8[:, :], GT), op0=ALU.is_equal, op1=ALU.mult))
                link(v.tensor_reduce(gbest[:, t], gv[:, t, :], AX, ALU.max))
                v.tensor_tensor(goh[:, t, :], bm(rank8[:, :], GT), bc(gbest[:, t], E), ALU.is_equal).then_inc(goh_ready, 1)
                v.tensor_scalar(base[:, t], gbest[:, t], -float(CAP), float(E * CAP - 1), ALU.mult, ALU.add)
                dve.wait_ge(gex_ready, g + 1)
                link(v.tensor_reduce(gsum[:, t], gex[:, t, :], AX, ALU.add))
                link(v.reciprocal(prob[:, t], gsum[:, t]))

            def place(g):
                t = group(g)
                dve.wait_ge(outp.filled, outp.number(("pos", g)))
                link(v.tensor_tensor(pc[:, t, :], outp.bank(("pos", g))[:, 0:GT * E].rearrange("p (t e) -> p t e", t=GT), goh[:, t, :], ALU.mult))
                dve.sem_inc(outp.freed["dve"], 1)
                link(v.tensor_reduce(pos1[:, t], pc[:, t, :], AX, ALU.add))
                v.tensor_scalar(kept[:, t], pos1[:, t], float(CAP), None, ALU.is_le)
                v.tensor_scalar(cpos[:, t], pos1[:, t], float(CAP), None, ALU.min)
                link(v.tensor_tensor(slot[:, t], base[:, t], trash[:, t], ALU.subtract))
                link(v.tensor_tensor(slot2[:, t], slot[:, t], pos1[:, t], ALU.add))
                link(v.tensor_tensor(slot[:, t], slot2[:, t], kept[:, t], ALU.mult))
                v.tensor_tensor(idx_g[:, t], cpos[:, t], base[:, t], ALU.add)
                v.tensor_tensor(pk[:, t], prob[:, t], kept[:, t], ALU.mult)
                v.tensor_tensor(idx_s[:, t], slot[:, t], trash[:, t], ALU.add).then_inc(idx_ready, 1)

            for s in range(NG + 1):
                if s < NG:
                    gate(s)
                if s >= 1:
                    place(s - 1)

            for e in range(E + 1):
                if e < E:
                    dve.wait_ge(wide.filled, wide.number(("em", e, 1)))
                    if e >= 2:
                        dve.wait_ge(outp.filled, outp.number(("ey", e - 2)))
                    v.tensor_scalar(hm[:, e % 2, 1, :], wide.bank(("em", e, 1))[:, 0:CAP], cols[:, R_E1 + e * EC + 1:R_E1 + e * EC + 2], 0.0,
                                    ALU.add, ALU.max).then_inc(wide.freed["dve"], 1)
                if e == 1:
                    dve.wait_ge(in_exp, 16 * (E + 2))
                if e >= 1:
                    q = e - 1
                    dve.wait_ge(outp.filled, outp.number(("ey", q)))
                    y = outp.bank(("ey", q))[:, 0:3 * W].rearrange("p (m w) -> p m w", m=3)
                    v.tensor_tensor(ye[:, q, 0:2, :], y[:, 0:2, :], bm(e_b2[:, q, :], 2), ALU.add)
                    R = CAP - 2 * P
                    v.tensor_tensor(ye[0:R, q, 2, :], y[0:R, 2, :], e_b2[0:R, q, :], ALU.add).then_inc(ye_ready, 1)
                    dve.wait_ge(ye_ready, q + 1)
                    dve.sem_inc(outp.freed["dve"], 1)
            for g in range(NG):
                t = group(g)
                dve.wait_ge(gathered, 16 * NT)
                link(v.tensor_tensor(yp[:, :, :], yg[:, t, :], bc(pk[:, t], W), ALU.mult))
                v.tensor_scalar(ya[:, :, :], yp[:, :, :], 0.0, None, ALU.max)
                link(v.tensor_scalar(yc[:, :, :], yp[:, :, :], 0.0, None, ALU.min))
                link(v.tensor_tensor(yn[:, :, :], ya[:, :, :], yc[:, :, :], ALU.add))
                v.tensor_scalar(yfin[:, :, :], yn[:, :, :], 0.0, 0.0, ALU.mult, ALU.is_equal)
                link(v.tensor_scalar(yc[:, :, :], yn[:, :, :], CLIP, -CLIP, ALU.min, ALU.max))
                link(v.copy_predicated(yc[:, :, :], yfin[:, :, :], yn[:, :, :]))
                link(v.tensor_tensor(h[:, t, :], h[:, t, :], yc[:, :, :], ALU.add))
                ln_stats(("a1", g), lambda j: h[:, g * GT + j, :])
                ln_norm(("a1", g), lambda j: h[:, g * GT + j, :], lambda j: z[:, g * GT + j, :]).then_inc(z_ready, 1)

            def k_masked(g):
                dve.wait_ge(wide.filled, wide.number(("k", g)))
                if g >= 2:
                    dve.wait_ge(wide.filled, wide.number(("s1", (g - 1) * GT - 1)))
                for j in range(GT):
                    last = v.tensor_tensor(km[:, g % 2, j, :, :], bm(wide.bank(("k", g))[:, j * WS:(j + 1) * WS], H1), bc(headmask[:, :], WS), ALU.mult)
                last.then_inc(km_ready, 1)
                dve.wait_ge(km_ready, g + 1)
                dve.sem_inc(wide.freed["dve"], 1)

            def biased(t):
                dve.wait_ge(wide.filled, wide.number(("s1", t)))
                if t >= 2:
                    dve.wait_ge(sd_ready, t - 1)
                s3 = wide.bank(("s1", t))[:, :].rearrange("p (h k) -> p h k", h=H1)
                link(v.scalar_tensor_tensor(out=sm[:, t % 2, :, :], in0=s3, scalar=float(HD) ** -0.5, in1=bm(relb[:, :], H1), op0=ALU.mult, op1=ALU.add))
                dve.sem_inc(wide.freed["dve"], 1)
                v.tensor_reduce(smx[:, t % 2, :], sm[:, t % 2, :, :], AX, ALU.max).then_inc(smx_ready, 1)

            def heads_out(t):
                dve.wait_ge(outp.filled, outp.number(("av", t)))
                av = outp.bank(("av", t))[:, 0:HP * 2 * VW].rearrange("p (h w i d) -> p w h i d", h=HP, w=2, i=2)
                r = rden[:, t % 2, :].rearrange("p (h i) -> p h i", i=2)
                for w in range(2):
                    part = slice(w * WS, (w + 1) * WS)
                    last = v.reciprocal(r[part], av[part, w, :, :, HD])
                link(last)
                for w in range(2):
                    part = slice(w * WS, (w + 1) * WS)
                    last = v.tensor_tensor(o[part, t, :].rearrange("p (h i d) -> p h i d", h=HP, i=2), av[part, w, :, :, 0:HD],
                                           r[part].unsqueeze(3).broadcast_to([WS, HP, 2, HD]), ALU.mult)
                last.then_inc(o_ready, 1)
                dve.wait_ge(o_ready, t + 1)
                dve.sem_inc(outp.freed["dve"], 1)

            dve.wait_ge(wT_ready, 1)
            for s in range(STEPS1):
                if (g := qkv_group(s)) is not None:
                    k_masked(g)
                if s < NT:
                    biased(s)
                if 0 <= s - LAG_A < NT:
                    heads_out(s - LAG_A)
                if (g := proj_group(s)) is not None:
                    dve.wait_ge(outp.filled, outp.number(("proj", g)))
                    link(v.tensor_tensor(h[:, group(g), :], outp.bank(("proj", g))[:, 0:GT * W].rearrange("p (t w) -> p t w", t=GT), h[:, group(g), :], ALU.add))
                    dve.sem_inc(outp.freed["dve"], 1)
                    ln_stats(("f1", g), lambda j: h[:, g * GT + j, :])
                    ln_norm(("f1", g), lambda j: h[:, g * GT + j, :], lambda j: z[:, g * GT + j, :]).then_inc(z_ready, 1)

            def first_highest(pr, top, hot):
                link(v.tensor_reduce(top[:, :], pr[:, :, :], AX, ALU.max))
                link(v.tensor_tensor(teq[:, :, :], pr[:, :, :], bc(top[:, :], X), ALU.is_equal))
                link(v.tensor_tensor(tv[:, :, :], teq[:, :, :], bm(rank6[:, :], GT), ALU.mult))
                link(v.tensor_reduce(tb[:, :], tv[:, :, :], AX, ALU.max))
                link(v.tensor_tensor(hot[:, :, :], bm(rank6[:, :], GT), bc(tb[:, :], X), ALU.is_equal))

            for s in range(NG + 1):
                if s < NG:
                    dve.wait_ge(outp.filled, outp.number(("rl", s)))
                    lg = outp.bank(("rl", s))[:, 0:GT * X].rearrange("p (t e) -> p t e", t=GT)
                    link(v.tensor_reduce(tm[:, :], lg, AX, ALU.max))
                    v.tensor_tensor(td[:, :, :], lg, bc(tm[:, :], X), ALU.subtract).then_inc(td_ready, 1)
                    dve.wait_ge(td_ready, s + 1)
                    dve.sem_inc(outp.freed["dve"], 1)
                    dve.wait_ge(te_ready, s + 1)
                    link(v.tensor_reduce(tsum[:, :], te[:, :, :], AX, ALU.add))
                    link(v.reciprocal(trs[:, :], tsum[:, :]))
                    link(v.tensor_tensor(tp[:, :, :], te[:, :, :], bc(trs[:, :], X), ALU.mult))
                    first_highest(tp, m1, o1)
                    link(v.scalar_tensor_tensor(out=tp[:, :, :], in0=o1[:, :, :], scalar=-4.0, in1=tp[:, :, :], op0=ALU.mult, op1=ALU.add))
                    first_highest(tp, m2, o2)
                    v.tensor_tensor(tdl[:, :], m2[:, :], m1[:, :], ALU.subtract).then_inc(tdl_ready, 1)
                    for q in range(XP):
                        dve.wait_ge(wide.filled, wide.number(("h2", s, q)))
                        if s >= 2:
                            dve.wait_ge(wide.filled, wide.number(("eo", s - 2, GT - 1)))
                        v.tensor_scalar(h2T[:, s % 2, q, :], wide.bank(("h2", s, q))[:, :], cols[:, R_X2 + q:R_X2 + q + 1], 0.0, ALU.add, ALU.max).then_inc(wide.freed["dve"], 1)
                    dve.wait_ge(tex_ready, s + 1)
                    link(v.tensor_scalar(tw0[:, :], tex[:, :], 1.0, None, ALU.add))
                    link(v.reciprocal(tw1[:, :], tw0[:, :]))
                    link(v.tensor_tensor(tw2[:, :], tw1[:, :], tex[:, :], ALU.mult))
                    link(v.tensor_tensor(o1[:, :, :], o1[:, :, :], bc(tw1[:, :], X), ALU.mult))
                    link(v.tensor_tensor(o2[:, :, :], o2[:, :, :], bc(tw2[:, :], X), ALU.mult))
                    v.tensor_tensor(route[:, group(s), :], o1[:, :, :], o2[:, :, :], ALU.add).then_inc(route_ready, 1)
                if s >= 1:
                    g = s - 1
                    dve.wait_ge(route_ready, g + 1)
                    dve.wait_ge(outp.filled, outp.number(("b3", g)))
                    link(v.tensor_tensor(res[:, group(g), :], outp.bank(("b3", g))[:, 0:GT * W].rearrange("p (t w) -> p t w", t=GT), h[:, group(g), :], ALU.add))
                    dve.sem_inc(outp.freed["dve"], 1)
                    for j in range(GT):
                        t = g * GT + j
                        dve.wait_ge(wide.filled, wide.number(("eo", g, j)))
                        for e in range(X):
                            ins = v.scalar_tensor_tensor(out=res[:, t, :], in0=wide.bank(("eo", g, j))[:, e * W:(e + 1) * W], scalar=route[:, t, e:e + 1],
                                                         in1=res[:, t, :], op0=ALU.mult, op1=ALU.add)
                            if e < X - 1:
                                link(ins)
                        ins.then_inc(wide.freed["dve"], 1)
                    wide.wait_read(dve, ("eo", g, GT - 1))
                    dve.sem_inc(res_ready, 1)

        @block.tensor
        def _(pe):
            def mm(o_, l_, r_, start=True, stop=True):
                return nc.tensor.matmul(o_, l_, r_, start=start, stop=stop)

            def turns(key, srcs, width):
                turn.wait_free(pe, key)
                for j, src in enumerate(srcs):
                    last = nc.tensor.transpose(turn.bank(key)[0:width, j * P:j * P + src.shape[0]], src, ident[0:src.shape[0], 0:src.shape[0]])
                last.then_inc(turn.filled, 1)

            pe.wait_ge(ident_ready, 1)
            pe.wait_ge(in_emb, 80)
            turns("emb", [emb[:, :]], D)
            pe.wait_ge(in_rows, 80)
            turns("rows", [rows[:, :]], P)
            pe.wait_ge(embT_ready, 1)
            mm(outp.bank("table")[0:V, 0:D], embT[:, :], w_upd[:, :]).then_inc(outp.filled, 1)
            pe.wait_ge(cols_ready, 1)
            for i in range(L):
                pe.wait_ge(in_w1[i], 16)
                for c in range(FC):
                    last = mm(outp.bank("b1")[:, i * FC + c:i * FC + c + 1], w1[:, i, c * P:(c + 1) * P], cols[:, L + i:L + i + 1])
            last.then_inc(outp.filled, 1)
            pe.wait_ge(table_ready, 1)
            pe.wait_ge(embf_ready, 1)
            pe.wait_ge(in_wf, 16)
            for s in range(NG + 1):
                if s < NG:
                    pe.wait_ge(hot_ready, s + 1)
                    wide.wait_free(pe, ("u", s))
                    mm(wide.bank(("u", s))[:, :], table[:, :], onehot[:, s * GN:(s + 1) * GN]).then_inc(wide.filled, 1)
                if s >= 1:
                    g = s - 1
                    wide.wait_read(pe, ("u", g))
                    outp.wait_free(pe, ("y", g))
                    for j in range(GT):
                        c = slice((g * GT + j) * P, (g * GT + j + 1) * P)
                        y = outp.bank(("y", g))[:, j * D:(j + 1) * D]
                        mm(y, onehot[:, c], embf[:, :], stop=False)
                        last = mm(y, mems[:, c], w_f[:, :], start=False)
                    last.then_inc(outp.filled, 1)

            for n in range(NSTEP + 1):
                if n < NSTEP:
                    i, g = n // NG, n % NG
                    pe.wait_ge(hn_ready, n + 1)
                    turns(("hT", n), [hn[:, g, j * P:(j + 1) * P] for j in range(GT)], P)
                    turn.wait_read(pe, ("hT", n))
                    pe.wait_ge(w1s_ready, i + 1)
                    for c in range(FC):
                        key = ("h", n, c)
                        wide.wait_free(pe, key)
                        mm(wide.bank(key)[:, :], w1s[:, i, c * P:(c + 1) * P], hT[:, n % 2, :]).then_inc(wide.filled, 1)
                if n >= 1:
                    i = (n - 1) // NG
                    key = ("o", n - 1)
                    wide.wait_read(pe, ("h", n - 1, FC - 1))
                    pe.wait_ge(in_w2[i], 16)
                    outp.wait_free(pe, key)
                    for j in range(GT):
                        for c in range(FC):
                            last = mm(outp.bank(key)[:, j * D:(j + 1) * D], gT[:, (n - 1) % 2, c, j * P:(j + 1) * P], w2[:, i, c, :],
                                      start=(c == 0), stop=(c == FC - 1))
                    last.then_inc(outp.filled, 1)
            pe.wait_ge(in_head, 32)
            for g in range(NG):
                pe.wait_ge(x_ready, NSTEP + g + 1)
                turns(("xT", g), [x[:, g * GT + j, :] for j in range(GT)], P)
                turn.wait_read(pe, ("xT", g))
                outp.wait_free(pe, ("head", g))
                for j in range(GT):
                    last = mm(outp.bank(("head", g))[:, j * W:(j + 1) * W], hT[:, g % 2, j * P:(j + 1) * P], head_w[:, :])
                last.then_inc(outp.filled, 1)

            def z_turned(key, src, width=W):
                i = ZT.index(key)
                turns(key, [src(j) for j in range(GT)], width)
                turn.wait_read(pe, key)
                return zT[:, i % 2, :]

            for s in range(NG + 1):
                if s < NG:
                    pe.wait_ge(z_ready, s + 1)
                    zt = z_turned(("a0", s), lambda j: z0[:, s * GT + j, 0:W])
                    wide.wait_free(pe, ("s0", s))
                    for j in range(GT):
                        q = zt[0:W, j * P:(j + 1) * P]
                        last = mm(wide.bank(("s0", s))[:, j * P:(j + 1) * P], q, q)
                    last.then_inc(wide.filled, 1)
                if s >= 1:
                    g = s - 1
                    wide.wait_read(pe, ("s0", g))
                    outp.wait_free(pe, ("ctx", g))
                    for j in range(GT):
                        last = mm(outp.bank(("ctx", g))[:, j * (W + 1):(j + 1) * (W + 1)], ex[:, g % 2, j * P:(j + 1) * P], z0[:, g * GT + j, :])
                    last.then_inc(outp.filled, 1)

            pe.wait_ge(in_gate, 32)
            for s in range(NG + 1):
                if s < NG:
                    pe.wait_ge(z_ready, NG + s + 1)
                    zt = z_turned(("f0", s), lambda j: z[:, s * GT + j, :])
                    outp.wait_free(pe, ("gate", s))
                    for j in range(GT):
                        last = mm(outp.bank(("gate", s))[:, j * E:(j + 1) * E], zt[:, j * P:(j + 1) * P], gate_w[:, :])
                    last.then_inc(outp.filled, 1)
                if s >= 1:
                    g = s - 1
                    pe.wait_ge(goh_ready, g + 1)
                    outp.wait_free(pe, ("pos", g))
                    cnt = outp.bank(("pos", g))[:, 0:GT * E].rearrange("p (t e) -> p t e", t=GT)
                    last = mm(cnt, tri[:, :], goh[:, g * GT:(g + 1) * GT, :], stop=False)
                    for t in range(g * GT + GT - 1):
                        j = max(0, t - g * GT + 1)
                        last = mm(cnt[:, j:GT, :], ones_b[:, :], bm(goh[:, t, :], GT - j), start=False, stop=(t == g * GT + GT - 2))
                    last.then_inc(outp.filled, 1)

            pe.wait_ge(in_att, 80)
            turns("qkv_w", [qkv_rows[:, 0, :], qkv_rows[0:W, 1, :]], W)
            turns("proj_w", [proj_rows[:, :]], W)
            pe.wait_ge(const_ready, 8)
            outp.wait_free(pe, "relb")
            mm(outp.bank("relb")[:, 0:WS], flip[:, :, :].rearrange("r w q -> r (w q)"), relb_up[:, :]).then_inc(outp.filled, 1)
            for k in range(XG):
                pe.wait_ge(rows_back, 16 * (k + 1))
                turns(("xe", k), [xe[:, 4 * k + j, :] for j in range(4)], W)
            pe.wait_ge(in_exp, 16 * (E + 2))
            turn.wait_read(pe, ("xe", XG - 1))
            for e in range(E + 1):
                if e < E:
                    for c in range(EC):
                        wide.wait_free(pe, ("em", e, c))
                        mm(wide.bank(("em", e, c))[:, 0:CAP], e_w1[:, e, c * P:(c + 1) * P], xeT[:, e * CAP:(e + 1) * CAP]).then_inc(wide.filled, 1)
                if e >= 1:
                    q = e - 1
                    for c in range(EC):
                        wide.wait_read(pe, ("em", q, c))
                    outp.wait_free(pe, ("ey", q))
                    for m in range(3):
                        r = min(P, CAP - m * P)
                        for c in range(EC):
                            last = mm(outp.bank(("ey", q))[0:r, m * W:(m + 1) * W], hm[:, q % 2, c, m * P:m * P + r], e_w2[:, q, c, :], start=(c == 0), stop=(c == EC - 1))
                    last.then_inc(outp.filled, 1)

            pe.wait_ge(wT_ready, 1)

            def qkv(g):
                pe.wait_ge(z_ready, 2 * NG + g + 1)
                zt = z_turned(("a1", g), lambda j: z[:, g * GT + j, :])
                zw = zt[0:W, :].rearrange("p (t w q) -> p w t q", t=GT, w=2)
                for key, at in (("k", W), ("q", 0)):
                    wide.wait_free(pe, (key, g))
                    for w in range(2):
                        last = mm(wide.bank((key, g))[w * W:(w + 1) * W, 0:GT * WS], qkv_w[:, at:at + W], zw[:, w, :, :])
                    last.then_inc(wide.filled, 1)
                outp.wait_free(pe, ("v", g))
                for t in range(2 * GT):
                    for i in range(2):
                        last = mm(outp.bank(("v", g))[i * WS:(i + 1) * WS, t * W:(t + 1) * W], zt[0:W, t * WS:(t + 1) * WS], qkv_w[:, 2 * W:3 * W])
                last.then_inc(outp.filled, 1)

            for s in range(STEPS1):
                if (g := qkv_group(s)) is not None:
                    qkv(g)
                if s < NT:
                    g, j = s // GT, s % GT
                    pe.wait_ge(km_ready, g + 1)
                    wide.wait_read(pe, ("q", g))
                    wide.wait_free(pe, ("s1", s))
                    mm(wide.bank(("s1", s))[:, :], qbd[:, g % 2, j, :], km[:, g % 2, j, :, :].rearrange("p h k -> p (h k)")).then_inc(wide.filled, 1)
                if 0 <= s - LAG_T < NT:
                    t = s - LAG_T
                    pe.wait_ge(pexp_ready, t + 1)
                    turns(("pT", t), [pe_[:, t % 2, q * P:(q + 1) * P] for q in range(HP)], P)
                if 0 <= s - LAG_A < NT:
                    t = s - LAG_A
                    g, j = t // GT, t % GT
                    turn.wait_read(pe, ("pT", t))
                    outp.wait_read(pe, ("v", g))
                    outp.wait_free(pe, ("av", t))
                    for q in range(HP):
                        last = mm(outp.bank(("av", t))[:, q * 2 * VW:(q + 1) * 2 * VW].rearrange("p (w d) -> p w d", w=2), pT[:, t % 2, q, :],
                                  vz[:, g % 2, 2 * j:2 * j + 2, q, :])
                    last.then_inc(outp.filled, 1)
                if (g := proj_group(s)) is not None:
                    pe.wait_ge(o_ready, (g + 1) * GT)
                    zt = z_turned(("oT", g), lambda j: o[:, g * GT + j, :])
                    outp.wait_free(pe, ("proj", g))
                    for j in range(GT):
                        last = mm(outp.bank(("proj", g))[:, j * W:(j + 1) * W], zt[:, j * P:(j + 1) * P], proj_w[:, :])
                    last.then_inc(outp.filled, 1)

            pe.wait_ge(in_x1, 16 * 7)
            pe.wait_ge(in_xbd, 64)
            for s in range(NG + 1):
                if s < NG:
                    pe.wait_ge(z_ready, 3 * NG + s + 1)
                    zt = z_turned(("f1", s), lambda j: z[:, s * GT + j, :])
                    wide.wait_free(pe, ("rh", s))
                    mm(wide.bank(("rh", s))[0:RH, :], r_w1[:, :], zt).then_inc(wide.filled, 1)
                    for q in range(XP):
                        wide.wait_free(pe, ("h1", s, q))
                        mm(wide.bank(("h1", s, q))[:, :], x_w1[:, q * P:(q + 1) * P], zt).then_inc(wide.filled, 1)
                    wide.wait_read(pe, ("rh", s))
                    outp.wait_free(pe, ("rl", s))
                    for j in range(GT):
                        last = mm(outp.bank(("rl", s))[:, j * X:(j + 1) * X], rhT[:, s % 2, j * P:(j + 1) * P], r_w2[:, :])
                    last.then_inc(outp.filled, 1)
                    for q in range(XP):
                        wide.wait_read(pe, ("h1", s, q))
                        wide.wait_free(pe, ("h2", s, q))
                        mm(wide.bank(("h2", s, q))[:, :], x_w2[:, q, :], h1T[:, s % 2, q, :]).then_inc(wide.filled, 1)
                if s >= 1:
                    g = s - 1
                    pe.wait_ge(route_ready, g + 1)
                    turns(("rT", g), [route[:, g * GT + j, :] for j in range(GT)], X)
                    turn.wait_read(pe, ("rT", g))
                    outp.wait_free(pe, ("b3", g))
                    for j in range(GT):
                        last = mm(outp.bank(("b3", g))[:, j * W:(j + 1) * W], routeT[:, g % 2, j * P:(j + 1) * P], x_b3[:, :])
                    last.then_inc(outp.filled, 1)
                    wide.wait_read(pe, ("h2", g, XP - 1))
                    for j in range(GT):
                        wide.wait_free(pe, ("eo", g, j))
                        for q in range(XP):
                            last = mm(wide.bank(("eo", g, j))[:, q * P:(q + 1) * P], h2T[:, g % 2, q, j * P:(j + 1) * P], x_w3[:, q, :])
                        last.then_inc(wide.filled, 1)


_INS = ["x", "L0_tok_emb", "L0_tok_W_upd", "L0_tok_b_upd", "L0_tok_W_f", "L0_tok_b_f", "L0_tok_decay_param",
        "L0_tok_norm_g", "L0_tok_norm_b", "L0_tok_cms_ln_g", "L0_tok_cms_ln_b", "L0_tok_cms_W1", "L0_tok_cms_b1",
        "L0_tok_cms_W2", "L0_tok_cms_b2", "L0_tok_head_W", "L0_tok_head_b", "L0_ffn_gate_w", "L0_ffn_gate_b",
        "L0_ffn_w1", "L0_ffn_b1", "L0_ffn_w2", "L0_ffn_b2", "L1_attn_w_qkv", "L1_attn_w_proj", "L1_attn_b_proj",
        "L1_attn_rel_bias", "L1_ffn_router_w1", "L1_ffn_router_b1", "L1_ffn_router_w2", "L1_ffn_router_b2",
        "L1_ffn_expert_w1", "L1_ffn_expert_b1", "L1_ffn_expert_w2", "L1_ffn_expert_b2", "L1_ffn_expert_w3",
        "L1_ffn_expert_b3"]


def kernel(**inputs):
    import numpy as _np
    import concourse.bacc as _bacc
    from concourse import mybir as _mybir
    from concourse.bass_utils import run_bass_kernel_spmd as _run

    nc = _bacc.Bacc("TRN2", target_bir_lowering=False, num_devices=1)
    arrays, args = {}, {}
    for name in _INS:
        a = _np.ascontiguousarray(inputs[name])
        arrays[f"in_{name}_dram"] = a
        args[name] = nc.dram_tensor(f"in_{name}_dram", a.shape, _mybir.dt.from_np(a.dtype), kind="ExternalInput").ap()
    nb, s = args["x"].shape
    out = nc.dram_tensor("out_dram", (nb, s, args["L0_tok_head_b"].shape[0]), F32, kind="ExternalOutput").ap()
    build(nc, args, out)
    r = _run(nc, [arrays], core_ids=[0])
    return r.results[0]["out_dram"]
```

```python
from contextlib import ExitStack

import numpy as np

import concourse.bass as bass
from concourse import mybir

F32 = mybir.dt.float32
F16 = mybir.dt.float16
I32 = mybir.dt.int32
U32 = mybir.dt.uint32
ALU = mybir.AluOpType
ACT = mybir.ActivationFunctionType
AX = mybir.AxisListType.X

P = 128
EPS = 1e-5
CLIP = 1e4
WS16 = 256.0
TS16 = 64.0


class Ring:

    def __init__(self, banks, filled, freed):
        self.banks, self.filled, self.freed = banks, filled, freed
        self.at, self.readers = {}, []

    def add(self, key, reader):
        self.at[key] = len(self.readers)
        self.readers.append(reader)

    def bank(self, key):
        return self.banks[self.at[key] % len(self.banks)]

    def number(self, key):
        return self.at[key] + 1

    def wait_free(self, pe, key):
        before = self.at[key] - len(self.banks)
        if before >= 0:
            reader = self.readers[before]
            pe.wait_ge(self.freed[reader], self.readers[:before + 1].count(reader))

    def wait_read(self, eng, key):
        reader = self.readers[self.at[key]]
        eng.wait_ge(self.freed[reader], self.readers[:self.at[key] + 1].count(reader))


def build(nc, a, out):
    NB, S = a["x"].shape
    V, D = a["L0_tok_emb"].shape
    L, _, FF = a["L0_tok_cms_W1"].shape
    FC = FF // P
    _, E, W = None, *a["L0_ffn_gate_w"].shape[::-1]
    EF = a["L0_ffn_w1"].shape[2]
    EC = EF // P
    T = NB * S
    NT = T // P
    GT = 4
    NG = NT // GT
    GN = GT * P
    CAP = -(-5 * T // (4 * E))
    SLOTS = E * CAP
    ST = SLOTS // P
    EP = E // 2
    WS = 64
    H1 = 8
    HD = W // H1
    HP = H1 // 2
    X, RH = a["L1_ffn_router_w1"].shape[0] and a["L1_ffn_expert_w1"].shape[0], a["L1_ffn_router_w1"].shape[1]
    XP = X // 2
    assert S == P and D == P and W == 64 and SLOTS % P == 0 and V == 64 and P == 2 * WS

    STEP = [(i, g) for i in range(L) for g in range(NG)]
    NSTEP = len(STEP)
    AT = {lg: n for n, lg in enumerate(STEP)}

    EXTRA = {("w1", 1): 0.9, ("w1", 2): 1.9, ("w1", 3): 2.9,
             ("prep", 0): 3.9, ("prep", 1): 4.9, ("prep", 2): 5.9, ("prep", 3): 6.9, ("prep", 4): 7.9, ("prep", 5): 8.9,
             ("xturn", 0): 13.1, ("head", 0): 13.2, ("zturn", 0): 14.1, ("score", 0): 14.2, ("context", 0): 15.0, ("fturn", 0): 15.9, ("gate", 0): 16.0, ("place", 0): 16.8, ("scatter", 0): 16.9,
             ("xturn", 1): 14.1, ("head", 1): 14.2, ("zturn", 1): 15.1, ("score", 1): 15.2, ("context", 1): 16.0, ("fturn", 1): 16.9, ("gate", 1): 17.0, ("place", 1): 17.8, ("scatter", 1): 17.9,
             ("xturn", 2): 15.1, ("head", 2): 15.2, ("zturn", 2): 16.1, ("score", 2): 16.2, ("context", 2): 17.0, ("fturn", 2): 17.9, ("gate", 2): 18.0, ("place", 2): 18.8, ("scatter", 2): 18.9,
             ("xturn", 3): 16.1, ("head", 3): 16.2, ("zturn", 3): 17.1, ("score", 3): 17.2, ("context", 3): 18.0, ("fturn", 3): 18.9, ("gate", 3): 19.0, ("place", 3): 19.8, ("scatter", 3): 19.9}
    time = {("front", 0): -5.0, ("front", 1): -4.9, ("w1", 0): -4.8, ("front", 2): -4.7, ("front", 3): -3.0, ("front", 4): -1.0,
            ("front", 5): 0.0, ("turn", 0): -4.0, ("turn", 1): -0.5, ("up", 0): -2.0}
    for n in range(NSTEP):
        if n >= 1:
            time["up", n] = n - 0.9
        time["down", n] = n + 0.5
        if n >= 2:
            i, g = STEP[n]
            time["turn", n] = n - 2 + (0.3 if i == 0 or AT[i - 1, g] < n - 2 else 0.7)
    time.update(EXTRA)
    PLAN = sorted(time, key=time.get)

    TILE_LAGS = {"scores": 0.0, "weights": 1.2, "turned": 3.3, "applied": 4.4}
    GROUP_LAGS = {"returned": -6.9, "turn_a1": -4.5, "qkv": -0.9, "project": 9.5, "rows": 10.6, "router": 10.7, "logits": 11.8, "choice": 12.1, "shares": 12.8}
    FIRST, FIRST_STEP, SECOND, SECOND_STEP, THIRD, THIRD_STEP = 10.71, 0.4, 12.0, 0.4, 13.6, 0.4
    RETURNED_1, TURNED_1 = -5.0, -3.5
    when = {("gather", g): -20.0 + g for g in range(NG)}
    for t in range(NT):
        for what, lag in TILE_LAGS.items():
            when[what, t] = t + lag
    for g in range(NG):
        for what, lag in GROUP_LAGS.items():
            when[what, g] = g * GT + lag
        for q in range(XP):
            when["first", (g, q)] = g * GT + FIRST + q * FIRST_STEP
            when["second", (g, q)] = g * GT + SECOND + q * SECOND_STEP
        for j in range(GT):
            when["third", (g, j)] = g * GT + THIRD + j * THIRD_STEP
    when["returned", 1], when["turn_a1", 1] = RETURNED_1, TURNED_1
    PLAN2 = sorted(when, key=when.get)

    RW = 2 * W
    xbuf = nc.dram_tensor("expert_rows", (SLOTS + T, RW), F16, kind="Internal").ap()
    ybuf = nc.dram_tensor("expert_outputs", (SLOTS, W), F32, kind="Internal").ap()

    with ExitStack() as ctx:
        def sb(name, shape, dt=F32):
            return ctx.enter_context(nc.sbuf_tensor(name, shape, dt))

        def sem(name):
            return ctx.enter_context(nc.semaphore(name))

        ident = sb("ident", [P, P])
        ident16 = sb("ident16", [P, P], F16)
        tri = sb("tri", [P, P], F16)
        ones16 = sb("ones16", [P, P], F16)
        iota_v = sb("iota_v", [P, 1], I32)
        iota_vf = sb("iota_vf", [P, 1])
        not_zero = sb("not_zero", [V, 1])
        rank8 = sb("rank8", [P, E])
        rank6 = sb("rank6", [P, X])
        rank_i = sb("rank_i", [P, E], I32)
        trash_i = sb("trash_i", [P, NT], I32)
        trash = sb("trash", [P, NT])
        headmask = sb("headmask", [P, H1])
        flip = sb("flip", [WS, 2, WS])
        relb_up = sb("relb_up", [WS, WS])
        relb = sb("relb", [P, WS])
        emb = sb("emb", [V, D])
        embf = sb("embf", [V, D])
        embT = sb("embT", [D, V])
        w_upd = sb("w_upd", [D, D])
        w_f = sb("w_f", [D, D])
        b_upd = sb("b_upd", [V, D])
        b_f = sb("b_f", [V, D])
        table0 = sb("table0", [V, D])
        table1 = sb("table1", [V, D])
        table = sb("table", [2 * V, D], F16)
        etable = sb("etable", [2 * V, D], F16)
        decay_in = sb("decay_in", [P, 1])
        decay = sb("decay", [P, 4])
        norm_g = sb("norm_g", [P, D])
        norm_b = sb("norm_b", [P, D])
        R_B1 = 2 * L
        R_X2 = R_B1 + L * FC
        R_X1 = R_X2 + XP
        R_E1 = R_X1 + XP
        NR = R_E1 + E * EC
        rows = sb("rows", [NR, P])
        cols = sb("cols", [P, NR])
        e_b1s = sb("e_b1s", [P, E * EC])
        r_b1 = sb("r_b1", [RH, 1])
        w1 = sb("w1", [D, L, FF])
        w1p = sb("w1p", [D, 2, L, FF], F16)
        w2 = sb("w2", [P, L, FC, D])
        b2 = sb("b2", [P, L, D])
        head_w = sb("head_w", [D, W])
        head_b = sb("head_b", [P, W])
        gate_b = sb("gate_b", [P, E])
        r_b2 = sb("r_b2", [P, X])
        e_w2 = sb("e_w2", [P, E, EC, W])
        e_b2 = sb("e_b2", [P, E, W])
        qkv_rows = sb("qkv_rows", [P, 2, W])
        proj_rows = sb("proj_rows", [W, W])
        x_w2 = sb("x_w2", [P, XP, P])
        x_w3 = sb("x_w3", [P, XP, P])
        C_E = E
        C_Q = C_E + E * EF
        C_P = C_Q + 3 * W
        C_R = C_P + W
        C_X = C_R + RH
        C_N = C_X + X * W
        wst = sb("wst", [P, C_N])
        wp = sb("wp", [P, 2, C_N], F16)
        r_w2 = sb("r_w2", [2 * RH, X])
        r_w2p = sb("r_w2p", [2 * RH, 2, X], F16)
        BR = 33
        BN = W + X * W
        bias_rows = sb("bias_rows", [BR, BN])
        bias_hi = sb("bias_hi", [BR, BN], F16)
        bias_p = sb("bias_p", [BR, BN], F16)

        onehot = sb("onehot", [2 * V, T], F16)
        scan_io = sb("scan_io", [P, 2, T])
        keep_mem = scan_io[:, 0, :]
        mems = scan_io[:, 1, :]
        ln_t = sb("ln_t", [P, GT, D])
        stream = sb("stream", [P, 2, NT, D])
        x = stream[:, 0, :, :]
        xb = stream[:, 1, :, :]
        hn = sb("hn", [P, NG, GN])
        hT = sb("hT", [P, 2, GN])
        hp = sb("hp", [P, 2, 2, GN], F16)
        gT = sb("gT", [P, 2, FC, GN])
        assert T <= FC * GN
        tokens = gT[0:1, 0, :, :].rearrange("p c n -> p (c n)")[:, 0:T].bitcast(I32)
        tokens16 = gT[0:1, 1, :, :].rearrange("p c n -> p (c n)")[:, 0:T // 2].bitcast(F16)
        st = sb("st", [P, 2, GT, 6])
        mv = sb("mv", [P, 2, GT, 2])
        ve = sb("ve", [P, 2, GT])
        rstd = sb("rstd", [P, 2, GT])
        one = sb("one", [P, 1])
        neg_half = sb("neg_half", [P, GT])
        h = sb("h", [P, NT, W])
        ZB = 4
        z0 = sb("z0", [P, NT, W + 1])
        z0T = sb("z0T", [W, 2, GN])
        zf = sb("zf", [P, 2, GT, W])
        zs = sb("zs", [P, NT, RW], F16)
        zT = sb("zT", [P, ZB, GN], F16)
        ex = sb("ex", [P, 2, GN])
        rs = sb("rs", [P, 2, GT])
        glog = sb("glog", [P, NT, E])
        gm = sb("gm", [P, NT])
        gd = sb("gd", [P, NT, E])
        gv = sb("gv", [P, NT, E])
        gbest = sb("gbest", [P, NT])
        goh = sb("goh", [P, NT, E], F16)
        gex = sb("gex", [P, NT, E])
        gsum = sb("gsum", [P, NT])
        prob = sb("prob", [P, NT])
        pc = sb("pc", [P, NT, E])
        pos1 = sb("pos1", [P, NT])
        kept = sb("kept", [P, NT])
        base = sb("base", [P, NT])
        slot = sb("slot", [P, NT])
        slot2 = sb("slot2", [P, NT])
        idx_s = sb("idx_s", [P, NT], I32)
        idx_g = sb("idx_g", [P, NT], I32)
        pk = sb("pk", [P, NT])
        w1_flat = w1[:, :, :].rearrange("p l f -> p (l f)")
        stream_flat = stream[:, :, :, :].rearrange("p a t d -> p (a t d)")
        w1p_flat = w1p[:, :, :, :].rearrange("p a l f -> p (a l f)").bitcast(F32)
        w2_flat = w2[:, :, :, :].rearrange("p l c d -> p (l c d)")
        hn_flat = hn[:, :, :].rearrange("p g n -> p (g n)")
        xe = w1_flat[:, 0:ST * RW // 2].bitcast(F16).rearrange("p (t w) -> p t w", t=ST)
        xeT = stream[:, 0, :, :].rearrange("p t d -> p (t d)")[:, 0:ST * P // 2].bitcast(F16)
        empty = stream[:, 0, :, :].rearrange("p t d -> p (t d)")[:, 0:ST * RW // 2]
        hm = sb("hm", [P, 2, EC, CAP])
        ye = w1p_flat[:, 0:ST * W].rearrange("p (t w) -> p t w", t=ST)
        yg = sb("yg", [P, NT, W])
        yp = sb("yp", [P, GT, W])
        ya = sb("ya", [P, GT, W])
        yc = sb("yc", [P, GT, W])
        yn = sb("yn", [P, GT, W])
        yfin = sb("yfin", [P, GT, W], U32)
        km = gT[:, :, :, :].rearrange("p b t (h k) -> p b t h k", h=H1)
        qbd = sb("qbd", [P, 2, GT, P])
        VW = 2 * (HD + 1)
        vf = onehot[:, :].bitcast(F32).rearrange("p (b n) -> p b n", b=2)
        vz = sb("vz", [P, 2, 2, GT * 2, HP, VW], F16)
        sm = hn_flat[:, 0:2 * H1 * WS].rearrange("p (b h k) -> p b h k", b=2, h=H1)
        smx = sb("smx", [P, 2, H1])
        sd = hn_flat[:, 2 * H1 * WS:4 * H1 * WS].rearrange("p (b h k) -> p b h k", b=2, h=H1)
        pf = w1_flat[:, 0:2 * H1 * WS].rearrange("p (b n) -> p b n", b=2)
        pp = w1_flat[:, 2 * H1 * WS:4 * H1 * WS].bitcast(F16).rearrange("p (b i n) -> p b i n", b=2, i=2)
        pT = w1p_flat[:, 0:HP * 2 * P].bitcast(F16).rearrange("p (b i h q) -> p b i h q", b=2, i=2, h=HP)
        rden = sb("rden", [P, 2, H1])
        o = w1p_flat[:, HP * 2 * P:HP * 2 * P + 2 * GT * W].rearrange("p (b t w) -> p b t w", b=2, t=GT)
        rhf = w2_flat[0:RH, NT * W:NT * W + 2 * GN].rearrange("p (b n) -> p b n", b=2)
        rhp = stream_flat[0:2 * RH, 2 * XP * GN:2 * XP * GN + GN].bitcast(F16).rearrange("p (b n) -> p b n", b=2)
        tl = sb("tl", [P, GT, X])
        tm = sb("tm", [P, GT])
        td = sb("td", [P, GT, X])
        te = sb("te", [P, GT, X])
        tsum = sb("tsum", [P, GT])
        trs = sb("trs", [P, GT])
        tp = sb("tp", [P, GT, X])
        shares = sb("shares", [P, 2, X, W])
        chosen = sb("chosen", [P, 2, GT, W])
        m2 = sb("m2", [P, GT])
        teq = sb("teq", [P, GT, X])
        tv = sb("tv", [P, GT, X])
        tb = sb("tb", [P, GT])
        o1 = sb("o1", [P, GT, X])
        o2 = sb("o2", [P, GT, X])
        tdl = sb("tdl", [P, GT])
        tex = sb("tex", [P, GT])
        tw0 = sb("tw0", [P, GT])
        tw1 = sb("tw1", [P, GT])
        tw2 = sb("tw2", [P, GT])
        route = sb("route", [P, NT, X])
        h1T = scan_io[:, :, :].rearrange("p a n -> p (a n)")[:, 0:2 * XP * GN].rearrange("p (b q n) -> p b q n", b=2, q=XP)
        h2T = stream_flat[:, 0:2 * XP * GN].rearrange("p (b q n) -> p b q n", b=2, q=XP)
        res = w2_flat[:, 0:NT * W].rearrange("p (t w) -> p t w", t=NT)

        banks = [ctx.enter_context(nc.psum_tensor(f"bank{i}", [P, 512], F32)) for i in range(8)]
        wide = Ring(banks[0:4], sem("wide_filled"), {"act": sem("wide_freed_act"), "dve": sem("wide_freed_dve")})
        turn = Ring(banks[4:6], sem("turn_filled"), {"act": sem("turn_freed_act")})
        outp = Ring(banks[6:8], sem("outp_filled"), {"act": sem("outp_freed_act"), "dve": sem("outp_freed_dve")})

        turn.add("emb", "act")
        turn.add("rows", "act")
        outp.add("table", "dve")
        for what, n in PLAN:
            if what == "front":
                if n < NG:
                    wide.add(("tok", n), "act")
                if 1 <= n <= NG:
                    wide.add(("u", n - 1), "dve")
                if n >= 2:
                    outp.add(("y", n - 2), "dve")
            if what == "turn":
                turn.add(("hT", n), "act")
            if what == "up":
                for c in range(FC):
                    wide.add(("h", n, c), "act")
            if what == "down":
                outp.add(("o", n), "dve")
            if what == "prep" and n == 4:
                turn.add("qkv_w", "act")
                turn.add("proj_w", "act")
                outp.add("relb", "act")
            if what == "xturn":
                turn.add(("xT", n), "act")
            if what == "zturn":
                turn.add(("a0", n), "act")
            if what == "fturn":
                turn.add(("f0", n), "act")
            if what == "head":
                outp.add(("head", n), "dve")
            if what == "score":
                wide.add(("s0", n), "act")
            if what == "context":
                outp.add(("ctx", n), "dve")
            if what == "gate":
                outp.add(("gate", n), "dve")
            if what == "place":
                outp.add(("pos", n), "dve")
        XG = ST // 4

        def slots_end(e):
            return min(XG, -(-(e + 1) * CAP // GN))

        for k in range(XG):
            turn.add(("xe", k), "act")
        for e in range(E + 1):
            if e < E:
                wide.add(("em", e, 0), "act")
                wide.add(("em", e, 1), "dve")
            if e >= 1:
                outp.add(("ey", e - 1), "dve")

        for what, n in PLAN2:
            if what == "turn_a1":
                turn.add(("a1", n), "act")
            if what == "qkv":
                wide.add(("k", n), "act")
                wide.add(("q", n), "act")
                outp.add(("v", n), "act")
            if what == "scores":
                wide.add(("s1", n), "dve")
            if what == "turned":
                turn.add(("pT", n), "act")
            if what == "applied":
                outp.add(("av", n), "dve")
            if what == "project":
                turn.add(("oT", n), "act")
                outp.add(("proj", n), "dve")
            if what == "rows":
                turn.add(("f1", n), "act")
            if what == "router":
                wide.add(("rh", n), "act")
            if what == "first":
                wide.add(("h1", *n), "act")
            if what == "logits":
                outp.add(("rl", n), "dve")
            if what == "second":
                wide.add(("h2", *n), "act" if n[1] == 0 else "dve")
            if what == "third":
                wide.add(("eo", *n), "dve")

        LNS, NEXT, HT, ZT = [], [], [], []
        for what, n in PLAN:
            if what == "front" and n >= 2:
                LNS += [("y", n - 2), ("c", AT[0, n - 2])]
                NEXT.append(AT[0, n - 2])
            if what == "turn":
                HT.append(("hT", n))
            if what == "down" and STEP[n][0] + 1 < L:
                NEXT.append(AT[STEP[n][0] + 1, STEP[n][1]])
                LNS.append(("c", NEXT[-1]))
            if what == "xturn":
                HT.append(("xT", n))
            if what == "head":
                LNS.append(("a0", n))
            if what == "context":
                LNS.append(("f0", n))
            if what == "fturn":
                ZT.append(("f0", n))
        for what, n in PLAN2:
            if what == "returned":
                LNS.append(("a1", n))
            if what == "turn_a1":
                ZT.append(("a1", n))
            if what == "project":
                ZT.append(("oT", n))
                LNS.append(("f1", n))
            if what == "rows":
                ZT.append(("f1", n))
        ZT_LAST = {"f0": (outp, lambda g: ("gate", g)), "a1": (outp, lambda g: ("v", g)),
                   "oT": (outp, lambda g: ("proj", g)), "f1": (wide, lambda g: ("h1", g, XP - 1))}
        ZS = [k for k in LNS if k[0] == "f0"]
        for k in LNS:
            if k[0] == "a1":
                ZS.append(k)
            if k[0] == "f1":
                ZS += [("oT", k[1]), k]

        in_emb, in_tok, in_rows, in_wf, in_norm = map(sem, ["in_emb", "in_tok", "in_rows", "in_wf", "in_norm"])
        in_w1 = [sem(f"in_w1_{i}") for i in range(L)]
        in_w2 = [sem(f"in_w2_{i}") for i in range(L)]
        in_b2, in_head, in_gate, in_exp, in_att, in_x1, in_xbd = map(
            sem, ["in_b2", "in_head", "in_gate", "in_exp", "in_att", "in_x1", "in_xbd"])
        zero_rows, scattered, ye_out, stored = map(sem, ["zero_rows", "scattered", "ye_out", "stored"])
        rows_back = [sem(f"rows_back_{k}") for k in range(XG)]
        gathered = [sem(f"gathered_{g}") for g in range(NG)]
        pool_step, ident_ready, const_ready, zeros_ready, xb_ready, rstd_ready, sd_ready, plo_ready, vlo_ready, parts_ready = map(
            sem, ["pool_step", "ident_ready", "const_ready", "zeros_ready", "xb_ready", "rstd_ready", "sd_ready",
                  "plo_ready", "vlo_ready", "parts_ready"])
        dve_step, decay_ready, stats_ready, table_ready, etable_ready, hot_ready, w1_ready, x_ready, hn_ready, hp_ready, prep_ready = map(
            sem, ["dve_step", "decay_ready", "stats_ready", "table_ready", "etable_ready", "hot_ready", "w1_ready", "x_ready",
                  "hn_ready", "hp_ready", "prep_ready"])
        z0_ready, zs_ready, goh_ready, gd_ready, idx_ready, ye_ready, km_ready, smx_ready, o_ready = map(
            sem, ["z0_ready", "zs_ready", "goh_ready", "gd_ready", "idx_ready", "ye_ready", "km_ready",
                  "smx_ready", "o_ready"])
        td_ready, tdl_ready, route_ready, rlo_ready, res_ready = map(
            sem, ["td_ready", "tdl_ready", "route_ready", "rlo_ready", "res_ready"])
        act_step, keep_ready, hi_ready, tok16_ready, cols_ready, decay_exp, gex_ready, turned_w, vf_ready, pexp_ready, rh_ready, te_ready, tex_ready = map(
            sem, ["act_step", "keep_ready", "hi_ready", "tok16_ready", "cols_ready", "decay_exp", "gex_ready", "turned_w", "vf_ready",
                  "pexp_ready", "rh_ready", "te_ready", "tex_ready"])

        def bc(ap, n):
            return ap.unsqueeze(2).broadcast_to([ap.shape[0], ap.shape[1], n])

        def bm(ap, n):
            return ap.unsqueeze(1).broadcast_to([ap.shape[0], n, ap.shape[1]])

        def over_partitions(ap, n=P):
            return bass.AP(ap.tensor, ap.offset, [[0, n]] + [list(d) for d in ap.ap])

        def row(ap):
            return ap.unsqueeze(0)

        def group(g):
            return slice(g * GT, (g + 1) * GT)

        block = ctx.enter_context(nc.Block())

        @block.sync
        def _(sp):
            sp.dma_start(tokens, row(a["x"].rearrange("b s -> (b s)"))).then_inc(in_tok, 16)
            sp.dma_start(emb[:, :], a["L0_tok_emb"]).then_inc(in_emb, 16)
            sp.dma_start(w_upd[:, :], a["L0_tok_W_upd"]).then_inc(in_emb, 16)
            sp.dma_start(b_upd[:, :], over_partitions(a["L0_tok_b_upd"], V)).then_inc(in_emb, 16)
            sp.dma_start(b_f[:, :], over_partitions(a["L0_tok_b_f"], V)).then_inc(in_emb, 16)
            sp.dma_start(w_f[:, :], a["L0_tok_W_f"]).then_inc(in_wf, 16)
            sp.dma_start(w1[:, 0, :], a["L0_tok_cms_W1"][0]).then_inc(in_w1[0], 16)
            sp.dma_start(w2[:, 0, :, :], a["L0_tok_cms_W2"][0].rearrange("(c p) d -> p c d", p=P)).then_inc(in_w2[0], 16)
            sp.dma_start(b2[:, :, :], over_partitions(a["L0_tok_cms_b2"])).then_inc(in_b2, 16)
            for i in range(1, L):
                sp.dma_start(w1[:, i, :], a["L0_tok_cms_W1"][i]).then_inc(in_w1[i], 16)
                sp.dma_start(w2[:, i, :, :], a["L0_tok_cms_W2"][i].rearrange("(c p) d -> p c d", p=P)).then_inc(in_w2[i], 16)
            sp.dma_start(head_w[:, :], a["L0_tok_head_W"]).then_inc(in_head, 16)
            sp.dma_start(head_b[:, :], over_partitions(a["L0_tok_head_b"])).then_inc(in_head, 16)
            sp.dma_start(gate_b[:, :], over_partitions(a["L0_ffn_gate_b"])).then_inc(in_gate, 16)
            sp.dma_start(r_b2[:, :], over_partitions(a["L1_ffn_router_b2"])).then_inc(in_gate, 16)
            sp.dma_start(qkv_rows[:, 0, :], a["L1_attn_w_qkv"][0:P, :]).then_inc(in_att, 16)
            sp.dma_start(qkv_rows[0:W, 1, :], a["L1_attn_w_qkv"][P:3 * W, :]).then_inc(in_att, 16)
            sp.dma_start(proj_rows[:, :], a["L1_attn_w_proj"]).then_inc(in_att, 16)
            rb = a["L1_attn_rel_bias"]
            sp.dma_start(relb_up[:, :], bass.AP(rb.tensor, rb.offset, [[1, WS], [1, WS]])).then_inc(in_att, 16)
            for i in range(2):
                half = slice(i * W, (i + 1) * W)
                sp.dma_start(wst[half, 0:C_E], a["L0_ffn_gate_w"]).then_inc(in_exp, 16)
                sp.dma_start(wst[half, C_E:C_Q].rearrange("d (e f) -> d e f", e=E), a["L0_ffn_w1"].rearrange("e d f -> d e f")).then_inc(in_exp, 16)
                sp.dma_start(wst[half, C_R:C_X], a["L1_ffn_router_w1"]).then_inc(in_x1, 16)
                sp.dma_start(wst[half, C_X:C_N].rearrange("d (e f) -> d e f", e=X), a["L1_ffn_expert_w1"].rearrange("e d f -> d e f")).then_inc(in_x1, 16)
                sp.dma_start(r_w2[i * RH:(i + 1) * RH, :], a["L1_ffn_router_w2"]).then_inc(in_x1, 16)
                sp.dma_start(bias_rows[32 * i:32 * i + 1, 0:W], row(a["L1_attn_b_proj"])).then_inc(in_x1, 16)
                sp.dma_start(bias_rows[32 * i:32 * i + 1, W:BN], row(a["L1_ffn_expert_b3"].rearrange("e w -> (e w)"))).then_inc(in_x1, 16)
            for e in range(E):
                sp.dma_start(e_w2[:, e, :, :], a["L0_ffn_w2"][e].rearrange("(c p) w -> p c w", p=P)).then_inc(in_exp, 16)
            sp.dma_start(e_b2[:, :, :], over_partitions(a["L0_ffn_b2"])).then_inc(in_exp, 16)
            sp.wait_ge(parts_ready, 3)
            for i in range(2):
                part = slice(i * W, (i + 1) * W)
                sp.dma_start(x_w2[part, :, part], a["L1_ffn_expert_w2"].rearrange("(q i) f g -> i f q g", i=2)[i]).then_inc(in_xbd, 16)
                sp.dma_start(x_w3[part, :, part], a["L1_ffn_expert_w3"].rearrange("(q i) f g -> i f q g", i=2)[i]).then_inc(in_xbd, 16)
            sp.wait_ge(scattered, 16 * NT)
            xr = xbuf[0:SLOTS, :].rearrange("(t p) w -> p t w", p=P)
            for k in range(XG):
                sp.dma_start(xe[:, 4 * k:4 * k + 4, :], xr[:, 4 * k:4 * k + 4, :]).then_inc(rows_back[k], 16)
            yr = ybuf.rearrange("(t p) w -> p t w", p=P)
            for k in range(EP):
                pair_tiles = slice(k * ST // EP, (k + 1) * ST // EP)
                sp.wait_ge(ye_ready, 2 * k + 2)
                sp.dma_start(yr[:, pair_tiles, :], ye[:, pair_tiles, :]).then_inc(ye_out, 16)
            for g in range(NG):
                sp.wait_ge(res_ready, g + 1)
                sp.dma_start(out.rearrange("b s w -> s b w")[:, group(g), :], res[:, group(g), :]).then_inc(stored, 16)
            sp.wait_ge(stored, 16 * NG)

        @block.gpsimd
        def _(pool):
            steps = [0]

            def link(ins):
                steps[0] += 1
                ins.then_inc(pool_step, 1)
                pool.wait_ge(pool_step, steps[0])

            def signal(ins, s, value):
                ins.then_inc(s, 1)
                pool.wait_ge(s, value)

            link(nc.gpsimd.memset(ident[:, :], 0.0))
            signal(nc.gpsimd.affine_select(out=ident[:, :], in_=ident[:, :], compare_op=ALU.not_equal, fill=1.0, base=0,
                                           pattern=[[-1, P]], channel_multiplier=1), ident_ready, 1)
            for i in range(2):
                link(nc.gpsimd.iota(iota_v[i * V:(i + 1) * V, :], pattern=[[0, 1]], base=0, channel_multiplier=1))
            signal(nc.gpsimd.memset(ones16[:, :], 1.0), const_ready, 1)
            signal(nc.gpsimd.memset(neg_half[:, :], -0.5), const_ready, 2)
            signal(nc.gpsimd.memset(one[:, :], 1.0), const_ready, 3)
            signal(nc.gpsimd.memset(empty, 0.0), zeros_ready, 1)
            nc.gpsimd.dma_start(xbuf[0:SLOTS, :].rearrange("(p k) w -> p (k w)", p=P), empty.bitcast(F16)).then_inc(zero_rows, 16)

            def more_constants():
                link(nc.gpsimd.tensor_copy(ident16[:, :], ident[:, :]))
                link(nc.gpsimd.memset(tri[:, :], 1.0))
                link(nc.gpsimd.affine_select(out=tri[:, :], in_=tri[:, :], compare_op=ALU.is_ge, fill=0.0, base=0,
                                             pattern=[[1, P]], channel_multiplier=-1))
                link(nc.gpsimd.iota(rank_i[:, :], pattern=[[-1, E]], base=E, channel_multiplier=0))
                link(nc.gpsimd.iota(trash_i[:, :], pattern=[[P, NT]], base=SLOTS, channel_multiplier=1))
                link(nc.gpsimd.memset(flip[:, :, :], 0.0))
                link(nc.gpsimd.affine_select(out=flip[:, :, :], in_=flip[:, :, :], compare_op=ALU.not_equal, fill=1.0, base=1 - WS,
                                             pattern=[[0, 2], [1, WS]], channel_multiplier=1))
                link(nc.gpsimd.memset(headmask[:, :], 1.0 / WS16))
                for w in range(2):
                    part = headmask[w * W:(w + 1) * W, :]
                    link(nc.gpsimd.affine_select(out=part, in_=part, compare_op=ALU.is_ge, fill=0.0, base=0,
                                                 pattern=[[-HD, H1]], channel_multiplier=1))
                    link(nc.gpsimd.affine_select(out=part, in_=part, compare_op=ALU.is_ge, fill=0.0, base=HD - 1,
                                                 pattern=[[HD, H1]], channel_multiplier=-1))
                link(nc.gpsimd.memset(z0[:, :, W], 1.0))
                signal(nc.gpsimd.memset(bias_p[:, :], 0.0), parts_ready, 1)
                link(nc.gpsimd.memset(x_w2[:, :, :], 0.0))
                signal(nc.gpsimd.memset(x_w3[:, :, :], 0.0), parts_ready, 2)
                signal(nc.gpsimd.memset(qbd[:, :, :, :], 0.0), parts_ready, 3)
                link(nc.gpsimd.memset(vz[:, :, :, :, :, :], 0.0))
                link(nc.gpsimd.memset(vz[0:WS, :, 0, :, :, HD], 1.0))
                signal(nc.gpsimd.memset(vz[WS:P, :, 0, :, :, VW - 1], 1.0), parts_ready, 4)

            def ln_root(key):
                k = LNS.index(key)
                pool.wait_ge(stats_ready, k + 1)
                eps = EPS * TS16 * TS16 if key[0] == "y" else EPS
                link(nc.gpsimd.tensor_scalar_add(ve[:, k % 2, :], mv[:, k % 2, :, 1], eps))
                signal(nc.gpsimd.tensor_tensor(rstd[:, k % 2, :], ve[:, k % 2, :], neg_half[:, :], ALU.pow), rstd_ready, k + 1)

            def add_b2(n):
                i, g = STEP[n]
                k = NEXT.index(n)
                pool.wait_ge(x_ready, k + 1)
                signal(nc.gpsimd.tensor_tensor(xb[:, group(g), :], x[:, group(g), :], bm(b2[:, i, :], GT), ALU.add), xb_ready, k + 1)

            more_constants()
            pool.wait_ge(in_b2, 16)
            pool.wait_ge(zero_rows, 16)
            for what, n in PLAN:
                if what == "front" and n >= 2:
                    ln_root(("y", n - 2))
                    ln_root(("c", AT[0, n - 2]))
                    add_b2(AT[0, n - 2])
                if what == "down" and STEP[n][0] + 1 < L:
                    m = AT[STEP[n][0] + 1, STEP[n][1]]
                    ln_root(("c", m))
                    add_b2(m)
                if what == "head":
                    ln_root(("a0", n))
                if what == "context":
                    ln_root(("f0", n))
                if what == "scatter":
                    pool.wait_ge(idx_ready, n + 1)
                    for t in range(n * GT, (n + 1) * GT):
                        nc.gpsimd.indirect_dma_start(out=xbuf[:, :], out_offset=bass.IndirectOffsetOnAxis(ap=idx_s[:, t:t + 1], axis=0),
                                                     in_=zs[:, t, :], in_offset=None).then_inc(scattered, 16)

            def gather(g):
                pool.wait_ge(ye_out, 16 * EP)
                for t in range(g * GT, (g + 1) * GT):
                    nc.gpsimd.indirect_dma_start(out=yg[:, t, :], out_offset=None, in_=ybuf[:, :],
                                                 in_offset=bass.IndirectOffsetOnAxis(ap=idx_g[:, t:t + 1], axis=0)).then_inc(gathered[g], 16)

            def low_values(g):
                for k in range(NG):
                    if PLAN2.index(("gather", k)) < PLAN2.index(("qkv", g)):
                        pool.wait_ge(gathered[k], 16 * GT)
                pool.wait_ge(vf_ready, g + 1)
                v5 = vf[:, g % 2, :].rearrange("p (t h i d) -> p t h i d", t=2 * GT, h=HP, i=2)
                for i in range(2):
                    part = slice(i * WS, (i + 1) * WS)
                    at = slice(i * (HD + 1), i * (HD + 1) + HD)
                    signal(nc.gpsimd.tensor_tensor(vz[part, g % 2, 1, :, :, at], v5[part, :, :, i, :], vz[part, g % 2, 0, :, :, at], ALU.subtract),
                           vlo_ready, 2 * g + i + 1)

            def sub_max(t):
                pool.wait_ge(smx_ready, t + 1)
                if t >= 2:
                    pool.wait_ge(pexp_ready, t - 1)
                signal(nc.gpsimd.tensor_tensor(sd[:, t % 2, :, :], sm[:, t % 2, :, :], bc(smx[:, t % 2, :], WS), ALU.subtract), sd_ready, t + 1)

            def low_weights(t):
                pool.wait_ge(pexp_ready, t + 1)
                if t >= 2:
                    pool.wait_ge(turn.filled, turn.number(("pT", t - 2)))
                signal(nc.gpsimd.tensor_tensor(pp[:, t % 2, 1, :], pf[:, t % 2, :], pp[:, t % 2, 0, :], ALU.subtract), plo_ready, t + 1)

            for what, n in PLAN2:
                if what == "gather":
                    gather(n)
                if what == "returned":
                    ln_root(("a1", n))
                if what == "qkv":
                    low_values(n)
                if what == "scores":
                    sub_max(n)
                if what == "weights":
                    low_weights(n)
                if what == "project":
                    ln_root(("f1", n))

        @block.scalar
        def _(act):
            steps = [0]

            def link(ins):
                steps[0] += 1
                ins.then_inc(act_step, 1)
                act.wait_ge(act_step, steps[0])

            def copy(dst, src, scale=1.0):
                return nc.scalar.activation(dst, src, ACT.Copy, scale=scale)

            def load(dst, src, loaded):
                nc.scalar.dma_start(dst, src).then_inc(loaded, 16)

            load(decay_in[:, :], over_partitions(a["L0_tok_decay_param"]), in_wf)
            load(rows[0:L, :], a["L0_tok_cms_ln_g"], in_rows)
            load(rows[L:2 * L, :], a["L0_tok_cms_ln_b"], in_rows)
            load(rows[R_B1:R_X2, :], a["L0_tok_cms_b1"].rearrange("l (c p) -> (l c) p", p=P), in_rows)
            load(rows[R_X2:R_X1, :], a["L1_ffn_expert_b2"].rearrange("(q i) f -> q (i f)", i=2), in_rows)
            load(rows[R_X1:R_E1, :], a["L1_ffn_expert_b1"].rearrange("(q i) f -> q (i f)", i=2), in_rows)
            load(rows[R_E1:NR, :], a["L0_ffn_b1"].rearrange("e (c p) -> (e c) p", p=P), in_rows)
            load(r_b1[:, :], a["L1_ffn_router_b1"].unsqueeze(1), in_rows)
            load(norm_g[:, :], over_partitions(a["L0_tok_norm_g"]), in_norm)
            load(norm_b[:, :], over_partitions(a["L0_tok_norm_b"]), in_norm)

            act.wait_ge(in_tok, 16)
            for g in range(NG):
                c = slice(g * GN, (g + 1) * GN)
                copy(tokens16[:, c], tokens[:, c]).then_inc(tok16_ready, 1)
                if g == 0:
                    act.wait_ge(turn.filled, turn.number("emb"))
                    copy(embT[:, :], turn.bank("emb")[:, 0:V]).then_inc(turn.freed["act"], 1)
                    act.wait_ge(in_wf, 32)
                    nc.scalar.activation(decay[:, 0:1], decay_in[:, :], ACT.Exp, scale=-1.0).then_inc(decay_exp, 1)
            act.wait_ge(const_ready, 3)
            act.wait_ge(decay_ready, 1)

            def keep(g):
                c = slice(g * GN, (g + 1) * GN)
                act.wait_ge(hot_ready, g + 1)
                nc.scalar.activation(keep_mem[:, c], wide.bank(("tok", g))[:, :], ACT.Relu, scale=-1.0, bias=one[:, 0:1]).then_inc(wide.freed["act"], 1)
                wide.wait_read(act, ("tok", g))
                nc.scalar.activation(keep_mem[:, c], keep_mem[:, c], ACT.Identity, scale=decay[:, 3:4], bias=decay[:, 2:3]).then_inc(keep_ready, 1)

            act.wait_ge(turn.filled, turn.number("rows"))
            copy(cols[:, :], turn.bank("rows")[:, 0:NR]).then_inc(turn.freed["act"], 1)
            turn.wait_read(act, "rows")

            def wait_hT(k):
                if k >= 2:
                    kind, n = HT[k - 2]
                    if kind == "hT":
                        act.wait_ge(hp_ready, n + 1)
                    else:
                        act.wait_ge(outp.filled, outp.number(("head", n)))

            def zT_copy(key):
                i = ZT.index(key)
                act.wait_ge(turn.filled, turn.number(key))
                if i >= ZB:
                    kind, g = ZT[i - ZB]
                    ring, job = ZT_LAST[kind]
                    act.wait_ge(ring.filled, ring.number(job(g)))
                copy(zT[:, i % ZB, :], turn.bank(key)[:, 0:GN // 2].bitcast(F16)).then_inc(turn.freed["act"], 1)

            for what, n in PLAN:
                if what == "front" and n < NG:
                    keep(n)
                if what == "turn":
                    i, k = STEP[n][0], HT.index(("hT", n))
                    act.wait_ge(turn.filled, turn.number(("hT", n)))
                    wait_hT(k)
                    if n >= 2:
                        act.wait_ge(wide.filled, wide.number(("h", n - 2, FC - 1)))
                    b, gain, shift = turn.bank(("hT", n))[:, :], cols[:, i:i + 1], cols[:, L + i:L + i + 1]
                    nc.scalar.activation(hp[:, n % 2, 0, :], b, ACT.Identity, bias=shift, scale=gain).then_inc(hi_ready, 1)
                    nc.scalar.activation(hT[:, k % 2, :], b, ACT.Identity, bias=shift, scale=gain).then_inc(turn.freed["act"], 1)
                if what == "up":
                    i = STEP[n][0]
                    for c in range(FC):
                        act.wait_ge(wide.filled, wide.number(("h", n, c)))
                        if n >= 2 and c == 0:
                            act.wait_ge(outp.filled, outp.number(("o", n - 2)))
                        nc.scalar.activation(gT[:, n % 2, c, :], wide.bank(("h", n, c))[:, :], ACT.Gelu, scale=1.0 / WS16,
                                             bias=cols[:, R_B1 + i * FC + c:R_B1 + i * FC + c + 1]).then_inc(wide.freed["act"], 1)
                if what == "prep" and n == 4:
                    for key, at, m in (("qkv_w", C_Q, 3 * W), ("proj_w", C_P, W)):
                        act.wait_ge(turn.filled, turn.number(key))
                        copy(wst[0:W, at:at + m], turn.bank(key)[0:W, 0:m])
                        copy(wst[W:P, at:at + m], turn.bank(key)[0:W, 0:m]).then_inc(turn.freed["act"], 1)
                    act.wait_ge(outp.filled, outp.number("relb"))
                    copy(relb[:, :], outp.bank("relb")[:, 0:WS]).then_inc(outp.freed["act"], 1)
                if what == "xturn":
                    k = HT.index(("xT", n))
                    act.wait_ge(turn.filled, turn.number(("xT", n)))
                    wait_hT(k)
                    copy(hT[:, k % 2, :], turn.bank(("xT", n))[:, :]).then_inc(turn.freed["act"], 1)
                if what == "zturn":
                    act.wait_ge(turn.filled, turn.number(("a0", n)))
                    if n >= 2:
                        act.wait_ge(wide.filled, wide.number(("s0", n - 2)))
                    copy(z0T[:, n % 2, :], turn.bank(("a0", n))[0:W, :]).then_inc(turn.freed["act"], 1)
                if what == "score":
                    act.wait_ge(wide.filled, wide.number(("s0", n)))
                    if n >= 2:
                        act.wait_ge(outp.filled, outp.number(("ctx", n - 2)))
                    nc.scalar.activation(ex[:, n % 2, :], wide.bank(("s0", n))[:, :], ACT.Exp, scale=float(W) ** -0.5).then_inc(wide.freed["act"], 1)
                if what == "fturn":
                    zT_copy(("f0", n))
            for g in range(NG):
                act.wait_ge(gd_ready, g + 1)
                nc.scalar.activation(gex[:, group(g), :], gd[:, group(g), :], ACT.Exp).then_inc(gex_ready, 1)
            def slots_turned(k):
                act.wait_ge(turn.filled, turn.number(("xe", k)))
                copy(xeT[:, k * GN:(k + 1) * GN], turn.bank(("xe", k))[:, 0:GN // 2].bitcast(F16)).then_inc(turn.freed["act"], 1)

            slots_turned(0)
            for e in range(E):
                for k in range(slots_end(e), slots_end(e + 1)):
                    slots_turned(k)
                act.wait_ge(wide.filled, wide.number(("em", e, 0)))
                if e >= 2:
                    act.wait_ge(outp.filled, outp.number(("ey", e - 2)))
                nc.scalar.activation(hm[:, e % 2, 0, :], wide.bank(("em", e, 0))[:, 0:CAP], ACT.Relu,
                                     bias=e_b1s[:, e * EC:e * EC + 1]).then_inc(wide.freed["act"], 1)

            def qkv_copies(g):
                act.wait_ge(wide.filled, wide.number(("k", g)))
                if g >= 2:
                    act.wait_ge(wide.filled, wide.number(("s1", (g - 1) * GT - 1)))
                k = wide.bank(("k", g))[:, 0:GT * WS].rearrange("p (t k) -> p t k", t=GT)
                for h_ in range(H1):
                    last = nc.scalar.activation(km[:, g % 2, :, h_, :], k, ACT.Copy, scale=headmask[:, h_:h_ + 1])
                last.then_inc(wide.freed["act"], 1)
                act.wait_ge(wide.filled, wide.number(("q", g)))
                q = wide.bank(("q", g))[:, 0:GT * WS].rearrange("p (t q) -> p t q", t=GT)
                for w in range(2):
                    part = slice(w * W, (w + 1) * W)
                    last = copy(qbd[part, g % 2, :, w * WS:(w + 1) * WS], q[part], 1.0 / WS16)
                last.then_inc(wide.freed["act"], 1)
                act.wait_ge(outp.filled, outp.number(("v", g)))
                if g >= 2:
                    act.wait_ge(outp.filled, outp.number(("av", (g - 1) * GT - 1)))
                v5 = outp.bank(("v", g))[:, :].rearrange("p (t h i d) -> p t h i d", t=2 * GT, h=HP, i=2)
                for i in range(2):
                    part = slice(i * WS, (i + 1) * WS)
                    copy(vz[part, g % 2, 0, :, :, i * (HD + 1):i * (HD + 1) + HD], v5[part, :, :, i, :], 1.0 / WS16)
                copy(vf[:, g % 2, :], outp.bank(("v", g))[:, :], 1.0 / WS16).then_inc(vf_ready, 1)
                act.wait_ge(vf_ready, g + 1)
                act.sem_inc(outp.freed["act"], 1)

            def probs(t):
                act.wait_ge(sd_ready, t + 1)
                if t >= 2:
                    act.wait_ge(turn.filled, turn.number(("pT", t - 2)))
                    act.wait_ge(plo_ready, t - 1)
                src = sd[:, t % 2, :, :].rearrange("p h k -> p (h k)")
                nc.scalar.activation(pf[:, t % 2, :], src, ACT.Exp)
                nc.scalar.activation(pp[:, t % 2, 0, :], src, ACT.Exp).then_inc(pexp_ready, 1)

            def probs_turned(t):
                act.wait_ge(turn.filled, turn.number(("pT", t)))
                if t >= 2:
                    act.wait_ge(outp.filled, outp.number(("av", t - 2)))
                copy(pT[:, t % 2, :, :, :].rearrange("p a h q -> p (a h q)"), turn.bank(("pT", t))[:, :].bitcast(F16)).then_inc(turn.freed["act"], 1)

            act.wait_ge(parts_ready, 4)
            for what, n in PLAN2:
                if what == "turn_a1":
                    zT_copy(("a1", n))
                if what == "qkv":
                    qkv_copies(n)
                if what == "weights":
                    probs(n)
                if what == "turned":
                    probs_turned(n)
                if what == "project":
                    zT_copy(("oT", n))
                if what == "rows":
                    zT_copy(("f1", n))
                if what == "router":
                    act.wait_ge(wide.filled, wide.number(("rh", n)))
                    if n >= 2:
                        act.wait_ge(outp.filled, outp.number(("rl", n - 2)))
                        act.wait_ge(rlo_ready, n - 1)
                    rh = wide.bank(("rh", n))[0:RH, :]
                    nc.scalar.activation(rhp[0:RH, n % 2, :], rh, ACT.Relu, scale=1.0 / WS16, bias=r_b1[:, 0:1])
                    nc.scalar.activation(rhf[:, n % 2, :], rh, ACT.Relu, scale=1.0 / WS16, bias=r_b1[:, 0:1]).then_inc(wide.freed["act"], 1)
                if what == "first":
                    g, q = n
                    act.wait_ge(wide.filled, wide.number(("h1", g, q)))
                    if g >= 2:
                        act.wait_ge(wide.filled, wide.number(("h2", g - 2, XP - 1)))
                    nc.scalar.activation(h1T[:, g % 2, q, :], wide.bank(("h1", g, q))[:, :], ACT.Relu, scale=1.0 / WS16,
                                         bias=cols[:, R_X1 + q:R_X1 + q + 1]).then_inc(wide.freed["act"], 1)
                if what == "logits":
                    act.wait_ge(td_ready, n + 1)
                    nc.scalar.activation(te[:, :, :], td[:, :, :], ACT.Exp).then_inc(te_ready, 1)
                if what == "second" and n[1] == 0:
                    g = n[0]
                    act.wait_ge(wide.filled, wide.number(("h2", g, 0)))
                    if g >= 2:
                        act.wait_ge(wide.filled, wide.number(("eo", g - 2, GT - 1)))
                    nc.scalar.activation(h2T[:, g % 2, 0, :], wide.bank(("h2", g, 0))[:, :], ACT.Relu,
                                         bias=cols[:, R_X2:R_X2 + 1]).then_inc(wide.freed["act"], 1)
                if what == "choice":
                    act.wait_ge(tdl_ready, n + 1)
                    nc.scalar.activation(tex[:, :], tdl[:, :], ACT.Exp).then_inc(tex_ready, 1)

        @block.vector
        def _(dve):
            steps = [0]
            v = nc.vector

            def link(ins):
                steps[0] += 1
                ins.then_inc(dve_step, 1)
                dve.wait_ge(dve_step, steps[0])

            def ln_stats(key, src):
                k = LNS.index(key)
                for j in range(GT):
                    last = v.bn_stats(st[:, k % 2, j, :], src(j))
                link(last)
                for j in range(GT):
                    last = v.bn_aggr(mv[:, k % 2, j, :], st[:, k % 2, j, :])
                last.then_inc(stats_ready, 1)
                dve.wait_ge(stats_ready, k + 1)

            def ln_norm(key, src, dst):
                k = LNS.index(key)
                dve.wait_ge(rstd_ready, k + 1)
                for j in range(GT):
                    last = v.tensor_scalar(dst(j), src(j), mv[:, k % 2, j, 0:1], rstd[:, k % 2, j:j + 1], ALU.subtract, ALU.mult)
                return last

            def split_rows(key, src):
                i, g = ZS.index(key), key[1]
                if key[0] == "f1":
                    dve.wait_ge(turn.filled, turn.number(("oT", g)))
                if key[0] == "oT":
                    dve.wait_ge(turn.filled, turn.number(("a1", g)))
                link(v.tensor_copy(zs[:, group(g), 0:W], src))
                v.tensor_tensor(zs[:, group(g), W:2 * W], src, zs[:, group(g), 0:W], ALU.subtract).then_inc(zs_ready, 1)

            def ln_rows(key):
                k, g = LNS.index(key), key[1]
                ln_stats(key, lambda j: h[:, g * GT + j, :])
                link(ln_norm(key, lambda j: h[:, g * GT + j, :], lambda j: zf[:, k % 2, j, :]))
                split_rows(key, zf[:, k % 2, :, :])

            def weight_pair(hi, lo, src, scale):
                link(v.tensor_scalar(hi, src, scale, None, ALU.mult))
                return v.scalar_tensor_tensor(out=lo, in0=src, scalar=scale, in1=hi, op0=ALU.mult, op1=ALU.subtract)

            dve.wait_ge(const_ready, 2)
            link(v.tensor_copy(iota_vf[:, :], iota_v[:, :]))
            link(v.tensor_scalar(not_zero[:, :], iota_vf[0:V, :], 0.0, None, ALU.not_equal))
            dve.wait_ge(in_emb, 64)
            link(v.tensor_tensor(embf[:, :], emb[:, :], b_f[:, :], ALU.add))
            link(v.tensor_scalar(etable[0:V, :], embf[:, :], TS16, None, ALU.mult))
            v.scalar_tensor_tensor(out=etable[V:2 * V, :], in0=embf[:, :], scalar=TS16, in1=etable[0:V, :],
                                   op0=ALU.mult, op1=ALU.subtract).then_inc(etable_ready, 1)
            dve.wait_ge(outp.filled, outp.number("table"))
            link(v.tensor_tensor(table0[:, :], outp.bank("table")[0:V, 0:D], b_upd[:, :], ALU.add))
            dve.sem_inc(outp.freed["dve"], 1)
            link(v.tensor_scalar(table1[:, :], table0[:, :], not_zero[:, 0:1], TS16, ALU.mult, ALU.mult))
            link(v.tensor_copy(table[0:V, :], table1[:, :]))
            v.tensor_tensor(table[V:2 * V, :], table1[:, :], table[0:V, :], ALU.subtract).then_inc(table_ready, 1)
            dve.wait_ge(decay_exp, 1)
            link(v.tensor_scalar(decay[:, 1:2], decay[:, 0:1], 1.0, None, ALU.add))
            link(v.reciprocal(decay[:, 2:3], decay[:, 1:2]))
            v.tensor_scalar(decay[:, 3:4], decay[:, 2:3], -1.0, 1.0, ALU.mult, ALU.add).then_inc(decay_ready, 1)

            def one_hot(g):
                c = slice(g * GN, (g + 1) * GN)
                dve.wait_ge(wide.filled, wide.number(("tok", g)))
                v.tensor_scalar(onehot[:, c], wide.bank(("tok", g))[:, :], iota_vf[:, 0:1], None, ALU.is_equal).then_inc(hot_ready, 1)
                dve.wait_ge(keep_ready, g + 1)
                link(v.memset(keep_mem[:, c].rearrange("p (t s) -> p t s", s=P)[:, :, 0:1], 0.0))

            def memory(g):
                c = slice(g * GN, (g + 1) * GN)
                dve.wait_ge(wide.filled, wide.number(("u", g)))
                v.tensor_tensor_scan(mems[:, c], keep_mem[:, c], wide.bank(("u", g))[:, :], 0.0, ALU.mult, ALU.add).then_inc(wide.freed["dve"], 1)

            def first_norm(g):
                dve.wait_ge(outp.filled, outp.number(("y", g)))
                y = outp.bank(("y", g))[:, :].rearrange("p (t d) -> p t d", t=GT)
                ln_stats(("y", g), lambda j: y[:, j, :])
                k = LNS.index(("y", g))
                for j in range(GT):
                    last = v.scalar_tensor_tensor(out=ln_t[:, j, :], in0=y[:, j, :], scalar=mv[:, k % 2, j, 0:1], in1=norm_g[:, :],
                                                  op0=ALU.subtract, op1=ALU.mult)
                last.then_inc(outp.freed["dve"], 1)
                outp.wait_read(dve, ("y", g))
                dve.wait_ge(rstd_ready, k + 1)
                for j in range(GT):
                    last = v.scalar_tensor_tensor(out=x[:, g * GT + j, :], in0=ln_t[:, j, :], scalar=rstd[:, k % 2, j:j + 1],
                                                  in1=norm_b[:, :], op0=ALU.mult, op1=ALU.add)
                last.then_inc(x_ready, 1)
                dve.wait_ge(x_ready, g + 1)
                n = AT[0, g]
                ln_stats(("c", n), lambda j: x[:, g * GT + j, :])
                ln_norm(("c", n), lambda j: x[:, g * GT + j, :], lambda j: hn[:, g, j * P:(j + 1) * P]).then_inc(hn_ready, 1)

            def w1_pair(i):
                dve.wait_ge(in_w1[i], 16)
                weight_pair(w1p[:, 0, i, :], w1p[:, 1, i, :], w1[:, i, :], WS16).then_inc(w1_ready, 1)

            def turn_pair(n):
                k = HT.index(("hT", n))
                dve.wait_ge(hi_ready, n + 1)
                turn.wait_read(dve, ("hT", n))
                v.tensor_tensor(hp[:, n % 2, 1, :], hT[:, k % 2, :], hp[:, n % 2, 0, :], ALU.subtract).then_inc(hp_ready, 1)

            def front(s):
                if s < NG:
                    one_hot(s)
                if 1 <= s <= NG:
                    memory(s - 1)
                if s == 2:
                    dve.wait_ge(zero_rows, 16)
                    dve.wait_ge(in_norm, 32)
                if s >= 2:
                    first_norm(s - 2)

            PIECES = [(i * C_Q // 4, (i + 1) * C_Q // 4) for i in range(4)] + [(C_Q, C_R), (C_R, C_N)]

            def prep(i):
                if i == 0:
                    dve.wait_ge(in_exp, 16 * (E + 5))
                    turn.wait_read(dve, "rows")
                    dve.wait_ge(parts_ready, 1)
                if i == 4:
                    turn.wait_read(dve, "proj_w")
                if i == 5:
                    dve.wait_ge(in_x1, 16 * 10)
                c = slice(*PIECES[i])
                weight_pair(wp[:, 0, c], wp[:, 1, c], wst[:, c], WS16).then_inc(prep_ready, 1)
                if i == 0:
                    v.tensor_scalar(e_b1s[:, :], cols[:, R_E1:NR], WS16, None, ALU.mult)
                    v.tensor_copy(rank8[:, :], rank_i[:, :])
                    v.tensor_scalar(rank6[:, :], rank_i[:, 0:X], float(X - E), None, ALU.add)
                    link(v.tensor_copy(trash[:, :], trash_i[:, :]))
                if i == 5:
                    weight_pair(r_w2p[:, 0, :], r_w2p[:, 1, :], r_w2[:, :], WS16)
                    for c, scale in ((slice(0, W), WS16), (slice(W, BN), 1.0)):
                        v.tensor_scalar(bias_p[0:1, c], bias_rows[0:1, c], scale, None, ALU.mult)
                        link(v.tensor_scalar(bias_hi[32:33, c], bias_rows[32:33, c], scale, None, ALU.mult))
                        last = v.scalar_tensor_tensor(out=bias_p[32:33, c], in0=bias_rows[32:33, c], scalar=scale, in1=bias_hi[32:33, c],
                                                      op0=ALU.mult, op1=ALU.subtract)
                    last.then_inc(prep_ready, 1)

            def down(n):
                i, g = STEP[n]
                dve.wait_ge(outp.filled, outp.number(("o", n)))
                dve.wait_ge(xb_ready, NEXT.index(n) + 1)
                v.tensor_tensor(x[:, group(g), :], outp.bank(("o", n))[:, :].rearrange("p (t d) -> p t d", t=GT), xb[:, group(g), :],
                                ALU.add).then_inc(x_ready, 1)
                dve.wait_ge(x_ready, NG + n + 1)
                dve.sem_inc(outp.freed["dve"], 1)
                if i + 1 < L:
                    m = AT[i + 1, g]
                    ln_stats(("c", m), lambda j: x[:, g * GT + j, :])
                    ln_norm(("c", m), lambda j: x[:, g * GT + j, :], lambda j: hn[:, g, j * P:(j + 1) * P]).then_inc(hn_ready, 1)

            def head(g):
                dve.wait_ge(in_head, 32)
                dve.wait_ge(outp.filled, outp.number(("head", g)))
                link(v.tensor_tensor(h[:, group(g), :], outp.bank(("head", g))[:, 0:GT * W].rearrange("p (t w) -> p t w", t=GT),
                                     bm(head_b[:, :], GT), ALU.add))
                dve.sem_inc(outp.freed["dve"], 1)
                ln_stats(("a0", g), lambda j: h[:, g * GT + j, :])
                ln_norm(("a0", g), lambda j: h[:, g * GT + j, :], lambda j: z0[:, g * GT + j, 0:W]).then_inc(z0_ready, 1)

            def context(g):
                dve.wait_ge(outp.filled, outp.number(("ctx", g)))
                c = outp.bank(("ctx", g))[:, 0:GT * (W + 1)].rearrange("p (t w) -> p t w", t=GT)
                link(v.reciprocal(rs[:, g % 2, :], c[:, :, W]))
                for j in range(GT):
                    last = v.scalar_tensor_tensor(out=h[:, g * GT + j, :], in0=c[:, j, 0:W], scalar=rs[:, g % 2, j:j + 1],
                                                  in1=h[:, g * GT + j, :], op0=ALU.mult, op1=ALU.add)
                link(last)
                dve.sem_inc(outp.freed["dve"], 1)
                ln_rows(("f0", g))

            def gate(g):
                t = group(g)
                dve.wait_ge(in_gate, 32)
                dve.wait_ge(outp.filled, outp.number(("gate", g)))
                lg = outp.bank(("gate", g))[:, 0:GT * E].rearrange("p (t e) -> p t e", t=GT)
                link(v.scalar_tensor_tensor(out=glog[:, t, :], in0=lg, scalar=1.0 / WS16, in1=bm(gate_b[:, :], GT), op0=ALU.mult, op1=ALU.add))
                dve.sem_inc(outp.freed["dve"], 1)
                link(v.tensor_reduce(gm[:, t], glog[:, t, :], AX, ALU.max))
                v.tensor_tensor(gd[:, t, :], glog[:, t, :], bc(gm[:, t], E), ALU.subtract).then_inc(gd_ready, 1)
                dve.wait_ge(gd_ready, g + 1)
                link(v.scalar_tensor_tensor(out=gv[:, t, :], in0=gd[:, t, :], scalar=0.0, in1=bm(rank8[:, :], GT), op0=ALU.is_equal, op1=ALU.mult))
                link(v.tensor_reduce(gbest[:, t], gv[:, t, :], AX, ALU.max))
                v.tensor_tensor(goh[:, t, :], bm(rank8[:, :], GT), bc(gbest[:, t], E), ALU.is_equal).then_inc(goh_ready, 1)
                link(v.tensor_scalar(base[:, t], gbest[:, t], -float(CAP), float(E * CAP - 1), ALU.mult, ALU.add))
                link(v.tensor_tensor(slot[:, t], base[:, t], trash[:, t], ALU.subtract))

            def place(g):
                t = group(g)
                dve.wait_ge(outp.filled, outp.number(("pos", g)))
                dve.wait_ge(goh_ready, g + 1)
                link(v.tensor_tensor(pc[:, t, :], outp.bank(("pos", g))[:, 0:GT * E].rearrange("p (t e) -> p t e", t=GT), goh[:, t, :], ALU.mult))
                dve.sem_inc(outp.freed["dve"], 1)
                link(v.tensor_reduce(pos1[:, t], pc[:, t, :], AX, ALU.add))
                v.scalar_tensor_tensor(out=idx_g[:, t], in0=pos1[:, t], scalar=float(CAP), in1=base[:, t], op0=ALU.min, op1=ALU.add)
                v.tensor_scalar(kept[:, t], pos1[:, t], float(CAP), None, ALU.is_le)
                link(v.tensor_tensor(slot2[:, t], slot[:, t], pos1[:, t], ALU.add))
                link(v.tensor_tensor(slot2[:, t], slot2[:, t], kept[:, t], ALU.mult))
                v.tensor_tensor(idx_s[:, t], slot2[:, t], trash[:, t], ALU.add).then_inc(idx_ready, 1)

            for what, n in PLAN:
                if what == "front":
                    front(n)
                if what == "w1":
                    w1_pair(n)
                if what == "turn":
                    turn_pair(n)
                if what == "down":
                    down(n)
                if what == "prep":
                    prep(n)
                if what == "head":
                    head(n)
                if what == "context":
                    context(n)
                if what == "gate":
                    gate(n)
                if what == "place":
                    place(n)
            for g in range(NG):
                t = group(g)
                dve.wait_ge(gex_ready, g + 1)
                link(v.tensor_reduce(gsum[:, t], gex[:, t, :], AX, ALU.add))
                link(v.reciprocal(prob[:, t], gsum[:, t]))
                link(v.tensor_tensor(pk[:, t], prob[:, t], kept[:, t], ALU.mult))

            R = CAP - 2 * P
            for e in range(E + 1):
                if e < E:
                    dve.wait_ge(wide.filled, wide.number(("em", e, 1)))
                    if e >= 2:
                        dve.wait_ge(outp.filled, outp.number(("ey", e - 2)))
                    v.tensor_scalar(hm[:, e % 2, 1, :], wide.bank(("em", e, 1))[:, 0:CAP], e_b1s[:, e * EC + 1:e * EC + 2], 0.0,
                                    ALU.add, ALU.max).then_inc(wide.freed["dve"], 1)
                if e >= 1:
                    q = e - 1
                    dve.wait_ge(outp.filled, outp.number(("ey", q)))
                    y = outp.bank(("ey", q))[:, 0:3 * W].rearrange("p (m w) -> p m w", m=3)
                    t = 5 * (q // 2)
                    if q % 2 == 0:
                        whole, part, pt, m0 = slice(t, t + 2), slice(0, R), t + 2, 0
                    else:
                        whole, part, pt, m0 = slice(t + 3, t + 5), slice(P - R, P), t + 2, 1
                    v.scalar_tensor_tensor(out=ye[part, pt, :], in0=y[part, 2 - 2 * m0, :], scalar=1.0 / WS16, in1=e_b2[part, q, :], op0=ALU.mult, op1=ALU.add)
                    v.scalar_tensor_tensor(out=ye[:, whole, :], in0=y[:, m0:m0 + 2, :], scalar=1.0 / WS16, in1=bm(e_b2[:, q, :], 2),
                                           op0=ALU.mult, op1=ALU.add).then_inc(ye_ready, 1)
                    dve.wait_ge(ye_ready, q + 1)
                    dve.sem_inc(outp.freed["dve"], 1)

            def returned(g):
                t = group(g)
                dve.wait_ge(gathered[g], 16 * GT)
                link(v.tensor_tensor(yp[:, :, :], yg[:, t, :], bc(pk[:, t], W), ALU.mult))
                link(v.tensor_scalar(ya[:, :, :], yp[:, :, :], 0.0, None, ALU.max))
                link(v.scalar_tensor_tensor(out=yn[:, :, :], in0=yp[:, :, :], scalar=0.0, in1=ya[:, :, :], op0=ALU.min, op1=ALU.add))
                v.tensor_scalar(yfin[:, :, :], yn[:, :, :], 0.0, 0.0, ALU.mult, ALU.is_equal)
                link(v.tensor_scalar(yc[:, :, :], yn[:, :, :], CLIP, -CLIP, ALU.min, ALU.max))
                link(v.copy_predicated(yc[:, :, :], yfin[:, :, :], yn[:, :, :]))
                link(v.tensor_tensor(h[:, t, :], h[:, t, :], yc[:, :, :], ALU.add))
                ln_rows(("a1", g))

            def biased(t):
                dve.wait_ge(wide.filled, wide.number(("s1", t)))
                if t >= 2:
                    dve.wait_ge(sd_ready, t - 1)
                s3 = wide.bank(("s1", t))[:, :].rearrange("p (h k) -> p h k", h=H1)
                v.scalar_tensor_tensor(out=sm[:, t % 2, :, :], in0=s3, scalar=float(HD) ** -0.5, in1=bm(relb[:, :], H1),
                                       op0=ALU.mult, op1=ALU.add).then_inc(wide.freed["dve"], 1)
                wide.wait_read(dve, ("s1", t))
                v.tensor_reduce(smx[:, t % 2, :], sm[:, t % 2, :, :], AX, ALU.max).then_inc(smx_ready, 1)

            def heads_out(t):
                dve.wait_ge(outp.filled, outp.number(("av", t)))
                g, j = t // GT, t % GT
                av = outp.bank(("av", t))[:, 0:HP * 2 * VW].rearrange("p (h w i d) -> p w h i d", h=HP, w=2, i=2)
                r = rden[:, t % 2, :].rearrange("p (h i) -> p h i", i=2)
                for w in range(2):
                    part = slice(w * WS, (w + 1) * WS)
                    last = v.reciprocal(r[part], av[part, w, :, :, HD])
                link(last)
                for w in range(2):
                    part = slice(w * WS, (w + 1) * WS)
                    last = v.tensor_tensor(o[part, g % 2, j, :].rearrange("p (h i d) -> p h i d", h=HP, i=2), av[part, w, :, :, 0:HD],
                                           r[part].unsqueeze(3).broadcast_to([WS, HP, 2, HD]), ALU.mult)
                last.then_inc(outp.freed["dve"], 1)
                if j == GT - 1:
                    outp.wait_read(dve, ("av", t))
                    split_rows(("oT", g), o[:, g % 2, :, :])

            def projected(g):
                dve.wait_ge(outp.filled, outp.number(("proj", g)))
                link(v.scalar_tensor_tensor(out=h[:, group(g), :], in0=outp.bank(("proj", g))[:, 0:GT * W].rearrange("p (t w) -> p t w", t=GT),
                                            scalar=1.0 / WS16, in1=h[:, group(g), :], op0=ALU.mult, op1=ALU.add))
                dve.sem_inc(outp.freed["dve"], 1)
                ln_rows(("f1", g))

            for what, n in PLAN2:
                if what == "returned":
                    returned(n)
                if what == "scores":
                    biased(n)
                if what == "applied":
                    heads_out(n)
                if what == "project":
                    projected(n)
                if what == "router":
                    wide.wait_read(dve, ("rh", n))
                    if n >= 2:
                        dve.wait_ge(outp.filled, outp.number(("rl", n - 2)))
                    v.tensor_tensor(rhp[RH:2 * RH, n % 2, :], rhf[:, n % 2, :], rhp[0:RH, n % 2, :], ALU.subtract).then_inc(rlo_ready, 1)
                if what == "logits":
                    dve.wait_ge(outp.filled, outp.number(("rl", n)))
                    lg = outp.bank(("rl", n))[:, 0:GT * X].rearrange("p (t e) -> p t e", t=GT)
                    link(v.scalar_tensor_tensor(out=tl[:, :, :], in0=lg, scalar=1.0 / WS16, in1=bm(r_b2[:, :], GT), op0=ALU.mult, op1=ALU.add))
                    dve.sem_inc(outp.freed["dve"], 1)
                    link(v.tensor_reduce(tm[:, :], tl[:, :, :], AX, ALU.max))
                    v.tensor_tensor(td[:, :, :], tl[:, :, :], bc(tm[:, :], X), ALU.subtract).then_inc(td_ready, 1)
                    dve.wait_ge(td_ready, n + 1)
                    link(v.scalar_tensor_tensor(out=tv[:, :, :], in0=td[:, :, :], scalar=0.0, in1=bm(rank6[:, :], GT), op0=ALU.is_equal, op1=ALU.mult))
                    link(v.tensor_reduce(tb[:, :], tv[:, :, :], AX, ALU.max))
                    link(v.tensor_tensor(o1[:, :, :], bm(rank6[:, :], GT), bc(tb[:, :], X), ALU.is_equal))
                if what == "choice":
                    dve.wait_ge(te_ready, n + 1)
                    v.tensor_reduce(tsum[:, :], te[:, :, :], AX, ALU.add)
                    link(v.scalar_tensor_tensor(out=tp[:, :, :], in0=o1[:, :, :], scalar=-4.0, in1=te[:, :, :], op0=ALU.mult, op1=ALU.add))
                    v.reciprocal(trs[:, :], tsum[:, :])
                    link(v.tensor_reduce(m2[:, :], tp[:, :, :], AX, ALU.max))
                    link(v.tensor_tensor(teq[:, :, :], tp[:, :, :], bc(m2[:, :], X), ALU.is_equal))
                    v.scalar_tensor_tensor(out=tdl[:, :], in0=m2[:, :], scalar=-1.0, in1=trs[:, :], op0=ALU.add, op1=ALU.mult).then_inc(tdl_ready, 1)
                    link(v.tensor_tensor(tv[:, :, :], teq[:, :, :], bm(rank6[:, :], GT), ALU.mult))
                    link(v.tensor_reduce(tb[:, :], tv[:, :, :], AX, ALU.max))
                    link(v.tensor_tensor(o2[:, :, :], bm(rank6[:, :], GT), bc(tb[:, :], X), ALU.is_equal))
                if what == "second" and n[1] > 0:
                    g, q = n
                    dve.wait_ge(wide.filled, wide.number(("h2", g, q)))
                    v.tensor_scalar(h2T[:, g % 2, q, :], wide.bank(("h2", g, q))[:, :], cols[:, R_X2 + q:R_X2 + q + 1], 0.0, ALU.add, ALU.max).then_inc(wide.freed["dve"], 1)
                if what == "shares":
                    dve.wait_ge(tex_ready, n + 1)
                    link(v.tensor_scalar(tw0[:, :], tex[:, :], 1.0, None, ALU.add))
                    link(v.reciprocal(tw1[:, :], tw0[:, :]))
                    link(v.tensor_tensor(tw2[:, :], tw1[:, :], tex[:, :], ALU.mult))
                    link(v.tensor_tensor(o1[:, :, :], o1[:, :, :], bc(tw1[:, :], X), ALU.mult))
                    link(v.tensor_tensor(o2[:, :, :], o2[:, :, :], bc(tw2[:, :], X), ALU.mult))
                    v.tensor_tensor(route[:, group(n), :], o1[:, :, :], o2[:, :, :], ALU.add).then_inc(route_ready, 1)
                if what == "third":
                    g, j = n
                    t = g * GT + j
                    dve.wait_ge(route_ready, g + 1)
                    dve.wait_ge(wide.filled, wide.number(("eo", g, j)))
                    v.tensor_tensor(shares[:, j % 2, :, :], wide.bank(("eo", g, j))[:, 0:X * W].rearrange("p (e w) -> p e w", e=X),
                                    bc(route[:, t, :], W), ALU.mult).then_inc(wide.freed["dve"], 1)
                    wide.wait_read(dve, ("eo", g, j))
                    last = v.tensor_reduce(chosen[:, g % 2, j, :], shares[:, j % 2, :, :].rearrange("p e w -> p w e"), AX, ALU.add)
                    if j == GT - 1:
                        link(last)
                        v.tensor_tensor(res[:, group(g), :], chosen[:, g % 2, :, :], h[:, group(g), :], ALU.add).then_inc(res_ready, 1)

        @block.tensor
        def _(pe):
            def mm(o_, l_, r_, start=True, stop=True):
                return nc.tensor.matmul(o_, l_, r_, start=start, stop=stop)

            def turns(key, srcs, width):
                turn.wait_free(pe, key)
                for j, src in enumerate(srcs):
                    last = nc.tensor.transpose(turn.bank(key)[0:width, j * P:j * P + src.shape[0]], src, ident[0:src.shape[0], 0:src.shape[0]])
                last.then_inc(turn.filled, 1)

            def turns16(key, srcs):
                turn.wait_free(pe, key)
                bank = turn.bank(key)[:, :].bitcast(F16)
                for j, src in enumerate(srcs):
                    last = nc.tensor.transpose(bank[:, j * P:(j + 1) * P], src, ident16[:, :])
                last.then_inc(turn.filled, 1)

            def weights(a0, a1):
                return [wp[:, i, a0:a1] for i in range(2)]

            pe.wait_ge(ident_ready, 1)
            pe.wait_ge(in_emb, 64)
            turns("emb", [emb[:, :]], D)
            pe.wait_ge(in_rows, 112)
            turns("rows", [rows[:, :]], P)
            turn.wait_read(pe, "emb")
            mm(outp.bank("table")[0:V, 0:D], embT[:, :], w_upd[:, :]).then_inc(outp.filled, 1)
            def front(s):
                if s < NG:
                    pe.wait_ge(tok16_ready, s + 1)
                    pe.wait_ge(const_ready, 1)
                    wide.wait_free(pe, ("tok", s))
                    mm(wide.bank(("tok", s))[:, :], ones16[0:1, :], tokens16[:, s * GN:(s + 1) * GN]).then_inc(wide.filled, 1)
                if 1 <= s <= NG:
                    g = s - 1
                    pe.wait_ge(table_ready, 1)
                    pe.wait_ge(hot_ready, s)
                    wide.wait_free(pe, ("u", g))
                    mm(wide.bank(("u", g))[:, :], table[:, :], onehot[:, g * GN:(g + 1) * GN]).then_inc(wide.filled, 1)
                if s >= 2:
                    g = s - 2
                    pe.wait_ge(etable_ready, 1)
                    pe.wait_ge(in_wf, 32)
                    wide.wait_read(pe, ("u", g))
                    outp.wait_free(pe, ("y", g))
                    for j in range(GT):
                        c = slice((g * GT + j) * P, (g * GT + j + 1) * P)
                        y = outp.bank(("y", g))[:, j * D:(j + 1) * D]
                        mm(y, onehot[:, c], etable[:, :], stop=False)
                        last = mm(y, mems[:, c], w_f[:, :], start=False)
                    last.then_inc(outp.filled, 1)

            def up(n):
                i, g = STEP[n]
                pe.wait_ge(hi_ready, n + 1)
                pe.wait_ge(w1_ready, i + 1)

                def high_rows(c):
                    wide.wait_free(pe, ("h", n, c))
                    b = wide.bank(("h", n, c))[:, :]
                    mm(b, w1p[:, 0, i, c * P:(c + 1) * P], hp[:, n % 2, 0, :], stop=False)
                    mm(b, w1p[:, 1, i, c * P:(c + 1) * P], hp[:, n % 2, 0, :], start=False, stop=False)

                high_rows(0)
                high_rows(1)
                pe.wait_ge(hp_ready, n + 1)
                for c in range(FC):
                    if c >= 2:
                        high_rows(c)
                    mm(wide.bank(("h", n, c))[:, :], w1p[:, 0, i, c * P:(c + 1) * P], hp[:, n % 2, 1, :], start=False).then_inc(wide.filled, 1)

            def down(n):
                i = STEP[n][0]
                key = ("o", n)
                wide.wait_read(pe, ("h", n, FC - 1))
                pe.wait_ge(in_w2[i], 16)
                outp.wait_free(pe, key)
                for j in range(GT):
                    for c in range(FC):
                        last = mm(outp.bank(key)[:, j * D:(j + 1) * D], gT[:, n % 2, c, j * P:(j + 1) * P], w2[:, i, c, :],
                                  start=(c == 0), stop=(c == FC - 1))
                last.then_inc(outp.filled, 1)

            def z_turned(key):
                turn.wait_read(pe, key)
                return zT[:, ZT.index(key) % ZB, :]

            def turn_rows(key):
                pe.wait_ge(zs_ready, ZS.index(key) + 1)
                turns16(key, [zs[:, key[1] * GT + j, 0:2 * W] for j in range(GT)])

            for what, n in PLAN:
                if what == "front":
                    front(n)
                if what == "turn":
                    g = STEP[n][1]
                    pe.wait_ge(hn_ready, NEXT.index(n) + 1)
                    turns(("hT", n), [hn[:, g, j * P:(j + 1) * P] for j in range(GT)], P)
                if what == "up":
                    up(n)
                if what == "down":
                    down(n)
                if what == "prep" and n == 4:
                    pe.wait_ge(in_att, 64)
                    pe.wait_ge(parts_ready, 1)
                    turns("qkv_w", [qkv_rows[:, 0, :], qkv_rows[0:W, 1, :]], W)
                    turns("proj_w", [proj_rows[:, :]], W)
                    outp.wait_free(pe, "relb")
                    mm(outp.bank("relb")[:, 0:WS], flip[:, :, :].rearrange("r w q -> r (w q)"), relb_up[:, :]).then_inc(outp.filled, 1)
                if what == "xturn":
                    pe.wait_ge(x_ready, NG + AT[L - 1, n] + 1)
                    turns(("xT", n), [x[:, n * GT + j, :] for j in range(GT)], P)
                if what == "head":
                    pe.wait_ge(in_head, 32)
                    turn.wait_read(pe, ("xT", n))
                    outp.wait_free(pe, ("head", n))
                    k = HT.index(("xT", n))
                    for j in range(GT):
                        last = mm(outp.bank(("head", n))[:, j * W:(j + 1) * W], hT[:, k % 2, j * P:(j + 1) * P], head_w[:, :])
                    last.then_inc(outp.filled, 1)
                if what == "zturn":
                    pe.wait_ge(z0_ready, n + 1)
                    turns(("a0", n), [z0[:, n * GT + j, 0:W] for j in range(GT)], W)
                if what == "score":
                    turn.wait_read(pe, ("a0", n))
                    wide.wait_free(pe, ("s0", n))
                    for j in range(GT):
                        q = z0T[:, n % 2, j * P:(j + 1) * P]
                        last = mm(wide.bank(("s0", n))[:, j * P:(j + 1) * P], q, q)
                    last.then_inc(wide.filled, 1)
                if what == "context":
                    wide.wait_read(pe, ("s0", n))
                    outp.wait_free(pe, ("ctx", n))
                    for j in range(GT):
                        last = mm(outp.bank(("ctx", n))[:, j * (W + 1):(j + 1) * (W + 1)], ex[:, n % 2, j * P:(j + 1) * P], z0[:, n * GT + j, :])
                    last.then_inc(outp.filled, 1)
                if what == "fturn":
                    turn_rows(("f0", n))
                if what == "gate":
                    pe.wait_ge(prep_ready, 1)
                    zt = z_turned(("f0", n))
                    outp.wait_free(pe, ("gate", n))
                    hi, lo = weights(0, E)
                    for j in range(GT):
                        b = outp.bank(("gate", n))[:, j * E:(j + 1) * E]
                        mm(b, zt[:, j * P:(j + 1) * P], hi, stop=False)
                        last = mm(b, zt[:, j * P:(j + 1) * P], lo, start=False)
                    last.then_inc(outp.filled, 1)
                if what == "place":
                    g = n
                    pe.wait_ge(goh_ready, g + 1)
                    outp.wait_free(pe, ("pos", g))
                    cnt = outp.bank(("pos", g))[:, 0:GT * E].rearrange("p (t e) -> p t e", t=GT)
                    last = mm(cnt, tri[:, :], goh[:, group(g), :], stop=False)
                    for t in range(g * GT + GT - 1):
                        j = max(0, t - g * GT + 1)
                        last = mm(cnt[:, j:GT, :], ones16[:, :], bm(goh[:, t, :], GT - j), start=False, stop=(t == g * GT + GT - 2))
                    last.then_inc(outp.filled, 1)

            def turn_slots(k):
                pe.wait_ge(rows_back[k], 16)
                turns16(("xe", k), [xe[:, 4 * k + j, :] for j in range(4)])

            turn_slots(0)
            pe.wait_ge(prep_ready, 4)
            for e in range(E + 1):
                if e < E:
                    for k in range(slots_end(e), slots_end(e + 1)):
                        turn_slots(k)
                    turn.wait_read(pe, ("xe", slots_end(e) - 1))
                    for c in range(EC):
                        wide.wait_free(pe, ("em", e, c))
                        b = wide.bank(("em", e, c))[:, 0:CAP]
                        at = C_E + e * EF + c * P
                        hi, lo = weights(at, at + P)
                        mm(b, hi, xeT[:, e * CAP:(e + 1) * CAP], stop=False)
                        mm(b, lo, xeT[:, e * CAP:(e + 1) * CAP], start=False).then_inc(wide.filled, 1)
                if e >= 1:
                    q = e - 1
                    for c in range(EC):
                        wide.wait_read(pe, ("em", q, c))
                    outp.wait_free(pe, ("ey", q))
                    cuts = [(0, P, 0), (P, 2 * P, 0), (2 * P, CAP, 0)] if q % 2 == 0 else [(0, P // 2, P // 2), (P // 2, P // 2 + P, 0), (P // 2 + P, CAP, 0)]
                    for m, (s0, s1, p0) in enumerate(cuts):
                        for c in range(EC):
                            last = mm(outp.bank(("ey", q))[p0:p0 + s1 - s0, m * W:(m + 1) * W], hm[:, q % 2, c, s0:s1], e_w2[:, q, c, :], start=(c == 0), stop=(c == EC - 1))
                    last.then_inc(outp.filled, 1)

            def qkv(g):
                zt = z_turned(("a1", g))
                zw = zt.rearrange("p (t w q) -> p w t q", t=GT, w=2)
                for key, at in (("k", C_Q + W), ("q", C_Q)):
                    wide.wait_free(pe, (key, g))
                    hi, lo = weights(at, at + W)
                    for w in range(2):
                        b = wide.bank((key, g))[w * W:(w + 1) * W, 0:GT * WS]
                        mm(b, hi, zw[:, w, :, :], stop=False)
                        last = mm(b, lo, zw[:, w, :, :], start=False)
                    last.then_inc(wide.filled, 1)
                outp.wait_free(pe, ("v", g))
                hi, lo = weights(C_Q + 2 * W, C_Q + 3 * W)
                for t in range(2 * GT):
                    for i in range(2):
                        b = outp.bank(("v", g))[i * WS:(i + 1) * WS, t * W:(t + 1) * W]
                        mm(b, zt[:, t * WS:(t + 1) * WS], hi, stop=False)
                        last = mm(b, zt[:, t * WS:(t + 1) * WS], lo, start=False)
                last.then_inc(outp.filled, 1)

            def pair(b, at, m, zt):
                hi, lo = weights(at, at + m)
                mm(b, hi, zt, stop=False)
                return mm(b, lo, zt, start=False)

            pe.wait_ge(in_xbd, 64)
            pe.wait_ge(prep_ready, 7)
            pe.wait_ge(parts_ready, 4)
            for what, n in PLAN2:
                if what == "turn_a1":
                    turn_rows(("a1", n))
                if what == "qkv":
                    qkv(n)
                if what == "scores":
                    g, j = n // GT, n % GT
                    wide.wait_read(pe, ("q", g))
                    wide.wait_free(pe, ("s1", n))
                    mm(wide.bank(("s1", n))[:, :], qbd[:, g % 2, j, :], km[:, g % 2, j, :, :].rearrange("p h k -> p (h k)")).then_inc(wide.filled, 1)
                if what == "turned":
                    pe.wait_ge(pexp_ready, n + 1)
                    pe.wait_ge(plo_ready, n + 1)
                    turns16(("pT", n), [pp[:, n % 2, i, q * P:(q + 1) * P] for i in range(2) for q in range(HP)])
                if what == "applied":
                    t, g, j = n, n // GT, n % GT
                    turn.wait_read(pe, ("pT", t))
                    outp.wait_read(pe, ("v", g))
                    pe.wait_ge(vlo_ready, 2 * g + 2)
                    outp.wait_free(pe, ("av", t))
                    for q in range(HP):
                        b = outp.bank(("av", t))[:, q * 2 * VW:(q + 1) * 2 * VW].rearrange("p (w d) -> p w d", w=2)
                        hi, lo = (vz[:, g % 2, i, 2 * j:2 * j + 2, q, :] for i in range(2))
                        mm(b, pT[:, t % 2, 0, q, :], hi, stop=False)
                        mm(b, pT[:, t % 2, 0, q, :], lo, start=False, stop=False)
                        last = mm(b, pT[:, t % 2, 1, q, :], hi, start=False)
                    last.then_inc(outp.filled, 1)
                if what == "project":
                    g = n
                    turn_rows(("oT", g))
                    zt = z_turned(("oT", g))
                    outp.wait_free(pe, ("proj", g))
                    hi, lo = weights(C_P, C_P + W)
                    for j in range(GT):
                        b = outp.bank(("proj", g))[:, j * W:(j + 1) * W]
                        mm(b, ones16[0:BR, :], bias_p[:, 0:W], stop=False)
                        mm(b, zt[:, j * P:(j + 1) * P], hi, start=False, stop=False)
                        last = mm(b, zt[:, j * P:(j + 1) * P], lo, start=False)
                    last.then_inc(outp.filled, 1)
                if what == "rows":
                    turn_rows(("f1", n))
                if what == "router":
                    wide.wait_free(pe, ("rh", n))
                    pair(wide.bank(("rh", n))[0:RH, :], C_R, RH, z_turned(("f1", n))).then_inc(wide.filled, 1)
                if what == "first":
                    g, q = n
                    wide.wait_free(pe, ("h1", g, q))
                    pair(wide.bank(("h1", g, q))[:, :], C_X + q * P, P, z_turned(("f1", g))).then_inc(wide.filled, 1)
                if what == "logits":
                    pe.wait_ge(rlo_ready, n + 1)
                    outp.wait_free(pe, ("rl", n))
                    for j in range(GT):
                        b = outp.bank(("rl", n))[:, j * X:(j + 1) * X]
                        mm(b, rhp[:, n % 2, j * P:(j + 1) * P], r_w2p[:, 0, :], stop=False)
                        last = mm(b, rhp[:, n % 2, j * P:(j + 1) * P], r_w2p[:, 1, :], start=False)
                    last.then_inc(outp.filled, 1)
                if what == "second":
                    g, q = n
                    wide.wait_read(pe, ("h1", g, q))
                    wide.wait_free(pe, ("h2", g, q))
                    mm(wide.bank(("h2", g, q))[:, :], x_w2[:, q, :], h1T[:, g % 2, q, :]).then_inc(wide.filled, 1)
                if what == "third":
                    g, j = n
                    for q in range(XP):
                        wide.wait_read(pe, ("h2", g, q))
                    wide.wait_free(pe, ("eo", g, j))
                    b = wide.bank(("eo", g, j))
                    mm(b[:, 0:X * W], ones16[0:BR, :], bias_p[:, W:BN], stop=False)
                    for q in range(XP):
                        last = mm(b[:, q * P:(q + 1) * P], h2T[:, g % 2, q, j * P:(j + 1) * P], x_w3[:, q, :], start=False, stop=(q == XP - 1))
                    last.then_inc(wide.filled, 1)


_INS = ["x", "L0_tok_emb", "L0_tok_W_upd", "L0_tok_b_upd", "L0_tok_W_f", "L0_tok_b_f", "L0_tok_decay_param",
        "L0_tok_norm_g", "L0_tok_norm_b", "L0_tok_cms_ln_g", "L0_tok_cms_ln_b", "L0_tok_cms_W1", "L0_tok_cms_b1",
        "L0_tok_cms_W2", "L0_tok_cms_b2", "L0_tok_head_W", "L0_tok_head_b", "L0_ffn_gate_w", "L0_ffn_gate_b",
        "L0_ffn_w1", "L0_ffn_b1", "L0_ffn_w2", "L0_ffn_b2", "L1_attn_w_qkv", "L1_attn_w_proj", "L1_attn_b_proj",
        "L1_attn_rel_bias", "L1_ffn_router_w1", "L1_ffn_router_b1", "L1_ffn_router_w2", "L1_ffn_router_b2",
        "L1_ffn_expert_w1", "L1_ffn_expert_b1", "L1_ffn_expert_w2", "L1_ffn_expert_b2", "L1_ffn_expert_w3",
        "L1_ffn_expert_b3"]


def kernel(**inputs):
    import numpy as _np
    import concourse.bacc as _bacc
    from concourse import mybir as _mybir
    from concourse.bass_utils import run_bass_kernel_spmd as _run

    nc = _bacc.Bacc("TRN2", target_bir_lowering=False, num_devices=1)
    arrays, args = {}, {}
    for name in _INS:
        a = _np.ascontiguousarray(inputs[name])
        arrays[f"in_{name}_dram"] = a
        args[name] = nc.dram_tensor(f"in_{name}_dram", a.shape, _mybir.dt.from_np(a.dtype), kind="ExternalInput").ap()
    nb, s = args["x"].shape
    out = nc.dram_tensor("out_dram", (nb, s, args["L0_tok_head_b"].shape[0]), F32, kind="ExternalOutput").ap()
    build(nc, args, out)
    r = _run(nc, [arrays], core_ids=[0])
    return r.results[0]["out_dram"]
```

```python
from contextlib import ExitStack

import numpy as np

import concourse.bass as bass
from concourse import mybir

F32 = mybir.dt.float32
F16 = mybir.dt.float16
I32 = mybir.dt.int32
U32 = mybir.dt.uint32
ALU = mybir.AluOpType
ACT = mybir.ActivationFunctionType
AX = mybir.AxisListType.X

P = 128
EPS = 1e-5
CLIP = 1e4
WS16 = 256.0
TS16 = 64.0


class Ring:

    def __init__(self, banks, filled, freed):
        self.banks, self.filled, self.freed = banks, filled, freed
        self.at, self.readers = {}, []

    def add(self, key, reader):
        self.at[key] = len(self.readers)
        self.readers.append(reader)

    def bank(self, key):
        return self.banks[self.at[key] % len(self.banks)]

    def number(self, key):
        return self.at[key] + 1

    def wait_free(self, pe, key):
        before = self.at[key] - len(self.banks)
        if before >= 0:
            reader = self.readers[before]
            pe.wait_ge(self.freed[reader], self.readers[:before + 1].count(reader))

    def wait_read(self, eng, key):
        reader = self.readers[self.at[key]]
        eng.wait_ge(self.freed[reader], self.readers[:self.at[key] + 1].count(reader))


def build(nc, a, out):
    NB, S = a["x"].shape
    V, D = a["L0_tok_emb"].shape
    L, _, FF = a["L0_tok_cms_W1"].shape
    FC = FF // P
    W, E = a["L0_ffn_gate_w"].shape
    EF = a["L0_ffn_w1"].shape[2]
    EC = EF // P
    T = NB * S
    NT = T // P
    GT = 4
    NG = NT // GT
    GN = GT * P
    CAP = -(-5 * T // (4 * E))
    SLOTS = E * CAP
    ST = SLOTS // P
    EP = E // 2
    WS = 64
    H1 = 8
    HD = W // H1
    HP = H1 // 2
    X = a["L1_ffn_expert_w1"].shape[0]
    RH = a["L1_ffn_router_w1"].shape[1]
    XP = X // 2
    assert XP == 3 and S == P and D == P and W == 64 and SLOTS % P == 0 and V == 64 and P == 2 * WS

    STEP = [(i, g) for i in range(L) for g in range(NG)]
    NSTEP = len(STEP)
    AT = {lg: n for n, lg in enumerate(STEP)}

    EXTRA = {("zeros", 0): 5.40, ("w1", 1): 0.50, ("w1", 2): 0.90, ("w1", 3): 2.40,
             ("prep", 0): 3.90, ("prep", 1): 4.90, ("prep", 2): 6.30, ("prep", 3): 6.90, ("prep", 4): 7.90, ("prep", 5): 7.20,
             ("xturn", 0): 13.600, ("head", 0): 14.350, ("znorm", 0): 14.500, ("zturn", 0): 15.120, ("score", 0): 15.130, ("context", 0): 15.550,
             ("fnorm", 0): 15.900, ("fturn", 0): 16.280, ("gate", 0): 17.000, ("place", 0): 17.200, ("scatter", 0): 16.950,
             ("xturn", 1): 14.101, ("head", 1): 14.701, ("znorm", 1): 15.151, ("zturn", 1): 15.621, ("score", 1): 15.631, ("context", 1): 16.051,
             ("fnorm", 1): 16.551, ("fturn", 1): 16.781, ("gate", 1): 17.351, ("place", 1): 18.001, ("scatter", 1): 18.201,
             ("xturn", 2): 15.052, ("head", 2): 15.352, ("znorm", 2): 15.652, ("zturn", 2): 16.122, ("score", 2): 16.132, ("context", 2): 16.702,
             ("fnorm", 2): 17.052, ("fturn", 2): 17.882, ("gate", 2): 18.002, ("place", 2): 18.502, ("scatter", 2): 18.402,
             ("xturn", 3): 15.903, ("head", 3): 16.353, ("znorm", 3): 16.653, ("zturn", 3): 17.123, ("score", 3): 17.133, ("context", 3): 17.553,
             ("fnorm", 3): 18.053, ("fturn", 3): 19.033, ("gate", 3): 20.353, ("place", 3): 20.703, ("scatter", 3): 20.603}
    order = {("w1", 0): -4.60, ("up", 0): -1.60, ("turn", 0): -3.80, ("turn", 1): -0.50, ("norm", 0): -4.65,
            ("tokens", 0): -5.00, ("tokens", 1): -4.95, ("memory", 0): -4.90, ("embed", 0): -4.70, ("stream", 0): -4.69,
            ("tokens", 2): -4.59, ("memory", 1): -4.77, ("embed", 1): -4.20, ("stream", 1): -2.90, ("norm", 1): -2.90,
            ("tokens", 3): -3.09, ("memory", 2): -3.08, ("embed", 2): -1.00, ("stream", 2): -0.90, ("norm", 2): -0.80,
            ("memory", 3): -1.08, ("embed", 3): -0.40, ("stream", 3): 0.00, ("norm", 3): 0.10}
    NORM, TURN = 0.85, 0.40
    for n in range(NSTEP):
        if n >= 1:
            order["up", n] = n - 0.9
        order["down", n] = n + 0.5
        if n >= NG:
            order["norm", n] = n - NG + 0.5 + NORM
        if n >= 2:
            order["turn", n] = n - 2 + TURN
    order.update(EXTRA)
    PLAN = sorted(order, key=order.get)

    TILE_LAGS = {"scores": -0.10, "weights": 1.40, "turned": 3.30, "applied": 4.50}
    GROUP_LAGS = {"returned": -10.10, "anorm": -4.25, "turn_a1": -1.70, "qkv": -0.90, "values": -0.85, "turn_o": 8.80, "project": 9.10, "xnorm": 9.65, "rows": 10.30, "router": 10.50, "logits": 11.80, "choice": 12.40, "shares": 12.80}
    FIRST, FIRST_STEP, SECOND, SECOND_STEP, THIRD, THIRD_STEP = 11.21, 0.20, 11.90, 0.40, 13.30, 0.40
    GATHER = [-21.00, -20.90, -6.20, -4.30]
    RETURNED_1, NORMED_1, TURNED_1 = -5.70, -2.30, 0.20
    order2 = {("gather", g): GATHER[g] for g in range(NG)}
    for t in range(NT):
        for what, lag in TILE_LAGS.items():
            order2[what, t] = t + lag
    for g in range(NG):
        for what, lag in GROUP_LAGS.items():
            order2[what, g] = g * GT + lag
        for q in range(XP):
            order2["first", (g, q)] = g * GT + FIRST + q * FIRST_STEP
            order2["second", (g, q)] = g * GT + SECOND + q * SECOND_STEP
        for j in range(GT):
            order2["third", (g, j)] = g * GT + THIRD + j * THIRD_STEP
    order2["returned", 1], order2["anorm", 1], order2["turn_a1", 1] = RETURNED_1, NORMED_1, TURNED_1
    PLAN2 = sorted(order2, key=order2.get)

    RW = 2 * W
    xbuf = nc.dram_tensor("expert_rows", (SLOTS + T, RW), F16, kind="Internal").ap()
    ybuf = nc.dram_tensor("expert_outputs", (SLOTS, W), F32, kind="Internal").ap()

    with ExitStack() as ctx:
        def sb(name, shape, dt=F32):
            return ctx.enter_context(nc.sbuf_tensor(name, shape, dt))

        def sem(name):
            return ctx.enter_context(nc.semaphore(name))

        ident = sb("ident", [P, P])
        ident16 = sb("ident16", [P, P], F16)
        tri = sb("tri", [P, P], F16)
        ones16 = sb("ones16", [P, P], F16)
        iota_v = sb("iota_v", [P, 1], I32)
        iota_vf = sb("iota_vf", [P, 1])
        neg_v = sb("neg_v", [P, 1])
        not_zero = sb("not_zero", [V, 1])
        rank8 = sb("rank8", [P, E])
        rank6 = sb("rank6", [P, X])
        rank_i = sb("rank_i", [P, E], I32)
        trash_i = sb("trash_i", [P, NT], I32)
        trash = sb("trash", [P, NT])
        headmask = sb("headmask", [P, H1])
        flip = sb("flip", [WS, 2, WS])
        relb_up = sb("relb_up", [WS, WS])
        relb = sb("relb", [P, WS])
        emb = sb("emb", [V, D])
        embf = sb("embf", [V, D])
        embT = sb("embT", [D, V])
        w_upd = sb("w_upd", [D, D])
        w_f = sb("w_f", [D, D])
        b_upd = sb("b_upd", [V, D])
        b_f = sb("b_f", [V, D])
        table0 = sb("table0", [V, D])
        table1 = sb("table1", [V, D])
        table = sb("table", [2 * V, D], F16)
        etable = sb("etable", [2 * V, D], F16)
        decay_in = sb("decay_in", [P, 1])
        decay = sb("decay", [P, 4])
        norm_g = sb("norm_g", [P, D])
        norm_b = sb("norm_b", [P, D])
        R_B1 = 2 * L
        R_X2 = R_B1 + L * FC
        R_X1 = R_X2 + XP
        R_E1 = R_X1 + XP
        NR = R_E1 + E * EC
        rows = sb("rows", [NR, P])
        cols = sb("cols", [P, NR])
        e_b1s = sb("e_b1s", [P, E * EC])
        r_b1 = sb("r_b1", [RH, 1])
        w1 = sb("w1", [D, L, FF])
        w1p = sb("w1p", [D, 2, L, FF], F16)
        w2 = sb("w2", [P, L, FC, D])
        b2 = sb("b2", [P, L, D])
        head_w = sb("head_w", [D, W])
        head_b = sb("head_b", [P, W])
        gate_b = sb("gate_b", [P, E])
        r_b2 = sb("r_b2", [P, X])
        e_w2 = sb("e_w2", [P, E, EC, W])
        e_b2 = sb("e_b2", [P, E, W])
        qkv_rows = sb("qkv_rows", [P, 2, W])
        proj_rows = sb("proj_rows", [W, W])
        x_w2 = sb("x_w2", [P, XP, P])
        x_w3 = sb("x_w3", [P, XP, P])
        C_E = E
        C_Q = C_E + E * EF
        C_P = C_Q + 3 * W
        C_R = C_P + W
        C_X = C_R + RH
        C_N = C_X + X * W
        wst = sb("wst", [P, C_N])
        wp = sb("wp", [P, 2, C_N], F16)
        r_w2 = sb("r_w2", [2 * RH, X])
        r_w2p = sb("r_w2p", [2 * RH, 2, X], F16)
        BR = 33
        BN = W + X * W
        bias_rows = sb("bias_rows", [BR, BN])
        bias_hi = sb("bias_hi", [BR, BN], F16)
        bias_p = sb("bias_p", [BR, BN], F16)

        onehot = sb("onehot", [2 * V, T], F16)
        scan_io = sb("scan_io", [P, 2, T])
        keep_mem = scan_io[:, 0, :]
        mems = scan_io[:, 1, :]
        ln_t = sb("ln_t", [P, 2, GT, D])
        stream = sb("stream", [P, 2, NT, D])
        x = stream[:, 0, :, :]
        xb = stream[:, 1, :, :]
        hn = sb("hn", [P, NG, GN])
        hT = sb("hT", [P, 2, GN])
        hp = sb("hp", [P, 2, 2, GN], F16)
        gT = sb("gT", [P, 2, FC, GN])
        assert T <= FC * GN
        tokens = gT[0:1, 0, :, :].rearrange("p c n -> p (c n)")[:, 0:T].bitcast(I32)
        tokens16 = gT[0:1, 1, :, :].rearrange("p c n -> p (c n)")[:, 0:T // 2].bitcast(F16)
        LB = 4
        st = sb("st", [P, LB, GT, 6])
        mv = sb("mv", [P, LB, GT, 2])
        ve = sb("ve", [P, LB, GT])
        rstd = sb("rstd", [P, LB, GT])
        one = sb("one", [P, 1])
        neg_half = sb("neg_half", [P, GT])
        h = sb("h", [P, NT, W])
        ZB = 4
        z0 = sb("z0", [P, NT, W + 1])
        z0T = sb("z0T", [W, 2, GN])
        zf = sb("zf", [P, 2, GT, W])
        zs = sb("zs", [P, NT, RW], F16)
        zT = sb("zT", [P, ZB, GN], F16)
        ex = sb("ex", [P, 2, GN])
        rs = sb("rs", [P, 2, GT])
        glog = sb("glog", [P, NT, E])
        gm = sb("gm", [P, NT])
        gd = sb("gd", [P, NT, E])
        gv = sb("gv", [P, NT, E])
        gbest = sb("gbest", [P, NT])
        goh = sb("goh", [P, NT, E], F16)
        gex = sb("gex", [P, NT, E])
        gsum = sb("gsum", [P, NT])
        prob = sb("prob", [P, NT])
        pc = sb("pc", [P, NT, E])
        pos1 = sb("pos1", [P, NT])
        kept = sb("kept", [P, NT])
        base = sb("base", [P, NT])
        slot = sb("slot", [P, NT])
        slot2 = sb("slot2", [P, NT])
        idx_s = sb("idx_s", [P, NT], I32)
        idx_g = sb("idx_g", [P, NT], I32)
        pk = sb("pk", [P, NT])
        w1_flat = w1[:, :, :].rearrange("p l f -> p (l f)")
        stream_flat = stream[:, :, :, :].rearrange("p a t d -> p (a t d)")
        w1p_flat = w1p[:, :, :, :].rearrange("p a l f -> p (a l f)").bitcast(F32)
        w2_flat = w2[:, :, :, :].rearrange("p l c d -> p (l c d)")
        hn_flat = hn[:, :, :].rearrange("p g n -> p (g n)")
        xe = w1_flat[:, 0:ST * RW // 2].bitcast(F16).rearrange("p (t w) -> p t w", t=ST)
        xeT = stream[:, 0, :, :].rearrange("p t d -> p (t d)")[:, 0:ST * P // 2].bitcast(F16)
        hm = sb("hm", [P, 2, EC, CAP])
        ye = w1p_flat[:, 0:ST * W].rearrange("p (t w) -> p t w", t=ST)
        yg = sb("yg", [P, NT, W])
        zeros = yg[:, :, :].rearrange("p t w -> p (t w)")[:, 0:ST * RW // 4]
        yp = sb("yp", [P, GT, W])
        ya = sb("ya", [P, GT, W])
        yc = sb("yc", [P, GT, W])
        yn = sb("yn", [P, GT, W])
        yfin = sb("yfin", [P, GT, W], U32)
        km = gT[:, :, :, :].rearrange("p b t (h k) -> p b t h k", h=H1)
        qbd = sb("qbd", [P, 2, GT, P])
        VW = 2 * (HD + 1)
        vf = onehot[:, :].bitcast(F32).rearrange("p (b n) -> p b n", b=2)
        vz = sb("vz", [P, 2, 2, GT * 2, HP, VW], F16)
        sm = hn_flat[:, 0:2 * H1 * WS].rearrange("p (b h k) -> p b h k", b=2, h=H1)
        smx = sb("smx", [P, 2, H1])
        sd = hn_flat[:, 2 * H1 * WS:4 * H1 * WS].rearrange("p (b h k) -> p b h k", b=2, h=H1)
        pf = w1_flat[:, 0:2 * H1 * WS].rearrange("p (b n) -> p b n", b=2)
        pp = w1_flat[:, 2 * H1 * WS:4 * H1 * WS].bitcast(F16).rearrange("p (b i n) -> p b i n", b=2, i=2)
        pT = w1p_flat[:, 0:HP * 2 * P].bitcast(F16).rearrange("p (b i h q) -> p b i h q", b=2, i=2, h=HP)
        rden = sb("rden", [P, 2, H1])
        o = w1p_flat[:, HP * 2 * P:HP * 2 * P + 2 * GT * W].rearrange("p (b t w) -> p b t w", b=2, t=GT)
        rhf = w2_flat[0:RH, NT * W:NT * W + 2 * GN].rearrange("p (b n) -> p b n", b=2)
        rhp = stream_flat[0:2 * RH, 2 * XP * GN:2 * XP * GN + GN].bitcast(F16).rearrange("p (b n) -> p b n", b=2)
        tl = sb("tl", [P, GT, X])
        tm = sb("tm", [P, GT])
        td = sb("td", [P, GT, X])
        te = sb("te", [P, GT, X])
        tsum = sb("tsum", [P, GT])
        trs = sb("trs", [P, GT])
        tp = sb("tp", [P, GT, X])
        shares = sb("shares", [P, 2, 2, X, W])
        share3 = sb("share3", [P, 2, XP, W])
        share1 = sb("share1", [P, 2, W])
        chosen = sb("chosen", [P, GT, W])
        m2 = sb("m2", [P, GT])
        teq = sb("teq", [P, GT, X])
        tv = sb("tv", [P, GT, X])
        tb = sb("tb", [P, GT])
        o1 = sb("o1", [P, GT, X])
        o2 = sb("o2", [P, GT, X])
        tdl = sb("tdl", [P, GT])
        tex = sb("tex", [P, GT])
        tw0 = sb("tw0", [P, GT])
        tw1 = sb("tw1", [P, GT])
        tw2 = sb("tw2", [P, GT])
        route = sb("route", [P, NT, X])
        h1T = scan_io[:, :, :].rearrange("p a n -> p (a n)")[:, 0:2 * XP * GN].rearrange("p (b q n) -> p b q n", b=2, q=XP)
        h2T = stream_flat[:, 0:2 * XP * GN].rearrange("p (b q n) -> p b q n", b=2, q=XP)
        res = w2_flat[:, 0:NT * W].rearrange("p (t w) -> p t w", t=NT)

        banks = [ctx.enter_context(nc.psum_tensor(f"bank{i}", [P, 512], F32)) for i in range(8)]
        wide = Ring(banks[0:4], sem("wide_filled"), {"act": sem("wide_freed_act"), "dve": sem("wide_freed_dve")})
        turn = Ring(banks[4:6], sem("turn_filled"), {"act": sem("turn_freed_act")})
        outp = Ring(banks[6:8], sem("outp_filled"), {"act": sem("outp_freed_act"), "dve": sem("outp_freed_dve")})

        turn.add("emb", "act")
        turn.add("rows", "act")
        outp.add("table", "dve")
        for what, n in PLAN:
            if what == "tokens":
                wide.add(("tok", n), "act")
            if what == "memory":
                wide.add(("u", n), "dve")
            if what == "embed":
                outp.add(("y", n), "dve")
            if what == "turn":
                turn.add(("hT", n), "act")
            if what == "up":
                for c in range(FC):
                    wide.add(("h", n, c), "act")
            if what == "down":
                outp.add(("o", n), "dve")
            if what == "prep" and n == 4:
                turn.add("qkv_w", "act")
                turn.add("proj_w", "act")
                outp.add("relb", "act")
            if what == "xturn":
                turn.add(("xT", n), "act")
            if what == "zturn":
                turn.add(("a0", n), "act")
            if what == "fturn":
                turn.add(("f0", n), "act")
            if what == "head":
                outp.add(("head", n), "dve")
            if what == "score":
                wide.add(("s0", n), "act")
            if what == "context":
                outp.add(("ctx", n), "dve")
            if what == "gate":
                outp.add(("gate", n), "dve")
            if what == "place":
                outp.add(("pos", n), "dve")
        XG = ST // 4

        def slots_end(e):
            return min(XG, -(-(e + 1) * CAP // GN))

        for k in range(XG):
            turn.add(("xe", k), "act")
        for e in range(E + 1):
            if e < E:
                wide.add(("em", e, 0), "act")
                wide.add(("em", e, 1), "dve")
            if e >= 1:
                outp.add(("ey", e - 1), "dve")

        for what, n in PLAN2:
            if what == "turn_a1":
                turn.add(("a1", n), "act")
            if what == "qkv":
                wide.add(("k", n), "act")
                wide.add(("q", n), "act")
            if what == "values":
                outp.add(("v", n), "act")
            if what == "scores":
                wide.add(("s1", n), "dve")
            if what == "turned":
                turn.add(("pT", n), "act")
            if what == "applied":
                outp.add(("av", n), "dve")
            if what == "turn_o":
                turn.add(("oT", n), "act")
            if what == "project":
                outp.add(("proj", n), "dve")
            if what == "rows":
                turn.add(("f1", n), "act")
            if what == "router":
                wide.add(("rh", n), "act")
            if what == "first":
                wide.add(("h1", *n), "act")
            if what == "logits":
                outp.add(("rl", n), "dve")
            if what == "second":
                wide.add(("h2", *n), "act" if n[1] < 2 else "dve")
            if what == "third":
                wide.add(("eo", *n), "dve")

        LNS, NEXT, HT, ZT = [], [], [], []
        NORMS = [n for what, n in PLAN if what == "norm"]
        for what, n in PLAN:
            if what == "embed":
                LNS.append(("y", n))
            if what == "stream":
                LNS.append(("c", AT[0, n]))
                NEXT.append(AT[0, n])
            if what == "turn":
                HT.append(("hT", n))
            if what == "down" and STEP[n][0] + 1 < L:
                NEXT.append(AT[STEP[n][0] + 1, STEP[n][1]])
                LNS.append(("c", NEXT[-1]))
            if what == "xturn":
                HT.append(("xT", n))
            if what == "head":
                LNS.append(("a0", n))
            if what == "context":
                LNS.append(("f0", n))
            if what == "fturn":
                ZT.append(("f0", n))
        for what, n in PLAN2:
            if what == "returned":
                LNS.append(("a1", n))
            if what == "turn_a1":
                ZT.append(("a1", n))
            if what == "turn_o":
                ZT.append(("oT", n))
            if what == "project":
                LNS.append(("f1", n))
            if what == "rows":
                ZT.append(("f1", n))
        def last_of_a1(g):
            return (outp, ("v", g)) if PLAN2.index(("values", g)) > PLAN2.index(("qkv", g)) else (wide, ("q", g))

        ZT_LAST = {"f0": lambda g: (outp, ("gate", g)), "a1": last_of_a1,
                   "oT": lambda g: (outp, ("proj", g)), "f1": lambda g: (wide, ("h1", g, XP - 1))}
        ZS = [("f0", n) for what, n in PLAN if what == "fnorm"]
        for what, n in PLAN2:
            if what == "anorm":
                ZS.append(("a1", n))
            if what == "applied" and n % GT == GT - 1:
                ZS.append(("oT", n // GT))
            if what == "xnorm":
                ZS.append(("f1", n))

        in_emb, in_tok, in_rows, in_wf, in_norm = map(sem, ["in_emb", "in_tok", "in_rows", "in_wf", "in_norm"])
        in_w1 = [sem(f"in_w1_{i}") for i in range(L)]
        in_w2 = [sem(f"in_w2_{i}") for i in range(L)]
        in_b2, in_head, in_gate, in_exp, in_att, in_x1, in_xbd = map(
            sem, ["in_b2", "in_head", "in_gate", "in_exp", "in_att", "in_x1", "in_xbd"])
        zero_rows, scattered, ye_out, stored = map(sem, ["zero_rows", "scattered", "ye_out", "stored"])
        rows_back = [sem(f"rows_back_{k}") for k in range(XG)]
        gathered = [sem(f"gathered_{g}") for g in range(NG)]
        pool_step, ident_ready, const_ready, zeros_ready, xb_ready, rstd_ready, sd_ready, plo_ready, vlo_ready, parts_ready = map(
            sem, ["pool_step", "ident_ready", "const_ready", "zeros_ready", "xb_ready", "rstd_ready", "sd_ready",
                  "plo_ready", "vlo_ready", "parts_ready"])
        dve_step, neg_ready, decay_ready, stats_ready, table_ready, etable_ready, hot_ready, w1_ready, x_ready, hn_ready, hp_ready, prep_ready = map(
            sem, ["dve_step", "neg_ready", "decay_ready", "stats_ready", "table_ready", "etable_ready", "hot_ready", "w1_ready", "x_ready",
                  "hn_ready", "hp_ready", "prep_ready"])
        z0_ready, zs_ready, goh_ready, gd_ready, idx_ready, ye_ready, smx_ready = map(
            sem, ["z0_ready", "zs_ready", "goh_ready", "gd_ready", "idx_ready", "ye_ready", "smx_ready"])
        td_ready, tdl_ready, route_ready, rlo_ready, res_ready, shares_used, last_ready = map(
            sem, ["td_ready", "tdl_ready", "route_ready", "rlo_ready", "res_ready", "shares_used", "last_ready"])
        act_step, keep_ready, hi_ready, tok16_ready, decay_exp, gex_ready, vf_ready, pexp_ready, te_ready, tex_ready = map(
            sem, ["act_step", "keep_ready", "hi_ready", "tok16_ready", "decay_exp", "gex_ready", "vf_ready",
                  "pexp_ready", "te_ready", "tex_ready"])

        def bc(ap, n):
            return ap.unsqueeze(2).broadcast_to([ap.shape[0], ap.shape[1], n])

        def bm(ap, n):
            return ap.unsqueeze(1).broadcast_to([ap.shape[0], n, ap.shape[1]])

        def over_partitions(ap, n=P):
            return bass.AP(ap.tensor, ap.offset, [[0, n]] + [list(d) for d in ap.ap])

        def row(ap):
            return ap.unsqueeze(0)

        def group(g):
            return slice(g * GT, (g + 1) * GT)

        block = ctx.enter_context(nc.Block())

        @block.sync
        def _(sp):
            sp.dma_start(tokens, row(a["x"].rearrange("b s -> (b s)"))).then_inc(in_tok, 16)
            sp.dma_start(emb[:, :], a["L0_tok_emb"]).then_inc(in_emb, 16)
            sp.dma_start(w_upd[:, :], a["L0_tok_W_upd"]).then_inc(in_emb, 16)
            sp.dma_start(b_upd[:, :], over_partitions(a["L0_tok_b_upd"], V)).then_inc(in_emb, 16)
            sp.dma_start(b_f[:, :], over_partitions(a["L0_tok_b_f"], V)).then_inc(in_emb, 16)
            sp.dma_start(w_f[:, :], a["L0_tok_W_f"]).then_inc(in_wf, 16)
            sp.dma_start(norm_g[:, :], over_partitions(a["L0_tok_norm_g"])).then_inc(in_norm, 16)
            sp.dma_start(norm_b[:, :], over_partitions(a["L0_tok_norm_b"])).then_inc(in_norm, 16)
            sp.dma_start(rows[0:L, :], a["L0_tok_cms_ln_g"]).then_inc(in_rows, 16)
            sp.dma_start(rows[L:2 * L, :], a["L0_tok_cms_ln_b"]).then_inc(in_rows, 16)
            sp.dma_start(rows[R_B1:R_X2, :], a["L0_tok_cms_b1"].rearrange("l (c p) -> (l c) p", p=P)).then_inc(in_rows, 16)
            sp.dma_start(rows[R_X2:R_X1, :], a["L1_ffn_expert_b2"].rearrange("(q i) f -> q (i f)", i=2)).then_inc(in_rows, 16)
            sp.dma_start(rows[R_X1:R_E1, :], a["L1_ffn_expert_b1"].rearrange("(q i) f -> q (i f)", i=2)).then_inc(in_rows, 16)
            sp.dma_start(rows[R_E1:NR, :], a["L0_ffn_b1"].rearrange("e (c p) -> (e c) p", p=P)).then_inc(in_rows, 16)
            sp.dma_start(r_b1[:, :], a["L1_ffn_router_b1"].unsqueeze(1)).then_inc(in_rows, 16)
            sp.dma_start(w1[:, 0, :], a["L0_tok_cms_W1"][0]).then_inc(in_w1[0], 16)
            sp.dma_start(w2[:, 0, :, :], a["L0_tok_cms_W2"][0].rearrange("(c p) d -> p c d", p=P)).then_inc(in_w2[0], 16)
            sp.dma_start(b2[:, :, :], over_partitions(a["L0_tok_cms_b2"])).then_inc(in_b2, 16)
            for i in range(1, L):
                sp.dma_start(w1[:, i, :], a["L0_tok_cms_W1"][i]).then_inc(in_w1[i], 16)
                sp.dma_start(w2[:, i, :, :], a["L0_tok_cms_W2"][i].rearrange("(c p) d -> p c d", p=P)).then_inc(in_w2[i], 16)
            sp.dma_start(head_w[:, :], a["L0_tok_head_W"]).then_inc(in_head, 16)
            sp.dma_start(head_b[:, :], over_partitions(a["L0_tok_head_b"])).then_inc(in_head, 16)
            sp.dma_start(gate_b[:, :], over_partitions(a["L0_ffn_gate_b"])).then_inc(in_gate, 16)
            sp.dma_start(r_b2[:, :], over_partitions(a["L1_ffn_router_b2"])).then_inc(in_gate, 16)
            sp.dma_start(qkv_rows[:, 0, :], a["L1_attn_w_qkv"][0:P, :]).then_inc(in_att, 16)
            sp.dma_start(qkv_rows[0:W, 1, :], a["L1_attn_w_qkv"][P:3 * W, :]).then_inc(in_att, 16)
            sp.dma_start(proj_rows[:, :], a["L1_attn_w_proj"]).then_inc(in_att, 16)
            rb = a["L1_attn_rel_bias"]
            sp.dma_start(relb_up[:, :], bass.AP(rb.tensor, rb.offset, [[1, WS], [1, WS]])).then_inc(in_att, 16)
            for i in range(2):
                half = slice(i * W, (i + 1) * W)
                sp.dma_start(wst[half, 0:C_E], a["L0_ffn_gate_w"]).then_inc(in_exp, 16)
                sp.dma_start(wst[half, C_E:C_Q].rearrange("d (e f) -> d e f", e=E), a["L0_ffn_w1"].rearrange("e d f -> d e f")).then_inc(in_exp, 16)
                sp.dma_start(wst[half, C_R:C_X], a["L1_ffn_router_w1"]).then_inc(in_x1, 16)
                sp.dma_start(wst[half, C_X:C_N].rearrange("d (e f) -> d e f", e=X), a["L1_ffn_expert_w1"].rearrange("e d f -> d e f")).then_inc(in_x1, 16)
                sp.dma_start(r_w2[i * RH:(i + 1) * RH, :], a["L1_ffn_router_w2"]).then_inc(in_x1, 16)
                sp.dma_start(bias_rows[32 * i:32 * i + 1, 0:W], row(a["L1_attn_b_proj"])).then_inc(in_x1, 16)
                sp.dma_start(bias_rows[32 * i:32 * i + 1, W:BN], row(a["L1_ffn_expert_b3"].rearrange("e w -> (e w)"))).then_inc(in_x1, 16)
            for e in range(E):
                sp.dma_start(e_w2[:, e, :, :], a["L0_ffn_w2"][e].rearrange("(c p) w -> p c w", p=P)).then_inc(in_exp, 16)
            sp.dma_start(e_b2[:, :, :], over_partitions(a["L0_ffn_b2"])).then_inc(in_exp, 16)
            sp.wait_ge(parts_ready, 3)
            for i in range(2):
                part = slice(i * W, (i + 1) * W)
                sp.dma_start(x_w2[part, :, part], a["L1_ffn_expert_w2"].rearrange("(q i) f g -> i f q g", i=2)[i]).then_inc(in_xbd, 16)
                sp.dma_start(x_w3[part, :, part], a["L1_ffn_expert_w3"].rearrange("(q i) f g -> i f q g", i=2)[i]).then_inc(in_xbd, 16)
            sp.wait_ge(scattered, 16 * NT)
            xr = xbuf[0:SLOTS, :].rearrange("(t p) w -> p t w", p=P)
            for k in range(XG):
                sp.dma_start(xe[:, 4 * k:4 * k + 4, :], xr[:, 4 * k:4 * k + 4, :]).then_inc(rows_back[k], 16)
            yr = ybuf.rearrange("(t p) w -> p t w", p=P)
            for k in range(EP):
                pair_tiles = slice(k * ST // EP, (k + 1) * ST // EP)
                sp.wait_ge(ye_ready, 2 * k + 2)
                sp.dma_start(yr[:, pair_tiles, :], ye[:, pair_tiles, :]).then_inc(ye_out, 16)
            for g in range(NG):
                if g < NG - 1:
                    sp.wait_ge(res_ready, g + 1)
                else:
                    sp.wait_ge(last_ready, 1)
                sp.dma_start(out.rearrange("b s w -> s b w")[:, group(g), :], res[:, group(g), :]).then_inc(stored, 16)
            sp.wait_ge(stored, 16 * NG)

        @block.gpsimd
        def _(pool):
            steps = [0]

            def link(ins):
                steps[0] += 1
                ins.then_inc(pool_step, 1)
                pool.wait_ge(pool_step, steps[0])

            def signal(ins, s, value):
                ins.then_inc(s, 1)
                pool.wait_ge(s, value)

            link(nc.gpsimd.memset(ident[:, :], 0.0))
            signal(nc.gpsimd.affine_select(out=ident[:, :], in_=ident[:, :], compare_op=ALU.not_equal, fill=1.0, base=0,
                                           pattern=[[-1, P]], channel_multiplier=1), ident_ready, 1)
            for i in range(2):
                link(nc.gpsimd.iota(iota_v[i * V:(i + 1) * V, :], pattern=[[0, 1]], base=0, channel_multiplier=1))
            signal(nc.gpsimd.memset(ones16[:, :], 1.0), const_ready, 1)
            signal(nc.gpsimd.memset(neg_half[:, :], -0.5), const_ready, 2)
            signal(nc.gpsimd.memset(one[:, :], 1.0), const_ready, 3)
            signal(nc.gpsimd.memset(keep_mem.rearrange("p (t s) -> p t s", s=P)[:, :, 0:1], 0.0), const_ready, 4)
            signal(nc.gpsimd.memset(zeros, 0.0), zeros_ready, 1)

            def more_constants():
                link(nc.gpsimd.tensor_copy(ident16[:, :], ident[:, :]))
                link(nc.gpsimd.memset(tri[:, :], 1.0))
                link(nc.gpsimd.affine_select(out=tri[:, :], in_=tri[:, :], compare_op=ALU.is_ge, fill=0.0, base=0,
                                             pattern=[[1, P]], channel_multiplier=-1))
                link(nc.gpsimd.iota(rank_i[:, :], pattern=[[-1, E]], base=E, channel_multiplier=0))
                link(nc.gpsimd.iota(trash_i[:, :], pattern=[[P, NT]], base=SLOTS, channel_multiplier=1))
                link(nc.gpsimd.memset(flip[:, :, :], 0.0))
                link(nc.gpsimd.affine_select(out=flip[:, :, :], in_=flip[:, :, :], compare_op=ALU.not_equal, fill=1.0, base=1 - WS,
                                             pattern=[[0, 2], [1, WS]], channel_multiplier=1))
                link(nc.gpsimd.memset(headmask[:, :], 1.0 / WS16))
                for w in range(2):
                    part = headmask[w * W:(w + 1) * W, :]
                    link(nc.gpsimd.affine_select(out=part, in_=part, compare_op=ALU.is_ge, fill=0.0, base=0,
                                                 pattern=[[-HD, H1]], channel_multiplier=1))
                    link(nc.gpsimd.affine_select(out=part, in_=part, compare_op=ALU.is_ge, fill=0.0, base=HD - 1,
                                                 pattern=[[HD, H1]], channel_multiplier=-1))
                link(nc.gpsimd.memset(z0[:, :, W], 1.0))
                signal(nc.gpsimd.memset(bias_p[:, :], 0.0), parts_ready, 1)
                link(nc.gpsimd.memset(x_w2[:, :, :], 0.0))
                signal(nc.gpsimd.memset(x_w3[:, :, :], 0.0), parts_ready, 2)
                signal(nc.gpsimd.memset(qbd[:, :, :, :], 0.0), parts_ready, 3)
                link(nc.gpsimd.memset(vz[:, :, :, :, :, :], 0.0))
                link(nc.gpsimd.memset(vz[0:WS, :, 0, :, :, HD], 1.0))
                signal(nc.gpsimd.memset(vz[WS:P, :, 0, :, :, VW - 1], 1.0), parts_ready, 4)

            def ln_root(key):
                k = LNS.index(key)
                pool.wait_ge(stats_ready, k + 1)
                eps = EPS * TS16 * TS16 if key[0] == "y" else EPS
                link(nc.gpsimd.tensor_scalar_add(ve[:, k % LB, :], mv[:, k % LB, :, 1], eps))
                signal(nc.gpsimd.tensor_tensor(rstd[:, k % LB, :], ve[:, k % LB, :], neg_half[:, :], ALU.pow), rstd_ready, k + 1)

            def add_b2(n):
                i, g = STEP[n]
                k = NEXT.index(n)
                pool.wait_ge(x_ready, k + 1)
                signal(nc.gpsimd.tensor_tensor(xb[:, group(g), :], x[:, group(g), :], bm(b2[:, i, :], GT), ALU.add), xb_ready, k + 1)

            more_constants()
            pool.wait_ge(in_b2, 16)
            for what, n in PLAN:
                if what == "embed":
                    ln_root(("y", n))
                if what == "stream":
                    ln_root(("c", AT[0, n]))
                    add_b2(AT[0, n])
                if what == "down" and STEP[n][0] + 1 < L:
                    m = AT[STEP[n][0] + 1, STEP[n][1]]
                    ln_root(("c", m))
                    add_b2(m)
                if what == "head":
                    ln_root(("a0", n))
                if what == "context":
                    ln_root(("f0", n))
                if what == "zeros":
                    halves = xbuf[0:SLOTS, :].rearrange("(i p k) w -> i p (k w)", i=2, p=P)
                    for i in range(2):
                        nc.gpsimd.dma_start(halves[i], zeros.bitcast(F16)).then_inc(zero_rows, 16)
                if what == "scatter":
                    pool.wait_ge(zero_rows, 32)
                    pool.wait_ge(idx_ready, n + 1)
                    for t in range(n * GT, (n + 1) * GT):
                        nc.gpsimd.indirect_dma_start(out=xbuf[:, :], out_offset=bass.IndirectOffsetOnAxis(ap=idx_s[:, t:t + 1], axis=0),
                                                     in_=zs[:, t, :], in_offset=None).then_inc(scattered, 16)

            def gather(g):
                pool.wait_ge(ye_out, 16 * EP)
                for t in range(g * GT, (g + 1) * GT):
                    nc.gpsimd.indirect_dma_start(out=yg[:, t, :], out_offset=None, in_=ybuf[:, :],
                                                 in_offset=bass.IndirectOffsetOnAxis(ap=idx_g[:, t:t + 1], axis=0)).then_inc(gathered[g], 16)

            def low_values(g):
                for k in range(NG):
                    if PLAN2.index(("gather", k)) < PLAN2.index(("values", g)):
                        pool.wait_ge(gathered[k], 16 * GT)
                pool.wait_ge(vf_ready, g + 1)
                v5 = vf[:, g % 2, :].rearrange("p (t h i d) -> p t h i d", t=2 * GT, h=HP, i=2)
                for i in range(2):
                    part = slice(i * WS, (i + 1) * WS)
                    at = slice(i * (HD + 1), i * (HD + 1) + HD)
                    signal(nc.gpsimd.tensor_tensor(vz[part, g % 2, 1, :, :, at], v5[part, :, :, i, :], vz[part, g % 2, 0, :, :, at], ALU.subtract),
                           vlo_ready, 2 * g + i + 1)

            def sub_max(t):
                pool.wait_ge(smx_ready, t + 1)
                if t >= 2:
                    pool.wait_ge(pexp_ready, t - 1)
                signal(nc.gpsimd.tensor_tensor(sd[:, t % 2, :, :], sm[:, t % 2, :, :], bc(smx[:, t % 2, :], WS), ALU.subtract), sd_ready, t + 1)

            def low_weights(t):
                pool.wait_ge(pexp_ready, t + 1)
                if t >= 2:
                    pool.wait_ge(turn.filled, turn.number(("pT", t - 2)))
                signal(nc.gpsimd.tensor_tensor(pp[:, t % 2, 1, :], pf[:, t % 2, :], pp[:, t % 2, 0, :], ALU.subtract), plo_ready, t + 1)

            for what, n in PLAN2:
                if what == "gather":
                    gather(n)
                if what == "returned":
                    ln_root(("a1", n))
                if what == "values":
                    low_values(n)
                if what == "scores":
                    sub_max(n)
                if what == "weights":
                    low_weights(n)
                if what == "project":
                    ln_root(("f1", n))
                if what == "third" and n[1] % 2 == 1 and n[0] < NG - 1:
                    g, j = n
                    wide.wait_read(pool, ("eo", g, j))
                    s6 = shares[:, j // 2, :, :, :]
                    signal(nc.gpsimd.tensor_tensor(share3[:, :, :, :], s6[:, :, 0:XP, :], s6[:, :, XP:X, :], ALU.add), shares_used, 2 * g + j // 2 + 1)
                    link(nc.gpsimd.tensor_tensor(share1[:, :, :], share3[:, :, 0, :], share3[:, :, 1, :], ALU.add))
                    link(nc.gpsimd.tensor_tensor(chosen[:, j - 1:j + 1, :], share1[:, :, :], share3[:, :, 2, :], ALU.add))
                    if j == GT - 1:
                        signal(nc.gpsimd.tensor_tensor(res[:, group(g), :], chosen[:, :, :], h[:, group(g), :], ALU.add), res_ready, g + 1)

        @block.scalar
        def _(act):
            steps = [0]

            def link(ins):
                steps[0] += 1
                ins.then_inc(act_step, 1)
                act.wait_ge(act_step, steps[0])

            def copy(dst, src, scale=1.0):
                return nc.scalar.activation(dst, src, ACT.Copy, scale=scale)

            def load(dst, src, loaded):
                nc.scalar.dma_start(dst, src).then_inc(loaded, 16)

            load(decay_in[:, :], over_partitions(a["L0_tok_decay_param"]), in_wf)
            act.wait_ge(in_tok, 16)
            for g in range(NG):
                c = slice(g * GN, (g + 1) * GN)
                copy(tokens16[:, c], tokens[:, c]).then_inc(tok16_ready, 1)
                if g == 0:
                    act.wait_ge(turn.filled, turn.number("emb"))
                    copy(embT[:, :], turn.bank("emb")[:, 0:V]).then_inc(turn.freed["act"], 1)
                    act.wait_ge(in_wf, 32)
                    nc.scalar.activation(decay[:, 0:1], decay_in[:, :], ACT.Exp, scale=-1.0).then_inc(decay_exp, 1)
            act.wait_ge(const_ready, 3)
            act.wait_ge(neg_ready, 1)

            def keep(g):
                act.wait_ge(wide.filled, wide.number(("tok", g)))
                distance = hn[:, g, :]
                link(nc.scalar.activation(distance, wide.bank(("tok", g))[:, :], ACT.Square, bias=neg_v[:, 0:1]))
                nc.scalar.activation(onehot[:, g * GN:(g + 1) * GN], distance, ACT.Relu, scale=-1.0, bias=one[:, 0:1]).then_inc(hot_ready, 1)
                after_start = keep_mem[:, g * GN:(g + 1) * GN].rearrange("p (t s) -> p t s", s=P)[:, :, 1:P]
                tok = wide.bank(("tok", g))[:, :].rearrange("p (t s) -> p t s", s=P)[:, :, 1:P]
                nc.scalar.activation(after_start, tok, ACT.Relu, scale=-1.0, bias=one[:, 0:1]).then_inc(wide.freed["act"], 1)
                wide.wait_read(act, ("tok", g))
                act.wait_ge(decay_ready, 1)
                nc.scalar.activation(after_start, after_start, ACT.Identity, scale=decay[:, 3:4], bias=decay[:, 2:3]).then_inc(keep_ready, 1)

            act.wait_ge(turn.filled, turn.number("rows"))
            copy(cols[:, :], turn.bank("rows")[:, 0:NR]).then_inc(turn.freed["act"], 1)
            turn.wait_read(act, "rows")

            def wait_hT(k):
                if k >= 2:
                    kind, n = HT[k - 2]
                    if kind == "hT":
                        act.wait_ge(hp_ready, n + 1)
                    else:
                        act.wait_ge(outp.filled, outp.number(("head", n)))

            def zT_copy(key):
                i = ZT.index(key)
                act.wait_ge(turn.filled, turn.number(key))
                if i >= ZB:
                    kind, g = ZT[i - ZB]
                    ring, job = ZT_LAST[kind](g)
                    act.wait_ge(ring.filled, ring.number(job))
                copy(zT[:, i % ZB, :], turn.bank(key)[:, 0:GN // 2].bitcast(F16)).then_inc(turn.freed["act"], 1)

            for what, n in PLAN:
                if what == "tokens":
                    keep(n)
                if what == "turn":
                    i, k = STEP[n][0], HT.index(("hT", n))
                    act.wait_ge(turn.filled, turn.number(("hT", n)))
                    wait_hT(k)
                    if n >= 2:
                        act.wait_ge(wide.filled, wide.number(("h", n - 2, FC - 1)))
                    b, gain, shift = turn.bank(("hT", n))[:, :], cols[:, i:i + 1], cols[:, L + i:L + i + 1]
                    nc.scalar.activation(hp[:, n % 2, 0, :], b, ACT.Identity, bias=shift, scale=gain).then_inc(hi_ready, 1)
                    nc.scalar.activation(hT[:, k % 2, :], b, ACT.Identity, bias=shift, scale=gain).then_inc(turn.freed["act"], 1)
                if what == "up":
                    i = STEP[n][0]
                    for c in range(FC):
                        act.wait_ge(wide.filled, wide.number(("h", n, c)))
                        if n >= 2 and c == 0:
                            act.wait_ge(outp.filled, outp.number(("o", n - 2)))
                        nc.scalar.activation(gT[:, n % 2, c, :], wide.bank(("h", n, c))[:, :], ACT.Gelu, scale=1.0 / WS16,
                                             bias=cols[:, R_B1 + i * FC + c:R_B1 + i * FC + c + 1]).then_inc(wide.freed["act"], 1)
                if what == "prep" and n == 4:
                    for key, at, m in (("qkv_w", C_Q, 3 * W), ("proj_w", C_P, W)):
                        act.wait_ge(turn.filled, turn.number(key))
                        copy(wst[0:W, at:at + m], turn.bank(key)[0:W, 0:m])
                        copy(wst[W:P, at:at + m], turn.bank(key)[0:W, 0:m]).then_inc(turn.freed["act"], 1)
                    act.wait_ge(outp.filled, outp.number("relb"))
                    copy(relb[:, :], outp.bank("relb")[:, 0:WS]).then_inc(outp.freed["act"], 1)
                if what == "xturn":
                    k = HT.index(("xT", n))
                    act.wait_ge(turn.filled, turn.number(("xT", n)))
                    wait_hT(k)
                    copy(hT[:, k % 2, :], turn.bank(("xT", n))[:, :]).then_inc(turn.freed["act"], 1)
                if what == "zturn":
                    act.wait_ge(turn.filled, turn.number(("a0", n)))
                    if n >= 2:
                        act.wait_ge(wide.filled, wide.number(("s0", n - 2)))
                    copy(z0T[:, n % 2, :], turn.bank(("a0", n))[0:W, :]).then_inc(turn.freed["act"], 1)
                if what == "score":
                    act.wait_ge(wide.filled, wide.number(("s0", n)))
                    if n >= 2:
                        act.wait_ge(outp.filled, outp.number(("ctx", n - 2)))
                    nc.scalar.activation(ex[:, n % 2, :], wide.bank(("s0", n))[:, :], ACT.Exp, scale=float(W) ** -0.5).then_inc(wide.freed["act"], 1)
                if what == "fturn":
                    zT_copy(("f0", n))
            for g in range(NG):
                act.wait_ge(gd_ready, g + 1)
                nc.scalar.activation(gex[:, group(g), :], gd[:, group(g), :], ACT.Exp).then_inc(gex_ready, 1)
            def slots_turned(k):
                act.wait_ge(turn.filled, turn.number(("xe", k)))
                copy(xeT[:, k * GN:(k + 1) * GN], turn.bank(("xe", k))[:, 0:GN // 2].bitcast(F16)).then_inc(turn.freed["act"], 1)

            slots_turned(0)
            for e in range(E):
                for k in range(slots_end(e), slots_end(e + 1)):
                    slots_turned(k)
                act.wait_ge(wide.filled, wide.number(("em", e, 0)))
                if e >= 2:
                    act.wait_ge(outp.filled, outp.number(("ey", e - 2)))
                nc.scalar.activation(hm[:, e % 2, 0, :], wide.bank(("em", e, 0))[:, 0:CAP], ACT.Relu,
                                     bias=e_b1s[:, e * EC:e * EC + 1]).then_inc(wide.freed["act"], 1)

            def qkv_copies(g):
                act.wait_ge(wide.filled, wide.number(("k", g)))
                if g >= 2:
                    act.wait_ge(wide.filled, wide.number(("s1", (g - 1) * GT - 1)))
                k = wide.bank(("k", g))[:, 0:GT * WS].rearrange("p (t k) -> p t k", t=GT)
                for h_ in range(H1):
                    last = nc.scalar.activation(km[:, g % 2, :, h_, :], k, ACT.Copy, scale=headmask[:, h_:h_ + 1])
                last.then_inc(wide.freed["act"], 1)
                act.wait_ge(wide.filled, wide.number(("q", g)))
                q = wide.bank(("q", g))[:, 0:GT * WS].rearrange("p (t q) -> p t q", t=GT)
                for w in range(2):
                    part = slice(w * W, (w + 1) * W)
                    last = copy(qbd[part, g % 2, :, w * WS:(w + 1) * WS], q[part], 1.0 / WS16)
                last.then_inc(wide.freed["act"], 1)

            def value_copies(g):
                act.wait_ge(outp.filled, outp.number(("v", g)))
                if g >= 2:
                    act.wait_ge(outp.filled, outp.number(("av", (g - 1) * GT - 1)))
                v5 = outp.bank(("v", g))[:, :].rearrange("p (t h i d) -> p t h i d", t=2 * GT, h=HP, i=2)
                for i in range(2):
                    part = slice(i * WS, (i + 1) * WS)
                    copy(vz[part, g % 2, 0, :, :, i * (HD + 1):i * (HD + 1) + HD], v5[part, :, :, i, :], 1.0 / WS16)
                copy(vf[:, g % 2, :], outp.bank(("v", g))[:, :], 1.0 / WS16).then_inc(vf_ready, 1)
                act.wait_ge(vf_ready, g + 1)
                act.sem_inc(outp.freed["act"], 1)

            def probs(t):
                act.wait_ge(sd_ready, t + 1)
                if t >= 2:
                    act.wait_ge(turn.filled, turn.number(("pT", t - 2)))
                    act.wait_ge(plo_ready, t - 1)
                src = sd[:, t % 2, :, :].rearrange("p h k -> p (h k)")
                nc.scalar.activation(pf[:, t % 2, :], src, ACT.Exp)
                nc.scalar.activation(pp[:, t % 2, 0, :], src, ACT.Exp).then_inc(pexp_ready, 1)

            def probs_turned(t):
                act.wait_ge(turn.filled, turn.number(("pT", t)))
                if t >= 2:
                    act.wait_ge(outp.filled, outp.number(("av", t - 2)))
                copy(pT[:, t % 2, :, :, :].rearrange("p a h q -> p (a h q)"), turn.bank(("pT", t))[:, :].bitcast(F16)).then_inc(turn.freed["act"], 1)

            act.wait_ge(parts_ready, 4)
            for what, n in PLAN2:
                if what == "turn_a1":
                    zT_copy(("a1", n))
                if what == "qkv":
                    qkv_copies(n)
                if what == "values":
                    value_copies(n)
                if what == "weights":
                    probs(n)
                if what == "turned":
                    probs_turned(n)
                if what == "turn_o":
                    zT_copy(("oT", n))
                if what == "rows":
                    zT_copy(("f1", n))
                if what == "router":
                    act.wait_ge(wide.filled, wide.number(("rh", n)))
                    if n >= 2:
                        act.wait_ge(outp.filled, outp.number(("rl", n - 2)))
                        act.wait_ge(rlo_ready, n - 1)
                    rh = wide.bank(("rh", n))[0:RH, :]
                    nc.scalar.activation(rhp[0:RH, n % 2, :], rh, ACT.Relu, scale=1.0 / WS16, bias=r_b1[:, 0:1])
                    nc.scalar.activation(rhf[:, n % 2, :], rh, ACT.Relu, scale=1.0 / WS16, bias=r_b1[:, 0:1]).then_inc(wide.freed["act"], 1)
                if what == "first":
                    g, q = n
                    act.wait_ge(wide.filled, wide.number(("h1", g, q)))
                    if g >= 2:
                        act.wait_ge(wide.filled, wide.number(("h2", g - 2, XP - 1)))
                    nc.scalar.activation(h1T[:, g % 2, q, :], wide.bank(("h1", g, q))[:, :], ACT.Relu, scale=1.0 / WS16,
                                         bias=cols[:, R_X1 + q:R_X1 + q + 1]).then_inc(wide.freed["act"], 1)
                if what == "logits":
                    act.wait_ge(td_ready, n + 1)
                    nc.scalar.activation(te[:, :, :], td[:, :, :], ACT.Exp).then_inc(te_ready, 1)
                if what == "second" and n[1] < 2:
                    g, q = n
                    act.wait_ge(wide.filled, wide.number(("h2", g, q)))
                    if g >= 2:
                        act.wait_ge(wide.filled, wide.number(("eo", g - 2, GT - 1)))
                    nc.scalar.activation(h2T[:, g % 2, q, :], wide.bank(("h2", g, q))[:, :], ACT.Relu,
                                         bias=cols[:, R_X2 + q:R_X2 + q + 1]).then_inc(wide.freed["act"], 1)
                if what == "choice":
                    act.wait_ge(tdl_ready, n + 1)
                    nc.scalar.activation(tex[:, :], tdl[:, :], ACT.Exp).then_inc(tex_ready, 1)

        @block.vector
        def _(dve):
            steps = [0]
            v = nc.vector

            def link(ins):
                steps[0] += 1
                ins.then_inc(dve_step, 1)
                dve.wait_ge(dve_step, steps[0])

            def ln_stats(key, src):
                k = LNS.index(key)
                for j in range(GT):
                    last = v.bn_stats(st[:, k % LB, j, :], src(j))
                link(last)
                for j in range(GT):
                    last = v.bn_aggr(mv[:, k % LB, j, :], st[:, k % LB, j, :])
                last.then_inc(stats_ready, 1)
                dve.wait_ge(stats_ready, k + 1)

            def ln_norm(key, src, dst):
                k = LNS.index(key)
                dve.wait_ge(rstd_ready, k + 1)
                for j in range(GT):
                    last = v.tensor_scalar(dst(j), src(j), mv[:, k % LB, j, 0:1], rstd[:, k % LB, j:j + 1], ALU.subtract, ALU.mult)
                return last

            def split_rows(key, src):
                i, g = ZS.index(key), key[1]
                if key[0] == "f1":
                    dve.wait_ge(turn.filled, turn.number(("oT", g)))
                if key[0] == "oT":
                    dve.wait_ge(turn.filled, turn.number(("a1", g)))
                link(v.tensor_copy(zs[:, group(g), 0:W], src))
                v.tensor_tensor(zs[:, group(g), W:2 * W], src, zs[:, group(g), 0:W], ALU.subtract).then_inc(zs_ready, 1)

            def ln_rows(key):
                k, g = LNS.index(key), key[1]
                link(ln_norm(key, lambda j: h[:, g * GT + j, :], lambda j: zf[:, k % 2, j, :]))
                split_rows(key, zf[:, k % 2, :, :])

            def weight_pair(hi, lo, src, scale):
                link(v.tensor_scalar(hi, src, scale, None, ALU.mult))
                return v.scalar_tensor_tensor(out=lo, in0=src, scalar=scale, in1=hi, op0=ALU.mult, op1=ALU.subtract)

            dve.wait_ge(const_ready, 2)
            link(v.tensor_copy(iota_vf[:, :], iota_v[:, :]))
            v.tensor_scalar(neg_v[:, :], iota_vf[:, :], -1.0, None, ALU.mult).then_inc(neg_ready, 1)
            link(v.tensor_scalar(not_zero[:, :], iota_vf[0:V, :], 0.0, None, ALU.not_equal))
            dve.wait_ge(in_emb, 64)
            link(v.tensor_tensor(embf[:, :], emb[:, :], b_f[:, :], ALU.add))
            link(v.tensor_scalar(etable[0:V, :], embf[:, :], TS16, None, ALU.mult))
            v.scalar_tensor_tensor(out=etable[V:2 * V, :], in0=embf[:, :], scalar=TS16, in1=etable[0:V, :],
                                   op0=ALU.mult, op1=ALU.subtract).then_inc(etable_ready, 1)
            dve.wait_ge(outp.filled, outp.number("table"))
            link(v.tensor_tensor(table0[:, :], outp.bank("table")[0:V, 0:D], b_upd[:, :], ALU.add))
            dve.sem_inc(outp.freed["dve"], 1)
            link(v.tensor_scalar(table1[:, :], table0[:, :], not_zero[:, 0:1], TS16, ALU.mult, ALU.mult))
            link(v.tensor_copy(table[0:V, :], table1[:, :]))
            v.tensor_tensor(table[V:2 * V, :], table1[:, :], table[0:V, :], ALU.subtract).then_inc(table_ready, 1)
            dve.wait_ge(decay_exp, 1)
            link(v.tensor_scalar(decay[:, 1:2], decay[:, 0:1], 1.0, None, ALU.add))
            link(v.reciprocal(decay[:, 2:3], decay[:, 1:2]))
            v.tensor_scalar(decay[:, 3:4], decay[:, 2:3], -1.0, 1.0, ALU.mult, ALU.add).then_inc(decay_ready, 1)

            def memory(g):
                c = slice(g * GN, (g + 1) * GN)
                dve.wait_ge(keep_ready, g + 1)
                dve.wait_ge(const_ready, 4)
                dve.wait_ge(wide.filled, wide.number(("u", g)))
                v.tensor_tensor_scan(mems[:, c], keep_mem[:, c], wide.bank(("u", g))[:, :], 0.0, ALU.mult, ALU.add).then_inc(wide.freed["dve"], 1)

            def embed(g):
                dve.wait_ge(outp.filled, outp.number(("y", g)))
                y = outp.bank(("y", g))[:, :].rearrange("p (t d) -> p t d", t=GT)
                ln_stats(("y", g), lambda j: y[:, j, :])
                k = LNS.index(("y", g))
                for j in range(GT):
                    last = v.scalar_tensor_tensor(out=ln_t[:, g % 2, j, :], in0=y[:, j, :], scalar=mv[:, k % LB, j, 0:1], in1=norm_g[:, :],
                                                  op0=ALU.subtract, op1=ALU.mult)
                last.then_inc(outp.freed["dve"], 1)

            def stream_in(g):
                k = LNS.index(("y", g))
                outp.wait_read(dve, ("y", g))
                dve.wait_ge(rstd_ready, k + 1)
                for j in range(GT):
                    last = v.scalar_tensor_tensor(out=x[:, g * GT + j, :], in0=ln_t[:, g % 2, j, :], scalar=rstd[:, k % LB, j:j + 1],
                                                  in1=norm_b[:, :], op0=ALU.mult, op1=ALU.add)
                last.then_inc(x_ready, 1)
                dve.wait_ge(x_ready, 1 + NEXT.index(AT[0, g]))
                ln_stats(("c", AT[0, g]), lambda j: x[:, g * GT + j, :])

            def layer_norm(n):
                g = STEP[n][1]
                ln_norm(("c", n), lambda j: x[:, g * GT + j, :], lambda j: hn[:, g, j * P:(j + 1) * P]).then_inc(hn_ready, 1)

            def w1_pair(i):
                dve.wait_ge(in_w1[i], 16)
                weight_pair(w1p[:, 0, i, :], w1p[:, 1, i, :], w1[:, i, :], WS16).then_inc(w1_ready, 1)

            def turn_pair(n):
                k = HT.index(("hT", n))
                dve.wait_ge(hi_ready, n + 1)
                turn.wait_read(dve, ("hT", n))
                v.tensor_tensor(hp[:, n % 2, 1, :], hT[:, k % 2, :], hp[:, n % 2, 0, :], ALU.subtract).then_inc(hp_ready, 1)

            PIECES = [(i * C_Q // 4, (i + 1) * C_Q // 4) for i in range(4)] + [(C_Q, C_R), (C_R, C_N)]

            def prep(i):
                if i == 0:
                    dve.wait_ge(in_exp, 16 * (E + 5))
                    turn.wait_read(dve, "rows")
                    dve.wait_ge(parts_ready, 1)
                if i == 4:
                    turn.wait_read(dve, "proj_w")
                if i == 5:
                    dve.wait_ge(in_x1, 16 * 10)
                c = slice(*PIECES[i])
                weight_pair(wp[:, 0, c], wp[:, 1, c], wst[:, c], WS16).then_inc(prep_ready, 1)
                if i == 0:
                    v.tensor_scalar(e_b1s[:, :], cols[:, R_E1:NR], WS16, None, ALU.mult)
                    v.tensor_copy(rank8[:, :], rank_i[:, :])
                    v.tensor_scalar(rank6[:, :], rank_i[:, 0:X], float(X - E), None, ALU.add)
                    link(v.tensor_copy(trash[:, :], trash_i[:, :]))
                if i == 5:
                    weight_pair(r_w2p[:, 0, :], r_w2p[:, 1, :], r_w2[:, :], WS16)
                    for c, scale in ((slice(0, W), WS16), (slice(W, BN), 1.0)):
                        v.tensor_scalar(bias_p[0:1, c], bias_rows[0:1, c], scale, None, ALU.mult)
                        link(v.tensor_scalar(bias_hi[32:33, c], bias_rows[32:33, c], scale, None, ALU.mult))
                        last = v.scalar_tensor_tensor(out=bias_p[32:33, c], in0=bias_rows[32:33, c], scalar=scale, in1=bias_hi[32:33, c],
                                                      op0=ALU.mult, op1=ALU.subtract)
                    last.then_inc(prep_ready, 1)

            def down(n):
                i, g = STEP[n]
                dve.wait_ge(outp.filled, outp.number(("o", n)))
                dve.wait_ge(xb_ready, NEXT.index(n) + 1)
                v.tensor_tensor(x[:, group(g), :], outp.bank(("o", n))[:, :].rearrange("p (t d) -> p t d", t=GT), xb[:, group(g), :],
                                ALU.add).then_inc(x_ready, 1)
                dve.wait_ge(x_ready, NG + n + 1)
                dve.sem_inc(outp.freed["dve"], 1)
                if i + 1 < L:
                    ln_stats(("c", AT[i + 1, g]), lambda j: x[:, g * GT + j, :])

            def head(g):
                dve.wait_ge(in_head, 32)
                dve.wait_ge(outp.filled, outp.number(("head", g)))
                link(v.tensor_tensor(h[:, group(g), :], outp.bank(("head", g))[:, 0:GT * W].rearrange("p (t w) -> p t w", t=GT),
                                     bm(head_b[:, :], GT), ALU.add))
                dve.sem_inc(outp.freed["dve"], 1)
                ln_stats(("a0", g), lambda j: h[:, g * GT + j, :])

            def attend_norm(g):
                ln_norm(("a0", g), lambda j: h[:, g * GT + j, :], lambda j: z0[:, g * GT + j, 0:W]).then_inc(z0_ready, 1)

            def context(g):
                dve.wait_ge(outp.filled, outp.number(("ctx", g)))
                c = outp.bank(("ctx", g))[:, 0:GT * (W + 1)].rearrange("p (t w) -> p t w", t=GT)
                link(v.reciprocal(rs[:, g % 2, :], c[:, :, W]))
                for j in range(GT):
                    last = v.scalar_tensor_tensor(out=h[:, g * GT + j, :], in0=c[:, j, 0:W], scalar=rs[:, g % 2, j:j + 1],
                                                  in1=h[:, g * GT + j, :], op0=ALU.mult, op1=ALU.add)
                link(last)
                dve.sem_inc(outp.freed["dve"], 1)
                ln_stats(("f0", g), lambda j: h[:, g * GT + j, :])

            def gate(g):
                t = group(g)
                dve.wait_ge(in_gate, 32)
                dve.wait_ge(outp.filled, outp.number(("gate", g)))
                lg = outp.bank(("gate", g))[:, 0:GT * E].rearrange("p (t e) -> p t e", t=GT)
                link(v.scalar_tensor_tensor(out=glog[:, t, :], in0=lg, scalar=1.0 / WS16, in1=bm(gate_b[:, :], GT), op0=ALU.mult, op1=ALU.add))
                dve.sem_inc(outp.freed["dve"], 1)
                link(v.tensor_reduce(gm[:, t], glog[:, t, :], AX, ALU.max))
                v.tensor_tensor(gd[:, t, :], glog[:, t, :], bc(gm[:, t], E), ALU.subtract).then_inc(gd_ready, 1)
                dve.wait_ge(gd_ready, g + 1)
                link(v.scalar_tensor_tensor(out=gv[:, t, :], in0=gd[:, t, :], scalar=0.0, in1=bm(rank8[:, :], GT), op0=ALU.is_equal, op1=ALU.mult))
                link(v.tensor_reduce(gbest[:, t], gv[:, t, :], AX, ALU.max))
                v.tensor_tensor(goh[:, t, :], bm(rank8[:, :], GT), bc(gbest[:, t], E), ALU.is_equal).then_inc(goh_ready, 1)
                link(v.tensor_scalar(base[:, t], gbest[:, t], -float(CAP), float(E * CAP - 1), ALU.mult, ALU.add))
                link(v.tensor_tensor(slot[:, t], base[:, t], trash[:, t], ALU.subtract))

            def place(g):
                t = group(g)
                dve.wait_ge(outp.filled, outp.number(("pos", g)))
                dve.wait_ge(goh_ready, g + 1)
                link(v.tensor_tensor(pc[:, t, :], outp.bank(("pos", g))[:, 0:GT * E].rearrange("p (t e) -> p t e", t=GT), goh[:, t, :], ALU.mult))
                dve.sem_inc(outp.freed["dve"], 1)
                link(v.tensor_reduce(pos1[:, t], pc[:, t, :], AX, ALU.add))
                v.scalar_tensor_tensor(out=idx_g[:, t], in0=pos1[:, t], scalar=float(CAP), in1=base[:, t], op0=ALU.min, op1=ALU.add)
                v.tensor_scalar(kept[:, t], pos1[:, t], float(CAP), None, ALU.is_le)
                link(v.tensor_tensor(slot2[:, t], slot[:, t], pos1[:, t], ALU.add))
                link(v.tensor_tensor(slot2[:, t], slot2[:, t], kept[:, t], ALU.mult))
                v.tensor_tensor(idx_s[:, t], slot2[:, t], trash[:, t], ALU.add).then_inc(idx_ready, 1)

            for what, n in PLAN:
                if what == "memory":
                    memory(n)
                if what == "embed":
                    if outp.at["y", n] == outp.at["y", 0]:
                        dve.wait_ge(in_norm, 32)
                    embed(n)
                if what == "stream":
                    stream_in(n)
                if what == "norm":
                    layer_norm(n)
                if what == "w1":
                    w1_pair(n)
                if what == "turn":
                    turn_pair(n)
                if what == "down":
                    down(n)
                if what == "prep":
                    prep(n)
                if what == "head":
                    head(n)
                if what == "context":
                    context(n)
                if what == "znorm":
                    attend_norm(n)
                if what == "fnorm":
                    ln_rows(("f0", n))
                if what == "gate":
                    gate(n)
                if what == "place":
                    place(n)
            for g in range(NG):
                t = group(g)
                dve.wait_ge(gex_ready, g + 1)
                link(v.tensor_reduce(gsum[:, t], gex[:, t, :], AX, ALU.add))
                link(v.reciprocal(prob[:, t], gsum[:, t]))
                link(v.tensor_tensor(pk[:, t], prob[:, t], kept[:, t], ALU.mult))

            R = CAP - 2 * P
            for e in range(E + 1):
                if e < E:
                    dve.wait_ge(wide.filled, wide.number(("em", e, 1)))
                    if e >= 2:
                        dve.wait_ge(outp.filled, outp.number(("ey", e - 2)))
                    v.tensor_scalar(hm[:, e % 2, 1, :], wide.bank(("em", e, 1))[:, 0:CAP], e_b1s[:, e * EC + 1:e * EC + 2], 0.0,
                                    ALU.add, ALU.max).then_inc(wide.freed["dve"], 1)
                if e >= 1:
                    q = e - 1
                    dve.wait_ge(outp.filled, outp.number(("ey", q)))
                    y = outp.bank(("ey", q))[:, 0:3 * W].rearrange("p (m w) -> p m w", m=3)
                    t = 5 * (q // 2)
                    if q % 2 == 0:
                        whole, part, pt, m0 = slice(t, t + 2), slice(0, R), t + 2, 0
                    else:
                        whole, part, pt, m0 = slice(t + 3, t + 5), slice(P - R, P), t + 2, 1
                    v.scalar_tensor_tensor(out=ye[part, pt, :], in0=y[part, 2 - 2 * m0, :], scalar=1.0 / WS16, in1=e_b2[part, q, :], op0=ALU.mult, op1=ALU.add)
                    v.scalar_tensor_tensor(out=ye[:, whole, :], in0=y[:, m0:m0 + 2, :], scalar=1.0 / WS16, in1=bm(e_b2[:, q, :], 2),
                                           op0=ALU.mult, op1=ALU.add).then_inc(ye_ready, 1)
                    dve.wait_ge(ye_ready, q + 1)
                    dve.sem_inc(outp.freed["dve"], 1)

            def returned(g):
                t = group(g)
                dve.wait_ge(gathered[g], 16 * GT)
                link(v.tensor_tensor(yp[:, :, :], yg[:, t, :], bc(pk[:, t], W), ALU.mult))
                link(v.tensor_scalar(ya[:, :, :], yp[:, :, :], 0.0, None, ALU.max))
                link(v.scalar_tensor_tensor(out=yn[:, :, :], in0=yp[:, :, :], scalar=0.0, in1=ya[:, :, :], op0=ALU.min, op1=ALU.add))
                v.tensor_scalar(yfin[:, :, :], yn[:, :, :], 0.0, 0.0, ALU.mult, ALU.is_equal)
                link(v.tensor_scalar(yc[:, :, :], yn[:, :, :], CLIP, -CLIP, ALU.min, ALU.max))
                link(v.copy_predicated(yc[:, :, :], yfin[:, :, :], yn[:, :, :]))
                link(v.tensor_tensor(h[:, t, :], h[:, t, :], yc[:, :, :], ALU.add))
                ln_stats(("a1", g), lambda j: h[:, g * GT + j, :])

            def biased(t):
                dve.wait_ge(wide.filled, wide.number(("s1", t)))
                if t >= 2:
                    dve.wait_ge(sd_ready, t - 1)
                s3 = wide.bank(("s1", t))[:, :].rearrange("p (h k) -> p h k", h=H1)
                v.scalar_tensor_tensor(out=sm[:, t % 2, :, :], in0=s3, scalar=float(HD) ** -0.5, in1=bm(relb[:, :], H1),
                                       op0=ALU.mult, op1=ALU.add).then_inc(wide.freed["dve"], 1)
                wide.wait_read(dve, ("s1", t))
                v.tensor_reduce(smx[:, t % 2, :], sm[:, t % 2, :, :], AX, ALU.max).then_inc(smx_ready, 1)

            def heads_out(t):
                dve.wait_ge(outp.filled, outp.number(("av", t)))
                g, j = t // GT, t % GT
                av = outp.bank(("av", t))[:, 0:HP * 2 * VW].rearrange("p (h w i d) -> p w h i d", h=HP, w=2, i=2)
                r = rden[:, t % 2, :].rearrange("p (h i) -> p h i", i=2)
                for w in range(2):
                    part = slice(w * WS, (w + 1) * WS)
                    last = v.reciprocal(r[part], av[part, w, :, :, HD])
                link(last)
                for w in range(2):
                    part = slice(w * WS, (w + 1) * WS)
                    last = v.tensor_tensor(o[part, g % 2, j, :].rearrange("p (h i d) -> p h i d", h=HP, i=2), av[part, w, :, :, 0:HD],
                                           r[part].unsqueeze(3).broadcast_to([WS, HP, 2, HD]), ALU.mult)
                last.then_inc(outp.freed["dve"], 1)
                if j == GT - 1:
                    outp.wait_read(dve, ("av", t))
                    split_rows(("oT", g), o[:, g % 2, :, :])

            def projected(g):
                dve.wait_ge(outp.filled, outp.number(("proj", g)))
                link(v.scalar_tensor_tensor(out=h[:, group(g), :], in0=outp.bank(("proj", g))[:, 0:GT * W].rearrange("p (t w) -> p t w", t=GT),
                                            scalar=1.0 / WS16, in1=h[:, group(g), :], op0=ALU.mult, op1=ALU.add))
                dve.sem_inc(outp.freed["dve"], 1)
                ln_stats(("f1", g), lambda j: h[:, g * GT + j, :])

            for what, n in PLAN2:
                if what == "returned":
                    returned(n)
                if what == "anorm":
                    ln_rows(("a1", n))
                if what == "xnorm":
                    ln_rows(("f1", n))
                if what == "scores":
                    biased(n)
                if what == "applied":
                    heads_out(n)
                if what == "project":
                    projected(n)
                if what == "router":
                    wide.wait_read(dve, ("rh", n))
                    if n >= 2:
                        dve.wait_ge(outp.filled, outp.number(("rl", n - 2)))
                    v.tensor_tensor(rhp[RH:2 * RH, n % 2, :], rhf[:, n % 2, :], rhp[0:RH, n % 2, :], ALU.subtract).then_inc(rlo_ready, 1)
                if what == "logits":
                    dve.wait_ge(outp.filled, outp.number(("rl", n)))
                    lg = outp.bank(("rl", n))[:, 0:GT * X].rearrange("p (t e) -> p t e", t=GT)
                    link(v.scalar_tensor_tensor(out=tl[:, :, :], in0=lg, scalar=1.0 / WS16, in1=bm(r_b2[:, :], GT), op0=ALU.mult, op1=ALU.add))
                    dve.sem_inc(outp.freed["dve"], 1)
                    link(v.tensor_reduce(tm[:, :], tl[:, :, :], AX, ALU.max))
                    v.tensor_tensor(td[:, :, :], tl[:, :, :], bc(tm[:, :], X), ALU.subtract).then_inc(td_ready, 1)
                    dve.wait_ge(td_ready, n + 1)
                    link(v.scalar_tensor_tensor(out=tv[:, :, :], in0=td[:, :, :], scalar=0.0, in1=bm(rank6[:, :], GT), op0=ALU.is_equal, op1=ALU.mult))
                    link(v.tensor_reduce(tb[:, :], tv[:, :, :], AX, ALU.max))
                    link(v.tensor_tensor(o1[:, :, :], bm(rank6[:, :], GT), bc(tb[:, :], X), ALU.is_equal))
                if what == "choice":
                    dve.wait_ge(te_ready, n + 1)
                    v.tensor_reduce(tsum[:, :], te[:, :, :], AX, ALU.add)
                    link(v.scalar_tensor_tensor(out=tp[:, :, :], in0=o1[:, :, :], scalar=-4.0, in1=te[:, :, :], op0=ALU.mult, op1=ALU.add))
                    v.reciprocal(trs[:, :], tsum[:, :])
                    link(v.tensor_reduce(m2[:, :], tp[:, :, :], AX, ALU.max))
                    link(v.tensor_tensor(teq[:, :, :], tp[:, :, :], bc(m2[:, :], X), ALU.is_equal))
                    v.scalar_tensor_tensor(out=tdl[:, :], in0=m2[:, :], scalar=-1.0, in1=trs[:, :], op0=ALU.add, op1=ALU.mult).then_inc(tdl_ready, 1)
                    link(v.tensor_tensor(tv[:, :, :], teq[:, :, :], bm(rank6[:, :], GT), ALU.mult))
                    link(v.tensor_reduce(tb[:, :], tv[:, :, :], AX, ALU.max))
                    link(v.tensor_tensor(o2[:, :, :], bm(rank6[:, :], GT), bc(tb[:, :], X), ALU.is_equal))
                if what == "second" and n[1] >= 2:
                    g, q = n
                    dve.wait_ge(wide.filled, wide.number(("h2", g, q)))
                    v.tensor_scalar(h2T[:, g % 2, q, :], wide.bank(("h2", g, q))[:, :], cols[:, R_X2 + q:R_X2 + q + 1], 0.0, ALU.add, ALU.max).then_inc(wide.freed["dve"], 1)
                if what == "shares":
                    dve.wait_ge(tex_ready, n + 1)
                    link(v.tensor_scalar(tw0[:, :], tex[:, :], 1.0, None, ALU.add))
                    link(v.reciprocal(tw1[:, :], tw0[:, :]))
                    link(v.tensor_tensor(tw2[:, :], tw1[:, :], tex[:, :], ALU.mult))
                    link(v.tensor_tensor(o1[:, :, :], o1[:, :, :], bc(tw1[:, :], X), ALU.mult))
                    link(v.tensor_tensor(o2[:, :, :], o2[:, :, :], bc(tw2[:, :], X), ALU.mult))
                    v.tensor_tensor(route[:, group(n), :], o1[:, :, :], o2[:, :, :], ALU.add).then_inc(route_ready, 1)
                if what == "third":
                    g, j = n
                    t = g * GT + j
                    dve.wait_ge(route_ready, g + 1)
                    dve.wait_ge(wide.filled, wide.number(("eo", g, j)))
                    if 2 * g + j // 2 >= 2:
                        dve.wait_ge(shares_used, 2 * g + j // 2 - 1)
                    v.tensor_tensor(shares[:, j // 2, j % 2, :, :], wide.bank(("eo", g, j))[:, 0:X * W].rearrange("p (e w) -> p e w", e=X),
                                    bc(route[:, t, :], W), ALU.mult).then_inc(wide.freed["dve"], 1)
                    if g == NG - 1:
                        wide.wait_read(dve, ("eo", g, j))
                        link(v.tensor_reduce(yp[:, j, :], shares[:, j // 2, j % 2, :, :].rearrange("p e w -> p w e"), AX, ALU.add))
                        last = v.tensor_tensor(res[:, t, :], yp[:, j, :], h[:, t, :], ALU.add)
                        if j == GT - 1:
                            last.then_inc(last_ready, 1)

        @block.tensor
        def _(pe):
            def mm(o_, l_, r_, start=True, stop=True):
                return nc.tensor.matmul(o_, l_, r_, start=start, stop=stop)

            def turns(key, srcs, width):
                turn.wait_free(pe, key)
                for j, src in enumerate(srcs):
                    last = nc.tensor.transpose(turn.bank(key)[0:width, j * P:j * P + src.shape[0]], src, ident[0:src.shape[0], 0:src.shape[0]])
                last.then_inc(turn.filled, 1)

            def turns16(key, srcs):
                turn.wait_free(pe, key)
                bank = turn.bank(key)[:, :].bitcast(F16)
                for j, src in enumerate(srcs):
                    last = nc.tensor.transpose(bank[:, j * P:(j + 1) * P], src, ident16[:, :])
                last.then_inc(turn.filled, 1)

            def weights(a0, a1):
                return [wp[:, i, a0:a1] for i in range(2)]

            pe.wait_ge(ident_ready, 1)
            pe.wait_ge(in_emb, 64)
            turns("emb", [emb[:, :]], D)
            pe.wait_ge(in_rows, 112)
            turns("rows", [rows[:, :]], P)
            turn.wait_read(pe, "emb")
            mm(outp.bank("table")[0:V, 0:D], embT[:, :], w_upd[:, :]).then_inc(outp.filled, 1)
            def tokens_over_partitions(g):
                pe.wait_ge(tok16_ready, g + 1)
                pe.wait_ge(const_ready, 1)
                wide.wait_free(pe, ("tok", g))
                mm(wide.bank(("tok", g))[:, :], ones16[0:1, :], tokens16[:, g * GN:(g + 1) * GN]).then_inc(wide.filled, 1)

            def memory_inputs(g):
                pe.wait_ge(table_ready, 1)
                pe.wait_ge(hot_ready, g + 1)
                wide.wait_free(pe, ("u", g))
                mm(wide.bank(("u", g))[:, :], table[:, :], onehot[:, g * GN:(g + 1) * GN]).then_inc(wide.filled, 1)

            def embedded(g):
                pe.wait_ge(etable_ready, 1)
                pe.wait_ge(in_wf, 32)
                wide.wait_read(pe, ("u", g))
                outp.wait_free(pe, ("y", g))
                for j in range(GT):
                    c = slice((g * GT + j) * P, (g * GT + j + 1) * P)
                    y = outp.bank(("y", g))[:, j * D:(j + 1) * D]
                    mm(y, onehot[:, c], etable[:, :], stop=False)
                    last = mm(y, mems[:, c], w_f[:, :], start=False)
                last.then_inc(outp.filled, 1)

            def up(n):
                i, g = STEP[n]
                pe.wait_ge(hi_ready, n + 1)
                pe.wait_ge(w1_ready, i + 1)

                def high_rows(c):
                    wide.wait_free(pe, ("h", n, c))
                    b = wide.bank(("h", n, c))[:, :]
                    mm(b, w1p[:, 0, i, c * P:(c + 1) * P], hp[:, n % 2, 0, :], stop=False)
                    mm(b, w1p[:, 1, i, c * P:(c + 1) * P], hp[:, n % 2, 0, :], start=False, stop=False)

                high_rows(0)
                high_rows(1)
                pe.wait_ge(hp_ready, n + 1)
                for c in range(FC):
                    if c >= 2:
                        high_rows(c)
                    mm(wide.bank(("h", n, c))[:, :], w1p[:, 0, i, c * P:(c + 1) * P], hp[:, n % 2, 1, :], start=False).then_inc(wide.filled, 1)

            def down(n):
                i = STEP[n][0]
                key = ("o", n)
                wide.wait_read(pe, ("h", n, FC - 1))
                pe.wait_ge(in_w2[i], 16)
                outp.wait_free(pe, key)
                for j in range(GT):
                    for c in range(FC):
                        last = mm(outp.bank(key)[:, j * D:(j + 1) * D], gT[:, n % 2, c, j * P:(j + 1) * P], w2[:, i, c, :],
                                  start=(c == 0), stop=(c == FC - 1))
                last.then_inc(outp.filled, 1)

            def z_turned(key):
                turn.wait_read(pe, key)
                return zT[:, ZT.index(key) % ZB, :]

            def turn_rows(key):
                pe.wait_ge(zs_ready, ZS.index(key) + 1)
                turns16(key, [zs[:, key[1] * GT + j, 0:2 * W] for j in range(GT)])

            for what, n in PLAN:
                if what == "tokens":
                    tokens_over_partitions(n)
                if what == "memory":
                    memory_inputs(n)
                if what == "embed":
                    embedded(n)
                if what == "turn":
                    g = STEP[n][1]
                    pe.wait_ge(hn_ready, NORMS.index(n) + 1)
                    turns(("hT", n), [hn[:, g, j * P:(j + 1) * P] for j in range(GT)], P)
                if what == "up":
                    up(n)
                if what == "down":
                    down(n)
                if what == "prep" and n == 4:
                    pe.wait_ge(in_att, 64)
                    pe.wait_ge(parts_ready, 1)
                    turns("qkv_w", [qkv_rows[:, 0, :], qkv_rows[0:W, 1, :]], W)
                    turns("proj_w", [proj_rows[:, :]], W)
                    outp.wait_free(pe, "relb")
                    mm(outp.bank("relb")[:, 0:WS], flip[:, :, :].rearrange("r w q -> r (w q)"), relb_up[:, :]).then_inc(outp.filled, 1)
                if what == "xturn":
                    pe.wait_ge(x_ready, NG + AT[L - 1, n] + 1)
                    turns(("xT", n), [x[:, n * GT + j, :] for j in range(GT)], P)
                if what == "head":
                    pe.wait_ge(in_head, 32)
                    turn.wait_read(pe, ("xT", n))
                    outp.wait_free(pe, ("head", n))
                    k = HT.index(("xT", n))
                    for j in range(GT):
                        last = mm(outp.bank(("head", n))[:, j * W:(j + 1) * W], hT[:, k % 2, j * P:(j + 1) * P], head_w[:, :])
                    last.then_inc(outp.filled, 1)
                if what == "zturn":
                    pe.wait_ge(z0_ready, n + 1)
                    turns(("a0", n), [z0[:, n * GT + j, 0:W] for j in range(GT)], W)
                if what == "score":
                    turn.wait_read(pe, ("a0", n))
                    wide.wait_free(pe, ("s0", n))
                    for j in range(GT):
                        q = z0T[:, n % 2, j * P:(j + 1) * P]
                        last = mm(wide.bank(("s0", n))[:, j * P:(j + 1) * P], q, q)
                    last.then_inc(wide.filled, 1)
                if what == "context":
                    wide.wait_read(pe, ("s0", n))
                    outp.wait_free(pe, ("ctx", n))
                    for j in range(GT):
                        last = mm(outp.bank(("ctx", n))[:, j * (W + 1):(j + 1) * (W + 1)], ex[:, n % 2, j * P:(j + 1) * P], z0[:, n * GT + j, :])
                    last.then_inc(outp.filled, 1)
                if what == "fturn":
                    turn_rows(("f0", n))
                if what == "gate":
                    pe.wait_ge(prep_ready, 1)
                    zt = z_turned(("f0", n))
                    outp.wait_free(pe, ("gate", n))
                    hi, lo = weights(0, E)
                    for j in range(GT):
                        b = outp.bank(("gate", n))[:, j * E:(j + 1) * E]
                        mm(b, zt[:, j * P:(j + 1) * P], hi, stop=False)
                        last = mm(b, zt[:, j * P:(j + 1) * P], lo, start=False)
                    last.then_inc(outp.filled, 1)
                if what == "place":
                    g = n
                    pe.wait_ge(goh_ready, g + 1)
                    outp.wait_free(pe, ("pos", g))
                    cnt = outp.bank(("pos", g))[:, 0:GT * E].rearrange("p (t e) -> p t e", t=GT)
                    last = mm(cnt, tri[:, :], goh[:, group(g), :], stop=False)
                    for t in range(g * GT + GT - 1):
                        j = max(0, t - g * GT + 1)
                        last = mm(cnt[:, j:GT, :], ones16[:, :], bm(goh[:, t, :], GT - j), start=False, stop=(t == g * GT + GT - 2))
                    last.then_inc(outp.filled, 1)

            def turn_slots(k):
                pe.wait_ge(rows_back[k], 16)
                turns16(("xe", k), [xe[:, 4 * k + j, :] for j in range(4)])

            turn_slots(0)
            pe.wait_ge(prep_ready, 4)
            for e in range(E + 1):
                if e < E:
                    for k in range(slots_end(e), slots_end(e + 1)):
                        turn_slots(k)
                    turn.wait_read(pe, ("xe", slots_end(e) - 1))
                    for c in range(EC):
                        wide.wait_free(pe, ("em", e, c))
                        b = wide.bank(("em", e, c))[:, 0:CAP]
                        at = C_E + e * EF + c * P
                        hi, lo = weights(at, at + P)
                        mm(b, hi, xeT[:, e * CAP:(e + 1) * CAP], stop=False)
                        mm(b, lo, xeT[:, e * CAP:(e + 1) * CAP], start=False).then_inc(wide.filled, 1)
                if e >= 1:
                    q = e - 1
                    for c in range(EC):
                        wide.wait_read(pe, ("em", q, c))
                    outp.wait_free(pe, ("ey", q))
                    cuts = [(0, P, 0), (P, 2 * P, 0), (2 * P, CAP, 0)] if q % 2 == 0 else [(0, P // 2, P // 2), (P // 2, P // 2 + P, 0), (P // 2 + P, CAP, 0)]
                    for m, (s0, s1, p0) in enumerate(cuts):
                        for c in range(EC):
                            last = mm(outp.bank(("ey", q))[p0:p0 + s1 - s0, m * W:(m + 1) * W], hm[:, q % 2, c, s0:s1], e_w2[:, q, c, :], start=(c == 0), stop=(c == EC - 1))
                    last.then_inc(outp.filled, 1)

            def qkv(g):
                zt = z_turned(("a1", g))
                zw = zt.rearrange("p (t w q) -> p w t q", t=GT, w=2)
                for key, at in (("k", C_Q + W), ("q", C_Q)):
                    wide.wait_free(pe, (key, g))
                    hi, lo = weights(at, at + W)
                    for w in range(2):
                        b = wide.bank((key, g))[w * W:(w + 1) * W, 0:GT * WS]
                        mm(b, hi, zw[:, w, :, :], stop=False)
                        last = mm(b, lo, zw[:, w, :, :], start=False)
                    last.then_inc(wide.filled, 1)

            def values(g):
                zt = z_turned(("a1", g))
                outp.wait_free(pe, ("v", g))
                hi, lo = weights(C_Q + 2 * W, C_Q + 3 * W)
                for t in range(2 * GT):
                    for i in range(2):
                        b = outp.bank(("v", g))[i * WS:(i + 1) * WS, t * W:(t + 1) * W]
                        mm(b, zt[:, t * WS:(t + 1) * WS], hi, stop=False)
                        last = mm(b, zt[:, t * WS:(t + 1) * WS], lo, start=False)
                last.then_inc(outp.filled, 1)

            def pair(b, at, m, zt):
                hi, lo = weights(at, at + m)
                mm(b, hi, zt, stop=False)
                return mm(b, lo, zt, start=False)

            pe.wait_ge(in_xbd, 64)
            pe.wait_ge(prep_ready, 7)
            pe.wait_ge(parts_ready, 4)
            for what, n in PLAN2:
                if what == "turn_a1":
                    turn_rows(("a1", n))
                if what == "qkv":
                    qkv(n)
                if what == "values":
                    values(n)
                if what == "scores":
                    g, j = n // GT, n % GT
                    wide.wait_read(pe, ("q", g))
                    wide.wait_free(pe, ("s1", n))
                    mm(wide.bank(("s1", n))[:, :], qbd[:, g % 2, j, :], km[:, g % 2, j, :, :].rearrange("p h k -> p (h k)")).then_inc(wide.filled, 1)
                if what == "turned":
                    pe.wait_ge(pexp_ready, n + 1)
                    pe.wait_ge(plo_ready, n + 1)
                    turns16(("pT", n), [pp[:, n % 2, i, q * P:(q + 1) * P] for i in range(2) for q in range(HP)])
                if what == "applied":
                    t, g, j = n, n // GT, n % GT
                    turn.wait_read(pe, ("pT", t))
                    outp.wait_read(pe, ("v", g))
                    pe.wait_ge(vlo_ready, 2 * g + 2)
                    outp.wait_free(pe, ("av", t))
                    for q in range(HP):
                        b = outp.bank(("av", t))[:, q * 2 * VW:(q + 1) * 2 * VW].rearrange("p (w d) -> p w d", w=2)
                        hi, lo = (vz[:, g % 2, i, 2 * j:2 * j + 2, q, :] for i in range(2))
                        mm(b, pT[:, t % 2, 0, q, :], hi, stop=False)
                        mm(b, pT[:, t % 2, 0, q, :], lo, start=False, stop=False)
                        last = mm(b, pT[:, t % 2, 1, q, :], hi, start=False)
                    last.then_inc(outp.filled, 1)
                if what == "turn_o":
                    turn_rows(("oT", n))
                if what == "project":
                    g = n
                    zt = z_turned(("oT", g))
                    outp.wait_free(pe, ("proj", g))
                    hi, lo = weights(C_P, C_P + W)
                    for j in range(GT):
                        b = outp.bank(("proj", g))[:, j * W:(j + 1) * W]
                        mm(b, ones16[0:BR, :], bias_p[:, 0:W], stop=False)
                        mm(b, zt[:, j * P:(j + 1) * P], hi, start=False, stop=False)
                        last = mm(b, zt[:, j * P:(j + 1) * P], lo, start=False)
                    last.then_inc(outp.filled, 1)
                if what == "rows":
                    turn_rows(("f1", n))
                if what == "router":
                    wide.wait_free(pe, ("rh", n))
                    pair(wide.bank(("rh", n))[0:RH, :], C_R, RH, z_turned(("f1", n))).then_inc(wide.filled, 1)
                if what == "first":
                    g, q = n
                    wide.wait_free(pe, ("h1", g, q))
                    pair(wide.bank(("h1", g, q))[:, :], C_X + q * P, P, z_turned(("f1", g))).then_inc(wide.filled, 1)
                if what == "logits":
                    pe.wait_ge(rlo_ready, n + 1)
                    outp.wait_free(pe, ("rl", n))
                    for j in range(GT):
                        b = outp.bank(("rl", n))[:, j * X:(j + 1) * X]
                        mm(b, rhp[:, n % 2, j * P:(j + 1) * P], r_w2p[:, 0, :], stop=False)
                        last = mm(b, rhp[:, n % 2, j * P:(j + 1) * P], r_w2p[:, 1, :], start=False)
                    last.then_inc(outp.filled, 1)
                if what == "second":
                    g, q = n
                    wide.wait_read(pe, ("h1", g, q))
                    wide.wait_free(pe, ("h2", g, q))
                    mm(wide.bank(("h2", g, q))[:, :], x_w2[:, q, :], h1T[:, g % 2, q, :]).then_inc(wide.filled, 1)
                if what == "third":
                    g, j = n
                    for q in range(XP):
                        wide.wait_read(pe, ("h2", g, q))
                    wide.wait_free(pe, ("eo", g, j))
                    b = wide.bank(("eo", g, j))
                    mm(b[:, 0:X * W], ones16[0:BR, :], bias_p[:, W:BN], stop=False)
                    for q in range(XP):
                        last = mm(b[:, q * P:(q + 1) * P], h2T[:, g % 2, q, j * P:(j + 1) * P], x_w3[:, q, :], start=False, stop=(q == XP - 1))
                    last.then_inc(wide.filled, 1)


_INS = ["x", "L0_tok_emb", "L0_tok_W_upd", "L0_tok_b_upd", "L0_tok_W_f", "L0_tok_b_f", "L0_tok_decay_param",
        "L0_tok_norm_g", "L0_tok_norm_b", "L0_tok_cms_ln_g", "L0_tok_cms_ln_b", "L0_tok_cms_W1", "L0_tok_cms_b1",
        "L0_tok_cms_W2", "L0_tok_cms_b2", "L0_tok_head_W", "L0_tok_head_b", "L0_ffn_gate_w", "L0_ffn_gate_b",
        "L0_ffn_w1", "L0_ffn_b1", "L0_ffn_w2", "L0_ffn_b2", "L1_attn_w_qkv", "L1_attn_w_proj", "L1_attn_b_proj",
        "L1_attn_rel_bias", "L1_ffn_router_w1", "L1_ffn_router_b1", "L1_ffn_router_w2", "L1_ffn_router_b2",
        "L1_ffn_expert_w1", "L1_ffn_expert_b1", "L1_ffn_expert_w2", "L1_ffn_expert_b2", "L1_ffn_expert_w3",
        "L1_ffn_expert_b3"]


def kernel(**inputs):
    import numpy as _np
    import concourse.bacc as _bacc
    from concourse import mybir as _mybir
    from concourse.bass_utils import run_bass_kernel_spmd as _run

    nc = _bacc.Bacc("TRN2", target_bir_lowering=False, num_devices=1)
    arrays, args = {}, {}
    for name in _INS:
        a = _np.ascontiguousarray(inputs[name])
        arrays[f"in_{name}_dram"] = a
        args[name] = nc.dram_tensor(f"in_{name}_dram", a.shape, _mybir.dt.from_np(a.dtype), kind="ExternalInput").ap()
    nb, s = args["x"].shape
    out = nc.dram_tensor("out_dram", (nb, s, args["L0_tok_head_b"].shape[0]), F32, kind="ExternalOutput").ap()
    build(nc, args, out)
    r = _run(nc, [arrays], core_ids=[0])
    return r.results[0]["out_dram"]
```
